# Optimizing a Trainium2 kernel written in Bass

```python
import numpy as np
import jax
import jax.numpy as jnp

def _softmax(x, axis=-1):
    return jax.nn.softmax(x, axis=axis)

def _gelu(x):
    return jax.nn.gelu(x, approximate=True)

def _silu(x):
    return jax.nn.silu(x)

def _sigmoid(x):
    return jax.nn.sigmoid(x)

def _layernorm(x, axis=-1, eps=1e-05):
    m = jnp.mean(x, axis=axis, keepdims=True)
    v = jnp.var(x, axis=axis, keepdims=True)
    return (x - m) / jnp.sqrt(v + eps)

def _scatter_add(tgt, idx, src, axis=0):
    return tgt.at[idx].add(src)

def _segment_sum(src, seg, n):
    return jax.ops.segment_sum(src, seg, n)
kernel_name = 'mk_perceiver_d2_seqx_r8_fca024'

def setup_inputs(seed: int=0):
    np.random.seed(seed)
    _w = jnp.asarray

    def _rec_inputs():
        import jax
        import jax.numpy as jnp
        _rk = jax.random.key(seed)
        x = -0.000125 + 0.9999 * jax.random.normal(jax.random.fold_in(_rk, 1), (128, 32, 256), jnp.float32)
        _lenS = 32 - jax.random.randint(jax.random.fold_in(_rk, 7), (128,), 0, max(1, 32 // 4) + 1, jnp.int32)
        _lenS2 = 257 - jax.random.randint(jax.random.fold_in(_rk, 8), (128,), 0, max(1, 257 // 4) + 1, jnp.int32)
        _ctx_2048P = jax.random.normal(jax.random.fold_in(_rk, 11), (128, 16, 256), jnp.float32)
        _ctx_2048c = jax.random.dirichlet(jax.random.fold_in(_rk, 511), 0.3 * jnp.ones((16,), jnp.float32), (128, 257))
        _ctx_2048t = jnp.einsum('bsk,bkd->bsd', _ctx_2048c, _ctx_2048P)
        _ctx_2048t = _ctx_2048t * jax.lax.rsqrt(jnp.mean(jnp.square(_ctx_2048t)) + 1e-12) * 0.953939
        ctx_2048 = -0.000514642 + 1.00011 * (_ctx_2048t + 0.3 * jax.random.normal(jax.random.fold_in(_rk, 611), (128, 257, 256), jnp.float32))
        _validS = jnp.arange(32)[None, :] < _lenS[:, None]
        _validS2 = jnp.arange(257)[None, :] < _lenS2[:, None]
        _causal = jnp.tril(jnp.ones((32, 32), dtype=bool))
        mask_BxS2_bk0 = jnp.logical_not(jnp.broadcast_to(_validS2[:, :], (128, 257)))
        return (x, ctx_2048, mask_BxS2_bk0)
    x, ctx_2048, mask_BxS2_bk0 = _rec_inputs()

    def _L0_xattn_setup():
        import jax, jax.numpy as jnp
        import numpy as np
        key = jax.random.key(seed)
        k1, k2, k3 = jax.random.split(key, 3)
        B, S, D, M = (8, 256, 256, 128)
        hidden_states = jax.random.normal(k1, (B, S, D), dtype=jnp.float32)
        memory_tokens = jax.random.normal(k2, (B, M, D), dtype=jnp.float32)
        memory_mask = jax.random.randint(k3, (B, M), 0, 2).astype(jnp.bool_)
        return {'hidden_states': hidden_states, 'memory_tokens': memory_tokens, 'memory_mask': memory_mask}
    _L0_xattn_all = _L0_xattn_setup()
    _L0_xattn_in = {k: v for k, v in _L0_xattn_all.items() if k in ()}
    del _L0_xattn_all

    def _L0_attn_setup():
        import jax, jax.numpy as jnp
        import numpy as np
        N_HEAD = 32
        N_KV_HEAD = 8
        HEAD_DIM = 64
        N_EMBD = 256
        B, T = (2, 256)
        ROPE_BASE = 10000.0

        def _rope_cos_sin(T, head_dim, dtype):
            pos = jnp.arange(T, dtype=jnp.float32)
            dim_arr = jnp.arange(0, head_dim, 2, dtype=jnp.float32)
            freqs = ROPE_BASE ** (-dim_arr / head_dim)
            theta = jnp.outer(pos, freqs)
            cos = jnp.concatenate([jnp.cos(theta), jnp.cos(theta)], axis=-1)
            sin = jnp.concatenate([jnp.sin(theta), jnp.sin(theta)], axis=-1)
            return (cos[None, :, None, :].astype(dtype), sin[None, :, None, :].astype(dtype))

        def _rotate_half(v):
            h = v.shape[-1] // 2
            return jnp.concatenate([-v[..., h:], v[..., :h]], axis=-1)
        key = jax.random.key(seed)
        kx, kq, kk, kv, ko = jax.random.split(key, 5)
        s = 1.0 / np.sqrt(N_EMBD)
        return {'x': jax.random.normal(kx, (B, T, N_EMBD), dtype=jnp.float32), 'wq': jax.random.normal(kq, (N_EMBD, N_HEAD * HEAD_DIM), dtype=jnp.float32) * s, 'wk': jax.random.normal(kk, (N_EMBD, N_KV_HEAD * HEAD_DIM), dtype=jnp.float32) * s, 'wv': jax.random.normal(kv, (N_EMBD, N_KV_HEAD * HEAD_DIM), dtype=jnp.float32) * s, 'wo': jax.random.normal(ko, (N_HEAD * HEAD_DIM, N_EMBD), dtype=jnp.float32) * s}
    _L0_attn_all = _L0_attn_setup()
    _L0_attn_in = {k: v for k, v in _L0_attn_all.items() if k in ('wq', 'wk', 'wv', 'wo')}
    del _L0_attn_all

    def _L0_ffn_setup():
        import jax, jax.numpy as jnp
        import numpy as np
        DIM_IN = 256
        DIM_HIDDEN = 1024
        key = jax.random.key(seed)
        k_x, k_g, k_u, k_d = jax.random.split(key, 4)
        s_in = 1.0 / np.sqrt(DIM_IN)
        s_hid = 1.0 / np.sqrt(DIM_HIDDEN)
        x = jax.random.normal(k_x, (4, 256, DIM_IN), dtype=jnp.float32)
        w_gate = jax.random.uniform(k_g, (DIM_HIDDEN, DIM_IN), jnp.float32, -s_in, s_in)
        w_up = jax.random.uniform(k_u, (DIM_HIDDEN, DIM_IN), jnp.float32, -s_in, s_in)
        w_down = jax.random.uniform(k_d, (DIM_IN, DIM_HIDDEN), jnp.float32, -s_hid, s_hid)
        return {'x': x, 'w_gate': w_gate, 'w_up': w_up, 'w_down': w_down}
    _L0_ffn_all = _L0_ffn_setup()
    _L0_ffn_in = {k: v for k, v in _L0_ffn_all.items() if k in ('w_gate', 'w_up', 'w_down')}
    del _L0_ffn_all

    def _L1_xattn_setup():
        import jax, jax.numpy as jnp
        import numpy as np
        DIM = 256
        N_HEADS = 16
        HEAD_DIM = DIM // N_HEADS
        EPS = 1e-06
        IMG_LEN = 257

        def rms_norm(x, g, eps=EPS):
            var = jnp.mean(x * x, axis=-1, keepdims=True)
            return x * jax.lax.rsqrt(var + eps) * g

        def _attend(q, k, v, k_mask=None):
            scale = 1.0 / jnp.sqrt(jnp.asarray(HEAD_DIM, q.dtype))
            scores = jnp.einsum('bqnd,bknd->bnqk', q, k) * scale
            if k_mask is not None:
                neg = jnp.asarray(jnp.finfo(scores.dtype).min, scores.dtype)
                scores = jnp.where(k_mask[:, None, None, :], scores, neg)
            probs = jax.nn.softmax(scores, axis=-1)
            return jnp.einsum('bnqk,bknd->bqnd', probs, v)
        key = jax.random.key(seed)
        ks = jax.random.split(key, 16)
        B, L1, L2 = (1, 2048, 769)
        std = 0.02
        inp = {'x': jax.random.normal(ks[0], (B, L1, DIM), jnp.float32), 'context': jax.random.normal(ks[1], (B, L2, DIM), jnp.float32), 'context_lens': jax.random.randint(ks[2], (B,), 32, 513, jnp.int32), 'Wq': jax.random.normal(ks[3], (DIM, DIM), jnp.float32) * std, 'bq': jnp.zeros((DIM,), jnp.float32), 'gq': jnp.ones((DIM,), jnp.float32), 'Wk': jax.random.normal(ks[4], (DIM, DIM), jnp.float32) * std, 'bk': jnp.zeros((DIM,), jnp.float32), 'gk': jnp.ones((DIM,), jnp.float32), 'Wv': jax.random.normal(ks[5], (DIM, DIM), jnp.float32) * std, 'bv': jnp.zeros((DIM,), jnp.float32), 'Wk_img': jax.random.normal(ks[6], (DIM, DIM), jnp.float32) * std, 'bk_img': jnp.zeros((DIM,), jnp.float32), 'gk_img': jnp.ones((DIM,), jnp.float32), 'Wv_img': jax.random.normal(ks[7], (DIM, DIM), jnp.float32) * std, 'bv_img': jnp.zeros((DIM,), jnp.float32), 'Wo': jax.random.normal(ks[8], (DIM, DIM), jnp.float32) * std, 'bo': jnp.zeros((DIM,), jnp.float32)}
        return inp
    _L1_xattn_all = _L1_xattn_setup()
    _L1_xattn_in = {k: v for k, v in _L1_xattn_all.items() if k in ('context_lens', 'Wq', 'bq', 'gq', 'Wk', 'bk', 'gk', 'Wv', 'bv', 'Wk_img', 'bk_img', 'gk_img', 'Wv_img', 'bv_img', 'Wo', 'bo')}
    del _L1_xattn_all

    def _L1_attn_setup():
        import jax, jax.numpy as jnp
        import numpy as np
        B, T, D = (2, 256, 256)
        HQ, HKV = (32, 8)
        HD = D // HQ
        G = HQ // HKV
        ROPE_BASE = 10000.0

        def _rope(q, k):
            t, d = (q.shape[2], q.shape[3])
            inv_freq = 1.0 / ROPE_BASE ** (jnp.arange(0, d, 2, dtype=jnp.float32) / d)
            ang = jnp.arange(t, dtype=jnp.float32)[:, None] * inv_freq[None, :]
            cos = jnp.concatenate([jnp.cos(ang), jnp.cos(ang)], axis=-1)[None, None]
            sin = jnp.concatenate([jnp.sin(ang), jnp.sin(ang)], axis=-1)[None, None]

            def rot_half(x):
                x1, x2 = jnp.split(x, 2, axis=-1)
                return jnp.concatenate([-x2, x1], axis=-1)
            return (q * cos + rot_half(q) * sin, k * cos + rot_half(k) * sin)
        key = jax.random.key(seed)
        ks = jax.random.split(key, 5)
        s = 0.02
        x = jax.random.normal(ks[0], (B, T, D), dtype=jnp.float32)
        Wq = jax.random.normal(ks[1], (D, D), dtype=jnp.float32) * s
        Wk = jax.random.normal(ks[2], (HKV * HD, D), dtype=jnp.float32) * s
        Wv = jax.random.normal(ks[3], (HKV * HD, D), dtype=jnp.float32) * s
        Wo = jax.random.normal(ks[4], (D, D), dtype=jnp.float32) * s
        return {'x': x, 'Wq': Wq, 'bq': jnp.zeros((D,), jnp.float32), 'Wk': Wk, 'bk': jnp.zeros((HKV * HD,), jnp.float32), 'Wv': Wv, 'bv': jnp.zeros((HKV * HD,), jnp.float32), 'Wo': Wo, 'bo': jnp.zeros((D,), jnp.float32)}
    _L1_attn_all = _L1_attn_setup()
    _L1_attn_in = {k: v for k, v in _L1_attn_all.items() if k in ('Wq', 'bq', 'Wk', 'bk', 'Wv', 'bv', 'Wo', 'bo')}
    del _L1_attn_all

    def _L1_ffn_setup():
        import jax, jax.numpy as jnp
        import numpy as np
        D_MODEL = 256
        D_FF = 1024
        N_EXPERTS = 4
        B, S = (2, 256)
        key = jax.random.key(seed)
        ks = jax.random.split(key, 6)
        scale = 0.02
        return {'hidden_states': jax.random.normal(ks[0], (B, S, D_MODEL), dtype=jnp.float32), 'Wr': jax.random.normal(ks[1], (D_MODEL, N_EXPERTS), dtype=jnp.float32) * scale, 'br': jnp.zeros((N_EXPERTS,), dtype=jnp.float32), 'Wg': jax.random.normal(ks[2], (N_EXPERTS, D_MODEL, D_FF), dtype=jnp.float32) * scale, 'Wu': jax.random.normal(ks[3], (N_EXPERTS, D_MODEL, D_FF), dtype=jnp.float32) * scale, 'Wd': jax.random.normal(ks[4], (N_EXPERTS, D_FF, D_MODEL), dtype=jnp.float32) * scale}
    _L1_ffn_all = _L1_ffn_setup()
    _L1_ffn_in = {k: v for k, v in _L1_ffn_all.items() if k in ('Wr', 'br', 'Wg', 'Wu', 'Wd')}
    del _L1_ffn_all
    return {'x': x, 'ctx_2048': ctx_2048, 'mask_BxS2_bk0': mask_BxS2_bk0, 'L0_attn_wq': _L0_attn_in['wq'], 'L0_attn_wk': _L0_attn_in['wk'], 'L0_attn_wv': _L0_attn_in['wv'], 'L0_attn_wo': _L0_attn_in['wo'], 'L0_ffn_w_gate': _L0_ffn_in['w_gate'], 'L0_ffn_w_up': _L0_ffn_in['w_up'], 'L0_ffn_w_down': _L0_ffn_in['w_down'], 'L1_xattn_context_lens': _L1_xattn_in['context_lens'], 'L1_xattn_Wq': _L1_xattn_in['Wq'], 'L1_xattn_bq': _L1_xattn_in['bq'], 'L1_xattn_gq': _L1_xattn_in['gq'], 'L1_xattn_Wk': _L1_xattn_in['Wk'], 'L1_xattn_bk': _L1_xattn_in['bk'], 'L1_xattn_gk': _L1_xattn_in['gk'], 'L1_xattn_Wv': _L1_xattn_in['Wv'], 'L1_xattn_bv': _L1_xattn_in['bv'], 'L1_xattn_Wk_img': _L1_xattn_in['Wk_img'], 'L1_xattn_bk_img': _L1_xattn_in['bk_img'], 'L1_xattn_gk_img': _L1_xattn_in['gk_img'], 'L1_xattn_Wv_img': _L1_xattn_in['Wv_img'], 'L1_xattn_bv_img': _L1_xattn_in['bv_img'], 'L1_xattn_Wo': _L1_xattn_in['Wo'], 'L1_xattn_bo': _L1_xattn_in['bo'], 'L1_attn_Wq': _L1_attn_in['Wq'], 'L1_attn_bq': _L1_attn_in['bq'], 'L1_attn_Wk': _L1_attn_in['Wk'], 'L1_attn_bk': _L1_attn_in['bk'], 'L1_attn_Wv': _L1_attn_in['Wv'], 'L1_attn_bv': _L1_attn_in['bv'], 'L1_attn_Wo': _L1_attn_in['Wo'], 'L1_attn_bo': _L1_attn_in['bo'], 'L1_ffn_Wr': _L1_ffn_in['Wr'], 'L1_ffn_br': _L1_ffn_in['br'], 'L1_ffn_Wg': _L1_ffn_in['Wg'], 'L1_ffn_Wu': _L1_ffn_in['Wu'], 'L1_ffn_Wd': _L1_ffn_in['Wd']}

def reference(x, ctx_2048, mask_BxS2_bk0, L0_attn_wq, L0_attn_wk, L0_attn_wv, L0_attn_wo, L0_ffn_w_gate, L0_ffn_w_up, L0_ffn_w_down, L1_xattn_context_lens, L1_xattn_Wq, L1_xattn_bq, L1_xattn_gq, L1_xattn_Wk, L1_xattn_bk, L1_xattn_gk, L1_xattn_Wv, L1_xattn_bv, L1_xattn_Wk_img, L1_xattn_bk_img, L1_xattn_gk_img, L1_xattn_Wv_img, L1_xattn_bv_img, L1_xattn_Wo, L1_xattn_bo, L1_attn_Wq, L1_attn_bq, L1_attn_Wk, L1_attn_bk, L1_attn_Wv, L1_attn_bv, L1_attn_Wo, L1_attn_bo, L1_ffn_Wr, L1_ffn_br, L1_ffn_Wg, L1_ffn_Wu, L1_ffn_Wd):
    import jax
    import jax.numpy as jnp

    def _L0_xattn_ref(hidden_states, memory_tokens, memory_mask):
        import jax, jax.numpy as jnp
        import numpy as np
        B, S, D = hidden_states.shape
        scale = 1.0 / jnp.sqrt(jnp.asarray(D, hidden_states.dtype))
        scores = jnp.einsum('bsd,bmd->bsm', hidden_states, memory_tokens) * scale
        neg_inf = jnp.asarray(-1e+30, scores.dtype)
        scores = jnp.where(memory_mask[:, None, :], scores, neg_inf)
        attn = jax.nn.softmax(scores, axis=-1)
        readout = jnp.einsum('bsm,bmd->bsd', attn, memory_tokens)
        valid_b = jnp.any(memory_mask, axis=-1)
        out = jnp.where(valid_b[:, None, None], readout, jnp.zeros_like(readout))
        return out

    def _L0_attn_ref(x, wq, wk, wv, wo):
        import jax, jax.numpy as jnp
        import numpy as np
        N_HEAD = 32
        N_KV_HEAD = 8
        HEAD_DIM = 64
        N_EMBD = 256
        B, T = (2, 256)
        ROPE_BASE = 10000.0

        def _rope_cos_sin(T, head_dim, dtype):
            pos = jnp.arange(T, dtype=jnp.float32)
            dim_arr = jnp.arange(0, head_dim, 2, dtype=jnp.float32)
            freqs = ROPE_BASE ** (-dim_arr / head_dim)
            theta = jnp.outer(pos, freqs)
            cos = jnp.concatenate([jnp.cos(theta), jnp.cos(theta)], axis=-1)
            sin = jnp.concatenate([jnp.sin(theta), jnp.sin(theta)], axis=-1)
            return (cos[None, :, None, :].astype(dtype), sin[None, :, None, :].astype(dtype))

        def _rotate_half(v):
            h = v.shape[-1] // 2
            return jnp.concatenate([-v[..., h:], v[..., :h]], axis=-1)
        Bx, Tx, C = x.shape
        n_rep = N_HEAD // N_KV_HEAD
        xq = (x @ wq).reshape(Bx, Tx, N_HEAD, HEAD_DIM)
        xk = (x @ wk).reshape(Bx, Tx, N_KV_HEAD, HEAD_DIM)
        xv = (x @ wv).reshape(Bx, Tx, N_KV_HEAD, HEAD_DIM)
        cos, sin = _rope_cos_sin(Tx, HEAD_DIM, x.dtype)
        xq = xq * cos + _rotate_half(xq) * sin
        xk = xk * cos + _rotate_half(xk) * sin
        xk = jnp.repeat(xk, n_rep, axis=2)
        xv = jnp.repeat(xv, n_rep, axis=2)
        scale = 1.0 / np.sqrt(HEAD_DIM)
        scores = jnp.einsum('bqhd,bkhd->bhqk', xq, xk) * scale
        causal = jnp.tril(jnp.ones((Tx, Tx), dtype=bool))
        scores = jnp.where(causal[None, None], scores, -jnp.inf)
        probs = jax.nn.softmax(scores, axis=-1)
        out = jnp.einsum('bhqk,bkhd->bqhd', probs, xv).reshape(Bx, Tx, N_HEAD * HEAD_DIM)
        return out @ wo

    def _L0_ffn_ref(x, w_gate, w_up, w_down):
        import jax, jax.numpy as jnp
        import numpy as np
        DIM_IN = 256
        DIM_HIDDEN = 1024
        gate = jnp.einsum('bsd,hd->bsh', x, w_gate)
        up = jnp.einsum('bsd,hd->bsh', x, w_up)
        gated = jax.nn.silu(gate) * up
        return jnp.einsum('bsh,dh->bsd', gated, w_down)

    def _L1_xattn_ref(x, context, context_lens, Wq, bq, gq, Wk, bk, gk, Wv, bv, Wk_img, bk_img, gk_img, Wv_img, bv_img, Wo, bo):
        import jax, jax.numpy as jnp
        import numpy as np
        DIM = 256
        N_HEADS = 16
        HEAD_DIM = DIM // N_HEADS
        EPS = 1e-06
        IMG_LEN = 257

        def rms_norm(x, g, eps=EPS):
            var = jnp.mean(x * x, axis=-1, keepdims=True)
            return x * jax.lax.rsqrt(var + eps) * g

        def _attend(q, k, v, k_mask=None):
            scale = 1.0 / jnp.sqrt(jnp.asarray(HEAD_DIM, q.dtype))
            scores = jnp.einsum('bqnd,bknd->bnqk', q, k) * scale
            if k_mask is not None:
                neg = jnp.asarray(jnp.finfo(scores.dtype).min, scores.dtype)
                scores = jnp.where(k_mask[:, None, None, :], scores, neg)
            probs = jax.nn.softmax(scores, axis=-1)
            return jnp.einsum('bnqk,bknd->bqnd', probs, v)
        b = x.shape[0]
        n, d = (N_HEADS, HEAD_DIM)
        ctx_img = context[:, :IMG_LEN]
        ctx_txt = context[:, IMG_LEN:]
        q = rms_norm(x @ Wq + bq, gq).reshape(b, -1, n, d)
        k = rms_norm(ctx_txt @ Wk + bk, gk).reshape(b, -1, n, d)
        v = (ctx_txt @ Wv + bv).reshape(b, -1, n, d)
        k_img = rms_norm(ctx_img @ Wk_img + bk_img, gk_img).reshape(b, -1, n, d)
        v_img = (ctx_img @ Wv_img + bv_img).reshape(b, -1, n, d)
        img_x = _attend(q, k_img, v_img)
        k_mask = jnp.arange(k.shape[1])[None, :] < context_lens[:, None]
        txt_x = _attend(q, k, v, k_mask)
        out = (txt_x + img_x).reshape(b, -1, n * d)
        return out @ Wo + bo

    def _L1_attn_ref(x, Wq, bq, Wk, bk, Wv, bv, Wo, bo):
        import jax, jax.numpy as jnp
        import numpy as np
        B, T, D = (2, 256, 256)
        HQ, HKV = (32, 8)
        HD = D // HQ
        G = HQ // HKV
        ROPE_BASE = 10000.0

        def _rope(q, k):
            t, d = (q.shape[2], q.shape[3])
            inv_freq = 1.0 / ROPE_BASE ** (jnp.arange(0, d, 2, dtype=jnp.float32) / d)
            ang = jnp.arange(t, dtype=jnp.float32)[:, None] * inv_freq[None, :]
            cos = jnp.concatenate([jnp.cos(ang), jnp.cos(ang)], axis=-1)[None, None]
            sin = jnp.concatenate([jnp.sin(ang), jnp.sin(ang)], axis=-1)[None, None]

            def rot_half(x):
                x1, x2 = jnp.split(x, 2, axis=-1)
                return jnp.concatenate([-x2, x1], axis=-1)
            return (q * cos + rot_half(q) * sin, k * cos + rot_half(k) * sin)
        b, t, _ = x.shape
        Q = (x @ Wq.T + bq).reshape(b, t, HQ, HD).transpose(0, 2, 1, 3)
        K = (x @ Wk.T + bk).reshape(b, t, HKV, HD).transpose(0, 2, 1, 3)
        V = (x @ Wv.T + bv).reshape(b, t, HKV, HD).transpose(0, 2, 1, 3)
        Q, K = _rope(Q, K)
        K = jnp.repeat(K, G, axis=1)
        V = jnp.repeat(V, G, axis=1)
        scores = jnp.einsum('bhqd,bhkd->bhqk', Q, K) / np.sqrt(HD).astype(np.float32)
        w = jax.nn.softmax(scores, axis=-1)
        attn = jnp.einsum('bhqk,bhkd->bhqd', w, V)
        out = attn.transpose(0, 2, 1, 3).reshape(b, t, D)
        return out @ Wo.T + bo

    def _L1_ffn_ref(hidden_states, Wr, br, Wg, Wu, Wd):
        import jax, jax.numpy as jnp
        import numpy as np
        D_MODEL = 256
        D_FF = 1024
        N_EXPERTS = 4
        B, S = (2, 256)
        b, s, d = hidden_states.shape
        x = hidden_states.reshape(-1, d)
        logits = x @ Wr + br
        probs = jax.nn.softmax(logits, axis=-1)
        top_w, top_idx = jax.lax.top_k(probs, 1)
        g = jnp.einsum('td,edf->tef', x, Wg)
        u = jnp.einsum('td,edf->tef', x, Wu)
        h = jax.nn.silu(g) * u
        y = jnp.einsum('tef,efd->ted', h, Wd)
        sel = jnp.take_along_axis(y, top_idx[:, :, None], axis=1)[:, 0]
        out = sel * top_w
        return out.reshape(b, s, d)
    x = x + _L0_xattn_ref(_layernorm(x, axis=-1), ctx_2048, mask_BxS2_bk0)
    x = x + _L0_attn_ref(_layernorm(x, axis=-1), L0_attn_wq, L0_attn_wk, L0_attn_wv, L0_attn_wo)
    x = x + _L0_ffn_ref(_layernorm(x, axis=-1), L0_ffn_w_gate, L0_ffn_w_up, L0_ffn_w_down)
    x = x + _L1_xattn_ref(_layernorm(x, axis=-1), ctx_2048, L1_xattn_context_lens, L1_xattn_Wq, L1_xattn_bq, L1_xattn_gq, L1_xattn_Wk, L1_xattn_bk, L1_xattn_gk, L1_xattn_Wv, L1_xattn_bv, L1_xattn_Wk_img, L1_xattn_bk_img, L1_xattn_gk_img, L1_xattn_Wv_img, L1_xattn_bv_img, L1_xattn_Wo, L1_xattn_bo)
    x = x + _L1_attn_ref(_layernorm(x, axis=-1), L1_attn_Wq, L1_attn_bq, L1_attn_Wk, L1_attn_bk, L1_attn_Wv, L1_attn_bv, L1_attn_Wo, L1_attn_bo)
    x = x + _L1_ffn_ref(_layernorm(x, axis=-1), L1_ffn_Wr, L1_ffn_br, L1_ffn_Wg, L1_ffn_Wu, L1_ffn_Wd)
    return x

_drawn_inputs = setup_inputs


def setup_inputs(seed=0):
    import zlib

    import numpy as np

    out = dict(_drawn_inputs(seed))
    spreads = {'L1_xattn_bq': (0.0, 0.8),
     'L1_xattn_gq': (1.0, 0.6),
     'L1_xattn_bk': (0.0, 0.1),
     'L1_xattn_gk': (1.0, 0.2),
     'L1_xattn_bv': (0.0, 0.1),
     'L1_xattn_bk_img': (0.0, 2.0),
     'L1_xattn_gk_img': (1.0, 0.6),
     'L1_xattn_bv_img': (0.0, 0.598),
     'L1_xattn_bo': (0.0, 0.1),
     'L1_attn_bq': (0.0, 0.8),
     'L1_attn_bk': (0.0, 0.8),
     'L1_attn_bv': (0.0, 0.498),
     'L1_attn_bo': (0.0, 0.1),
     'L1_ffn_br': (0.0, 0.8)}
    factors = {'L1_xattn_Wq': 6.638,
     'L1_xattn_Wk_img': 6.339,
     'L1_attn_Wq': 8.0,
     'L1_attn_Wk': 8.0,
     'L1_ffn_Wr': 8.0,
     'L1_ffn_Wg': 8.0,
     'L1_ffn_Wu': 8.0,
     'L1_ffn_Wd': 8.0}
    for name, (base, spread) in spreads.items():
        noise = np.random.default_rng([zlib.crc32(name.encode()), seed]).standard_normal(out[name].shape)
        drawn = base * np.exp(spread * noise) if base else spread * noise
        out[name] = jnp.asarray(drawn.astype(out[name].dtype))
    for name, factor in factors.items():
        out[name] = (out[name] * factor).astype(out[name].dtype)
    return out
```

```python
from contextlib import ExitStack

import numpy as np

import concourse.bass as bass
from concourse import mybir

F32 = mybir.dt.float32
U8 = mybir.dt.uint8
I32 = mybir.dt.int32
ALU = mybir.AluOpType
ACT = mybir.ActivationFunctionType
AX = mybir.AxisListType

P = 128
S = 32
NB = P // S
D = 256
KC = D // P
M = 257
MC = 2
BATCHES = 128
TILES = BATCHES // NB
TOKENS = BATCHES * S
F = 1024
FC = F // P
EXPERTS = 4
H0, G0, HD0 = 32, 8, 64
KV0 = G0 * HD0
H1, HD1 = 16, 16
G2, HD2 = 8, 8
REP = 4
NEG = -1e30
LOADS = 4
RSQRT_SEED = 0x5F3759DF
CHAIN_A, CHAIN_B, CHAIN_M = 61, 73, 34
B_STEPS = ["ba0", "ba1", "ba2"] + [s + str(b) for b in range(NB) for s in ("bb", "bc", "bd", "be", "bf")] + [
    f"bg{n}" for n in range(10)]
A_STEPS = [f"a{n:02d}" for n in range(1, 16)]
ORDER = [s for n, s_a in enumerate(A_STEPS) for s in [s_a] + B_STEPS[n * len(B_STEPS) // 15:(n + 1) * len(B_STEPS) // 15]]
ds = bass.ds


class Tile:

    def __init__(self, i, slot, n):
        self.i, self.slot, self.n = i, slot, n
        self.first = isinstance(i, int) and i == 0
        self.slot_first = isinstance(n, int) and n == 0

    def upto(self, per, k):
        return self.i * per + k


class Chain:

    def __init__(self, eng, sem, per):
        self.eng, self.sem, self.per, self.t, self.n = eng, sem, per, None, 0

    def open(self, t):
        self.t, self.n = t, 0

    def close(self):
        assert self.n == self.per, ("CHAIN", self.n, self.per)

    def done(self, ins):
        self.n += 1
        ins.then_inc(self.sem, 1)
        self.eng.wait_ge(self.sem, self.t.upto(self.per, self.n))


def inverse_root(dve, chain, v, y, w):
    chain.done(dve.tensor_scalar(y.bitcast(I32), v.bitcast(I32), 1, None, ALU.logical_shift_right))
    chain.done(dve.tensor_scalar(y.bitcast(I32), y.bitcast(I32), -1.0, float(RSQRT_SEED), ALU.mult, ALU.add))
    for _ in range(3):
        chain.done(dve.scalar_tensor_tensor(w, v, y, y, ALU.mult, ALU.mult))
        chain.done(dve.tensor_scalar(w, w, -0.5, 1.5, ALU.mult, ALU.add))
        chain.done(dve.tensor_tensor(y, y, w, ALU.mult))


def layer_norm(dve, chain, x, y, stats, mv):
    chain.done(dve.bn_stats(stats, x))
    dve.memset(mv[:, 3:4], 0.0)
    chain.done(dve.bn_aggr(mv[:, 0:2], stats))
    chain.done(dve.tensor_scalar(mv[:, 1:2], mv[:, 1:2], 1e-5, None, ALU.add))
    inverse_root(dve, chain, mv[:, 1:2], mv[:, 2:3], mv[:, 3:4])
    return dve.tensor_scalar(y, x, mv[:, 0:1], mv[:, 2:3], ALU.subtract, ALU.mult)


def build(nc, a, out):
    x5_dram = nc.dram_tensor("x5_scratch", [TOKENS, D], F32, kind="Internal").ap()
    with ExitStack() as both:
        ident = both.enter_context(nc.sbuf_tensor("ident", [P, P], F32))
        with ExitStack() as ctx:
            layers_0_to_attention_1(nc, ctx, a, ident, x5_dram)
        with ExitStack() as ctx:
            mixture_of_experts(nc, ctx, a, ident, x5_dram, out)


def layers_0_to_attention_1(nc, ctx, a, ident, x5_dram):
    def sb(name, shape, dt=F32):
        return ctx.enter_context(nc.sbuf_tensor(name, shape, dt))

    def sem(name):
        return ctx.enter_context(nc.semaphore(name))

    loads = []

    def const(name, shape, src=None, dt=F32):
        t = sb("c_" + name, shape, dt)
        loads.append((t, a[src or name]))
        return t

    loads.append((ident, a["ident"]))
    wkv0 = const("wkv0", [P, KC, 2 * KV0])
    wq0 = const("wq0", [P, KC, H0 * HD0])
    wo0 = const("wo0", [P, H0 * HD0 // P, D])
    wgate0 = const("wgate0", [P, KC, F])
    wup0 = const("wup0", [P, KC, F])
    wdown0 = const("wdown0", [P, FC, D])
    wq1 = const("wq1", [P, KC, D])
    wk1 = const("wk1", [P, KC, D])
    wv1 = const("wv1", [P, KC, D])
    wo1 = const("wo1", [64, REP, D])
    wqkv2 = const("wqkv2", [P, KC, 384])
    wo2 = const("wo2", [64, REP, D])
    cos0 = const("cos0", [P, HD0])
    sin0 = const("sin0", [P, HD0])
    cos2 = const("cos2", [P, HD2])
    sin2 = const("sin2", [P, HD2])
    causal = const("causal", [P, S])
    own_batch = const("own_batch", [P, NB])
    head_rows = const("head_rows", [P, REP])
    group_rows = const("group_rows", [64, G2])
    bq1 = const("bq1", [P, D])
    gq1 = const("gq1", [P, D])
    bk1 = const("bk1", [P, KC])
    gk1 = const("gk1", [P, KC])
    bv1 = const("bv1", [64, REP])
    bo1 = const("bo1", [P, D])
    bqkv2 = const("bqkv2", [P, 384])
    bo2 = const("bo2", [P, D])

    x_in = sb("x_in", [P, 2, D])
    rows = sb("ctx_rows", [P, 2, NB, MC, D])
    last_row = sb("ctx_last_row", [NB, 2, D])
    mask_u8 = sb("mask_u8", [P, 2, M], U8)
    ctxT = sb("ctxT", [P, 2, KC, NB, M])
    xn = sb("xn", [P, D])
    xnT_sb = sb("xnT_sb", [P, KC, P])
    stats = sb("stats", [P, 6])
    mv = sb("mv", [P, 4])
    maskadd = sb("maskadd", [P, M])
    sc0 = sb("sc0", [P, M])
    p0 = sb("p0", [P, M])
    small = sb("small", [P, 8])
    p0_last = sb("p0_last", [P, NB])
    p0T = sb("p0T", [P, MC, P])
    p0T_last = sb("p0T_last", [NB, P])
    x1 = sb("x1", [P, D])
    v0 = sb("v0", [P, KV0])
    qT = sb("qT", [P, 4, NB, REP, S])
    kT = sb("kT", [P, 4, P])
    att = sb("att", [P, 2 * 512])
    rope_c, rope_s = att[:, 0:512], att[:, 512:1024]
    att_max = sb("att_max", [P, 32])
    att_sum = sb("att_sum", [P, 32])
    attT = sb("attT", [P, 2, 512])
    rot = attT
    oT = sb("oT", [P, 4, REP, NB, S])
    x2 = sb("x2", [P, D])
    th = qT[:].rearrange("p c b j q -> p (c b j q)")[:, 0:F]
    hid = qT[:].rearrange("p c b j q -> p (c b j q)")[:, F:2 * F]
    hT = oT[:].rearrange("p c j b q -> p (c j b q)")[:, 0:F]
    x3 = sb("x3", [P, 2, D])

    yn = sb("yn", [P, D])
    ynT = sb("ynT", [P, KC, P])
    stats_b = sb("stats_b", [P, 6])
    mv_b = sb("mv_b", [P, 4])
    ones = sb("ones", [P, P])
    gk_rows = sb("gk_rows", [P, KC, REP])
    q1 = sb("q1", [P, D])
    q1sq = sb("q1sq", [P, D])
    q1ss = sb("q1ss", [P, 3])
    qbd = sb("qbd", [P, KC, NB, REP, S])
    ksq = sb("ksq", [P, KC, M])
    krs = sb("krs", [P, M])
    kms = sb("kms", [P, M])
    k1n = sb("k1n", [P, KC, M])
    v1 = sb("v1", [P, MC, D])
    v1_last = sb("v1_last", [NB, D])
    p1 = sb("p1", [P, REP, M])
    p1max = sb("p1max", [P, REP])
    p1sum = sb("p1sum", [P, REP])
    p1rec = sb("p1rec", [P, REP])
    p1_last = sb("p1_last", [P, NB, REP, NB])
    p1T = sb("p1T", [P, 1024])
    p1T_last = sb("p1T_last", [NB, 512])
    o1 = sb("o1", [P, NB, REP, HD1])
    o1T = sb("o1T", [64, REP, NB, S])
    x3b = sb("x3b", [P, D])
    x4 = sb("x4", [P, D])
    x4b = sb("x4b", [P, D])
    qkv = sb("qkv", [P, 384])
    rc2 = sb("rc2", [P, 320])
    rs2 = sb("rs2", [P, 320])
    q2T = v1[0:64].rearrange("p c d -> p (c d)").rearrange("p (b j q) -> p b j q", b=NB, j=REP)
    k2bd = p1[0:64].rearrange("p j m -> p (j m)")[:, 0:NB * G2 * S].rearrange("p (b g k) -> p b g k", b=NB, g=G2)
    v2bd = ksq[:].rearrange("p c m -> p (c m)")[:, 0:D].rearrange("p (g b d) -> p g b d", g=G2, b=NB)
    att2 = qbd[:].rearrange("p c b h q -> p (c b h q)")
    att2_max = sb("att2_max", [P, 32])
    att2_sum = sb("att2_sum", [P, 32])
    att2T = p1T
    o2 = o1[:].rearrange("p b j d -> p (b j d)").rearrange("p (b g d) -> p b g d", b=NB, g=G2)
    o2T = o1T
    x5 = sb("x5", [P, 2, D])

    psA = ctx.enter_context(nc.psum_tensor("psA", [P, 4, 512], F32))
    psB = ctx.enter_context(nc.psum_tensor("psB", [P, 4, 512], F32))

    def sems(*names):
        return {n: sem(n) for n in names}

    const_in = sem("const_in")
    loaded = [sem("tile_loaded_slot0"), sem("tile_loaded_slot1")]
    stored = [sem("x5_stored_slot0"), sem("x5_stored_slot1")]
    dve_a, dve_b = sem("dve_own_results_a"), sem("dve_own_results_b")
    setup_done = sem("setup_done")
    setup_chain = sem("setup_chain")
    A = sems("xn", "xnT_mm", "xnT", "ctxT_mm", "ctxT_act", "ctxT_dve", "scores_mm", "scores", "probs", "probs_last",
             "probsT_mm", "probsT", "read_mm", "qkv_mm", "v", "rot", "rotT_mm", "rotT", "att_mm", "att_centred",
             "att_exp", "att", "attT_mm", "attT_act", "attT_dve", "pv_mm", "oT_act", "oT_dve", "wo_mm", "gate_mm",
             "up_mm", "exp_gate", "hid", "hT_mm", "hT_act", "hT_dve", "down_mm", "x3")
    B = sems("b_yn", "b_ynT_mm", "b_ynT", "b_q_mm", "b_q", "b_qT_mm", "b_qbd", "b_vlast_mm", "b_vlast",
             "b_k_mm", "b_v_mm", "b_ksq", "b_kss_mm", "b_kms", "b_kln", "b_krs", "b_kn", "b_v", "b_scores_mm", "b_max", "b_probs", "b_probs_last",
             "b_probsT_mm", "b_probsT_act", "b_probsT_dve", "b_pv_mm", "b_o", "b_oT_mm", "b_oT", "b_wo_mm",
             "b_qkv2_mm", "b_rot2", "b_rot2T_mm", "b_q2T", "b_k2bd", "b_att2_mm", "b_centred2", "b_exp2", "b_sum2",
             "b_att2T_mm", "b_att2T_act", "b_att2T_dve", "b_pv2_mm", "b_o2", "b_o2T_mm", "b_o2T", "b_wo2_mm", "b_x5")

    def run(eng, stage_a, stage_b):
        weave(stage_a, Tile(0, 0, 0), None, None)
        weave(stage_a, Tile(1, 1, 0), stage_b, Tile(0, 0, 0))
        weave(stage_a, Tile(2, 0, 1), stage_b, Tile(1, 1, 0))
        with eng.Fori(1, TILES // 2 - 1) as k:
            weave(stage_a, Tile(2 * k + 1, 1, k), stage_b, Tile(2 * k, 0, k))
            weave(stage_a, Tile(2 * k + 2, 0, k + 1), stage_b, Tile(2 * k + 1, 1, k))
        weave(stage_a, Tile(TILES - 1, 1, TILES // 2 - 1), stage_b, Tile(TILES - 2, 0, TILES // 2 - 1))
        weave(None, None, stage_b, Tile(TILES - 1, 1, TILES // 2 - 1))

    def weave(stage_a, ta, stage_b, tb):
        for name in ORDER:
            if name[0] == "a" and ta is not None and name in stage_a:
                stage_a[name](ta)
            if name[0] == "b" and tb is not None and name[:2] in stage_b:
                stage_b[name[:2]](tb, int(name[2:]))

    block = ctx.enter_context(nc.Block())

    @block.sync
    def _(sp):
        for dst, src in loads:
            sp.dma_start(dst[:], src).then_inc(const_in, 16)

        def load(t):
            if not t.slot_first:
                sp.wait_ge(A["xn"], t.upto(3, 2 - 6))
            done = loaded[t.slot]
            sp.dma_start(x_in[:, t.slot], a["x"][ds(t.i, 1)].rearrange("t p d -> (t p) d")).then_inc(done, 16)
            sp.dma_start(rows[:, t.slot].rearrange("p b c d -> p b (c d)"),
                         a["ctx"][ds(t.i * NB, NB), 0:MC * P].rearrange("b (p c) d -> p b (c d)", c=MC)).then_inc(done, 16)
            sp.dma_start(last_row[:, t.slot], a["ctx"][ds(t.i * NB, NB), M - 1]).then_inc(done, 16)
            sp.dma_start(mask_u8[:, t.slot], a["mask"][ds(t.i, 1)].rearrange("t p m -> (t p) m")).then_inc(done, 16)

        load(Tile(0, 0, 0))
        load(Tile(1, 1, 0))
        with sp.Fori(1, TILES // 2) as k:
            load(Tile(2 * k, 0, k))
            load(Tile(2 * k + 1, 1, k))

    @block.gpsimd
    def _(pool):
        def store(t):
            pool.wait_ge(B["b_x5"], t.upto(1, 1))
            pool.dma_start(x5_dram[ds(t.i * P, P)], x5[:, t.slot]).then_inc(stored[t.slot], 16)

        with pool.Fori(0, TILES // 2) as k:
            store(Tile(2 * k, 0, k))
            store(Tile(2 * k + 1, 1, k))
        for s in stored:
            pool.wait_ge(s, 16 * (TILES // 2))

    def wait_loaded(eng, t):
        eng.wait_ge(loaded[t.slot], t.n * 16 * LOADS + 16 * LOADS)

    @block.tensor
    def _(pe):
        pe.wait_ge(const_in, 16 * len(loads))
        pe.wait_ge(setup_done, 1)

        def transpose(out, in_):
            return pe.transpose(out, in_, ident[0:in_.shape[0], 0:in_.shape[0]])

        def xnT(t, k, bank):
            pe.wait_ge(A["xn"], t.upto(3, k))
            for c in range(KC):
                mm = transpose(psA[:, bank, c * P:(c + 1) * P], xn[:, c * P:(c + 1) * P])
            return mm

        def a01(t):
            wait_loaded(pe, t)
            if not t.first:
                pe.wait_ge(A["x3"], t.upto(1, 0))
            xnT(t, 1, 0)
            for c in range(KC):
                mm = transpose(psA[:, 0, 2 * P + c * NB:2 * P + (c + 1) * NB], last_row[:, t.slot, c * P:(c + 1) * P])
            mm.then_inc(A["xnT_mm"], 1)
            for b in range(NB):
                if b == NB - 1:
                    pe.wait_ge(A["xnT"], t.upto(3, 1))
                for kc in range(KC):
                    for c in range(MC):
                        at = (kc * MC + c) * P
                        mm = transpose(psA[:, (b + 1) % 4, at:at + P], rows[:, t.slot, b, c, kc * P:(kc + 1) * P])
                mm.then_inc(A["ctxT_mm"], 1)

        def a02(t):
            pe.wait_ge(A["xnT"], t.upto(3, 1))
            pe.wait_ge(A["ctxT_act"], t.upto(2, 2))
            pe.wait_ge(A["ctxT_dve"], t.upto(2, 2))
            for b in range(NB):
                for kc in range(KC):
                    mm = pe.matmul(psA[S * b:S * b + S, 1, 0:M], xnT_sb[:, kc, S * b:S * b + S],
                                   ctxT[:, t.slot, kc, b], start=(kc == 0), stop=(kc == KC - 1), tile_position=(0, S * b))
            mm.then_inc(A["scores_mm"], 1)

        def a03(t):
            pe.wait_ge(A["probs"], t.upto(1, 1))
            for c in range(MC):
                transpose(psA[:, 2, c * P:(c + 1) * P], p0[:, c * P:(c + 1) * P])
            pe.wait_ge(A["probs_last"], t.upto(1, 1))
            transpose(psA[0:NB, 2, 2 * P:3 * P], p0_last[:]).then_inc(A["probsT_mm"], 1)

        def a04(t):
            pe.wait_ge(A["probsT"], t.upto(1, 1))
            pe.matmul(psA[:, 3, 0:D], p0T_last[:], last_row[:, t.slot], start=True, stop=False, skip_group_check=True)
            for b in range(NB):
                for c in range(MC):
                    mm = pe.matmul(psA[S * b:S * b + S, 3, 0:D], p0T[:, c, S * b:S * b + S], rows[:, t.slot, b, c],
                                   start=False, stop=(c == MC - 1), tile_position=(0, S * b), skip_group_check=True)
            mm.then_inc(A["read_mm"], 1)

        def a05(t):
            xnT(t, 2, 0).then_inc(A["xnT_mm"], 1)

        def project(bank, w, lo, n):
            for kc in range(KC):
                mm = pe.matmul(psA[:, bank, 0:n], xnT_sb[:, kc], w[:, kc, lo:lo + n], start=(kc == 0), stop=(kc == KC - 1))
            return mm

        def a06(t):
            pe.wait_ge(A["xnT"], t.upto(3, 2))
            project(2, wkv0, 0, KV0).then_inc(A["qkv_mm"], 1)
            project(3, wkv0, KV0, KV0).then_inc(A["qkv_mm"], 1)
            project(0, wq0, 0, 512).then_inc(A["qkv_mm"], 1)
            project(1, wq0, 512, 512).then_inc(A["qkv_mm"], 1)

        def rotT(t, n, bank):
            pe.wait_ge(A["rot"], t.upto(5, n + 1))
            for c in range(4):
                mm = transpose(psA[:, bank, c * P:(c + 1) * P], rot[:, n % 2, c * P:(c + 1) * P])
            mm.then_inc(A["rotT_mm"], 1)

        def a07(t):
            rotT(t, 0, 2)
            pe.wait_ge(A["v"], t.upto(1, 1))
            rotT(t, 1, 3)
            project(0, wq0, 1024, 512).then_inc(A["qkv_mm"], 1)
            pe.wait_ge(A["rotT"], t.upto(5, 1))
            rotT(t, 2, 2)
            project(1, wq0, 1536, 512).then_inc(A["qkv_mm"], 1)
            pe.wait_ge(A["rotT"], t.upto(5, 2))
            rotT(t, 3, 3)
            pe.wait_ge(A["rotT"], t.upto(5, 3))
            rotT(t, 4, 2)

        def a08(t):
            pe.wait_ge(A["rotT"], t.upto(5, 5))
            for c in range(4):
                for b in range(NB):
                    for s in range(2):
                        mm = pe.matmul(psA[:, s, (c * NB + b) * S:(c * NB + b + 1) * S],
                                       qT[64 * s:64 * s + 64, c, b].rearrange("p j q -> p (j q)"),
                                       kT[64 * s:64 * s + 64, c, S * b:S * b + S], start=True, stop=True,
                                       tile_position=(64 * s, 0))
            mm.then_inc(A["att_mm"], 1)

        def a09(t):
            pe.wait_ge(A["att"], t.upto(1, 1))
            for s in range(2):
                for c in range(4):
                    at = s * 512 + c * P
                    mm = transpose(psA[:, 2 + s, c * P:(c + 1) * P], att[:, at:at + P])
                mm.then_inc(A["attT_mm"], 1)

        def a10(t):
            pe.wait_ge(A["attT_act"], t.upto(1, 1))
            pe.wait_ge(A["attT_dve"], t.upto(1, 1))
            for b in range(NB):
                for c in range(4):
                    for s in range(2):
                        g = 2 * c + s
                        mm = pe.matmul(psA[64 * s:64 * s + 64, b, c * P:(c + 1) * P], v0[S * b:S * b + S, g * HD0:(g + 1) * HD0],
                                       attT[S * b:S * b + S, s, c * P:(c + 1) * P], start=True, stop=True,
                                       tile_position=(S * b, 64 * s))
                mm.then_inc(A["pv_mm"], 1)

        def a11(t):
            pe.wait_ge(A["oT_act"], t.upto(2, 2))
            pe.wait_ge(A["oT_dve"], t.upto(2, 2))
            for c in range(16):
                mm = pe.matmul(psA[:, 0, 0:D], oT[:, c // 4, c % 4].rearrange("p b q -> p (b q)"), wo0[:, c],
                               start=(c == 0), stop=(c == 15))
            mm.then_inc(A["wo_mm"], 1)

        def a12(t):
            xnT(t, 3, 1).then_inc(A["xnT_mm"], 1)

        def a13(t):
            pe.wait_ge(A["xnT"], t.upto(3, 3))
            project(2, wgate0, 0, 512)
            project(3, wgate0, 512, 512).then_inc(A["gate_mm"], 1)
            project(0, wup0, 0, 512)
            project(1, wup0, 512, 512).then_inc(A["up_mm"], 1)

        def a14(t):
            pe.wait_ge(A["hid"], t.upto(1, 1))
            for h in range(2):
                for c in range(4):
                    at = h * 512 + c * P
                    mm = transpose(psA[:, 2 + h, c * P:(c + 1) * P], hid[:, at:at + P])
                mm.then_inc(A["hT_mm"], 1)

        def a15(t):
            pe.wait_ge(A["hT_act"], t.upto(1, 1))
            pe.wait_ge(A["hT_dve"], t.upto(1, 1))
            for c in range(FC):
                mm = pe.matmul(psA[:, 0, 0:D], hT[:, c * P:(c + 1) * P], wdown0[:, c], start=(c == 0), stop=(c == FC - 1))
            mm.then_inc(A["down_mm"], 1)

        def ynT_step(t, k, bank):
            pe.wait_ge(B["b_yn"], t.upto(2, k))
            for c in range(KC):
                mm = transpose(psB[:, bank, c * P:(c + 1) * P], yn[:, c * P:(c + 1) * P])
            mm.then_inc(B["b_ynT_mm"], 1)

        def ba(t, n):
            if n == 0:
                if not t.first:
                    pe.wait_ge(B["b_x5"], t.upto(1, 0))
                ynT_step(t, 1, 0)
            if n == 1:
                pe.wait_ge(B["b_ynT"], t.upto(2, 1))
                for kc in range(KC):
                    mm = pe.matmul(psB[:, 1, 0:D], ynT[:, kc], wq1[:, kc], start=(kc == 0), stop=(kc == KC - 1))
                mm.then_inc(B["b_q_mm"], 1)
                for kc in range(KC):
                    mm = pe.matmul(psB[0:NB, 3, 0:D], ctxT[:, t.slot, kc, :, M - 1], wv1[:, kc], start=(kc == 0),
                                   stop=(kc == KC - 1))
                mm.then_inc(B["b_vlast_mm"], 1)
            if n == 2:
                pe.wait_ge(B["b_q"], t.upto(1, 1))
                for c in range(KC):
                    mm = transpose(psB[:, 2, c * P:(c + 1) * P], q1[:, c * P:(c + 1) * P])
                mm.then_inc(B["b_qT_mm"], 1)

        def bb(t, b):
            if b == 0:
                pe.wait_ge(B["b_q"], t.upto(1, 1))
                pe.wait_ge(B["b_vlast"], t.upto(1, 1))
                pe.wait_ge(B["b_qbd"], t.upto(1, 1))
            else:
                pe.wait_ge(B["b_o"], t.upto(NB, b))
            for m in range(KC):
                for kc in range(KC):
                    mm = pe.matmul(psB[:, m, 0:M], wk1[:, kc, m * P:(m + 1) * P], ctxT[:, t.slot, kc, b],
                                   start=(kc == 0), stop=(kc == KC - 1))
            mm.then_inc(B["b_k_mm"], 1)
            for c in range(MC):
                for kc in range(KC):
                    mm = pe.matmul(psB[:, 2, c * D:(c + 1) * D], ctxT[:, t.slot, kc, b, c * P:(c + 1) * P], wv1[:, kc],
                                   start=(kc == 0), stop=(kc == KC - 1))
            mm.then_inc(B["b_v_mm"], 1)

        def bc(t, b):
            pe.wait_ge(B["b_ksq"], t.upto(NB, b + 1))
            for m in range(KC):
                mm = pe.matmul(psB[:, 3, 0:M], ones[:], ksq[:, m], start=(m == 0), stop=(m == KC - 1))
            mm.then_inc(B["b_kss_mm"], 1)

        def bd(t, b):
            pe.wait_ge(B["b_kn"], t.upto(NB, b + 1))
            pe.wait_ge(B["b_v"], t.upto(NB, b + 1))
            for j in range(REP):
                r = 64 * (j % 2)
                mm = pe.matmul(psB[:, j, 0:M], qbd[r:r + 64, j // 2, b].rearrange("p h q -> p (h q)"),
                               k1n[r:r + 64, j // 2], start=True, stop=True, tile_position=(r, 0))
            mm.then_inc(B["b_scores_mm"], 1)

        def be(t, b):
            pe.wait_ge(B["b_probs"], t.upto(NB, b + 1))
            for j in range(REP):
                for c in range(MC):
                    mm = transpose(psB[:, j // 2, ((j % 2) * MC + c) * P:((j % 2) * MC + c + 1) * P],
                                   p1[:, j, c * P:(c + 1) * P])
                if j % 2 == 1:
                    mm.then_inc(B["b_probsT_mm"], 1)
            pe.wait_ge(B["b_probs_last"], t.upto(NB, b + 1))
            for j in range(REP):
                mm = transpose(psB[0:NB, 2, j * P:(j + 1) * P], p1_last[:, b, j])
            mm.then_inc(B["b_probsT_mm"], 1)

        def bf(t, b):
            pe.wait_ge(B["b_probsT_act"], t.upto(2 * NB, 2 * b + 2))
            pe.wait_ge(B["b_probsT_dve"], t.upto(NB, b + 1))
            for j in range(REP):
                for c in range(MC):
                    at = (j * MC + c) * P
                    pe.matmul(psB[:, 3, j * 64:(j + 1) * 64], p1T[:, at:at + P], v1[:, c, j * 64:(j + 1) * 64],
                              start=(c == 0), stop=False)
                mm = pe.matmul(psB[:, 3, j * 64:(j + 1) * 64], p1T_last[:, j * P:(j + 1) * P],
                               v1_last[:, j * 64:(j + 1) * 64], start=False, stop=True)
            mm.then_inc(B["b_pv_mm"], 1)

        def out_T(src, bank):
            for b in range(NB):
                mm = transpose(psB[0:64, bank, b * P:(b + 1) * P], src[:, b].rearrange("p h d -> p (h d)"))
            return mm

        def out_w(srcT, w, bank):
            for h in range(REP):
                mm = pe.matmul(psB[:, bank, 0:D], srcT[:, h].rearrange("p b q -> p (b q)"), w[:, h], start=(h == 0),
                               stop=(h == REP - 1))
            return mm

        def bg(t, n):
            if n == 0:
                pe.wait_ge(setup_done, 1)
                pe.wait_ge(B["b_o"], t.upto(NB, NB))
                out_T(o1, 0).then_inc(B["b_oT_mm"], 1)
            if n == 1:
                pe.wait_ge(B["b_oT"], t.upto(1, 1))
                out_w(o1T, wo1, 1).then_inc(B["b_wo_mm"], 1)
            if n == 2:
                ynT_step(t, 2, 2)
            if n == 3:
                pe.wait_ge(B["b_ynT"], t.upto(2, 2))
                for kc in range(KC):
                    mm = pe.matmul(psB[:, 3, 0:384], ynT[:, kc], wqkv2[:, kc], start=(kc == 0), stop=(kc == KC - 1))
                mm.then_inc(B["b_qkv2_mm"], 1)
            if n == 4:
                pe.wait_ge(setup_done, 1)
                pe.wait_ge(B["b_rot2"], t.upto(1, 1))
                for j in range(REP):
                    transpose(psB[0:64, 0, j * P:(j + 1) * P], rc2[:, j * 64:(j + 1) * 64])
                transpose(psB[0:64, 1, 0:P], rc2[:, 256:320]).then_inc(B["b_rot2T_mm"], 1)
            if n == 5:
                pe.wait_ge(B["b_q2T"], t.upto(1, 1))
                pe.wait_ge(B["b_k2bd"], t.upto(1, 1))
                for b in range(NB):
                    for h in range(2):
                        o = psB[:, 2 + h].rearrange("p (g b k) -> p g b k", g=4, b=NB)[:, :, b]
                        mm = pe.matmul(o, q2T[:, b].rearrange("p j q -> p (j q)"), k2bd[:, b, 4 * h:4 * h + 4],
                                       start=True, stop=True)
                mm.then_inc(B["b_att2_mm"], 1)
            if n == 6:
                pe.wait_ge(B["b_exp2"], t.upto(1, 1))
                for h in range(2):
                    for g in range(4):
                        at = (4 * h + g) * P
                        mm = transpose(psB[:, h, g * P:(g + 1) * P], att2[:, at:at + P])
                    mm.then_inc(B["b_att2T_mm"], 1)
            if n == 7:
                pe.wait_ge(B["b_att2T_act"], t.upto(1, 1))
                pe.wait_ge(B["b_att2T_dve"], t.upto(1, 1))
                for g in range(G2):
                    mm = pe.matmul(psB[:, 2, g * 32:(g + 1) * 32], att2T[:, g * P:(g + 1) * P],
                                   v2bd[:, g].rearrange("p b d -> p (b d)"), start=True, stop=True)
                mm.then_inc(B["b_pv2_mm"], 1)
            if n == 8:
                pe.wait_ge(setup_done, 1)
                pe.wait_ge(B["b_o2"], t.upto(1, 1))
                out_T(o2, 3).then_inc(B["b_o2T_mm"], 1)
            if n == 9:
                pe.wait_ge(B["b_o2T"], t.upto(1, 1))
                out_w(o2T, wo2, 0).then_inc(B["b_wo2_mm"], 1)

        run(pe, dict(a01=a01, a02=a02, a03=a03, a04=a04, a05=a05, a06=a06, a07=a07, a08=a08, a09=a09, a10=a10, a11=a11,
                     a12=a12, a13=a13, a14=a14, a15=a15), dict(ba=ba, bb=bb, bc=bc, bd=bd, be=be, bf=bf, bg=bg))

    @block.scalar
    def _(act):
        act.wait_ge(const_in, 16 * len(loads))

        def xnT_copy(t, k, bank):
            act.wait_ge(A["xnT_mm"], t.upto(3, k))
            return act.copy(xnT_sb[:].rearrange("p c q -> p (c q)"), psA[:, bank, 0:D])

        def a01(t):
            ins = xnT_copy(t, 1, 0)
            act.copy(ctxT[:, t.slot, :, :, M - 1], psA[:, 0, D:D + KC * NB].rearrange("p (c b) -> p c b", c=KC)
                     ).then_inc(A["xnT"], 1)
            for b in (0, 2):
                act.wait_ge(A["ctxT_mm"], t.upto(NB, b + 1))
                act.copy(ctxT[:, t.slot, :, b, 0:MC * P], psA[:, b + 1, :].rearrange("p (k m) -> p k m", k=KC)
                         ).then_inc(A["ctxT_act"], 1)

        def a02(t):
            act.wait_ge(A["scores"], t.upto(1, 1))
            act.activation(p0[:], sc0[:], ACT.Exp, bias=small[:, 1:2], accum_out=small[:, 2:3]).then_inc(A["probs"], 1)

        def a03(t):
            act.wait_ge(A["probsT_mm"], t.upto(1, 1))
            act.copy(p0T[:].rearrange("p c q -> p (c q)"), psA[:, 2, 0:MC * P])
            act.copy(p0T_last[:], psA[0:NB, 2, MC * P:(MC + 1) * P]).then_inc(A["probsT"], 1)

        def a05(t):
            xnT_copy(t, 2, 0).then_inc(A["xnT"], 1)

        def a06(t):
            act.wait_ge(A["qkv_mm"], t.upto(6, 2))
            act.copy(v0[:], psA[:, 3, :]).then_inc(A["v"], 1)

        def a07(t):
            act.wait_ge(A["rotT_mm"], t.upto(5, 1))
            act.copy(kT[:].rearrange("p c q -> p (c q)"), psA[:, 2, :]).then_inc(A["rotT"], 1)
            for c in range(4):
                act.wait_ge(A["rotT_mm"], t.upto(5, c + 2))
                act.copy(qT[:, c].rearrange("p b j q -> p j b q"),
                         psA[:, 3 - c % 2, :].rearrange("p (j b q) -> p j b q", j=REP, b=NB)).then_inc(A["rotT"], 1)

        def a08(t):
            act.wait_ge(A["att_centred"], t.upto(1, 1))
            act.activation(att[:], att[:], ACT.Exp).then_inc(A["att_exp"], 1)

        def a09(t):
            act.wait_ge(A["attT_mm"], t.upto(2, 1))
            act.copy(attT[:, 0], psA[:, 2, :]).then_inc(A["attT_act"], 1)

        def a10(t):
            for b in (0, 2):
                act.wait_ge(A["pv_mm"], t.upto(NB, b + 1))
                act.copy(oT[:, :, :, b], psA[:, b, :].rearrange("p (c j q) -> p c j q", c=4, j=REP)).then_inc(A["oT_act"], 1)

        def a12(t):
            xnT_copy(t, 3, 1).then_inc(A["xnT"], 1)

        def a13(t):
            act.wait_ge(A["gate_mm"], t.upto(1, 1))
            act.activation(th, psA[:, 2:4, :].rearrange("p a n -> p (a n)"), ACT.Exp, scale=-1.0).then_inc(A["exp_gate"], 1)

        def a14(t):
            act.wait_ge(A["hT_mm"], t.upto(2, 1))
            act.copy(hT[:, 0:512], psA[:, 2, :]).then_inc(A["hT_act"], 1)

        def ynT_copy(t, k, bank):
            act.wait_ge(B["b_ynT_mm"], t.upto(2, k))
            act.copy(ynT[:].rearrange("p c q -> p (c q)"), psB[:, bank, 0:D]).then_inc(B["b_ynT"], 1)

        def ba(t, n):
            if n == 0:
                ynT_copy(t, 1, 0)
            if n == 1:
                act.wait_ge(B["b_vlast_mm"], t.upto(1, 1))
                act.copy(v1_last[:], psB[0:NB, 3, 0:D]).then_inc(B["b_vlast"], 1)

        def bb(t, b):
            act.wait_ge(B["b_k_mm"], t.upto(NB, b + 1))
            for m in range(KC):
                ins = act.activation(ksq[:, m], psB[:, m, 0:M], ACT.Square, bias=bk1[:, m:m + 1])
            ins.then_inc(B["b_ksq"], 1)
            act.wait_ge(B["b_v_mm"], t.upto(NB, b + 1))
            act.copy(v1[:].rearrange("p c d -> p (c d)"), psB[:, 2, :]).then_inc(B["b_v"], 1)

        def bc(t, b):
            act.wait_ge(B["b_kms"], t.upto(NB, b + 1))
            act.activation(krs[:], kms[:], ACT.Ln).then_inc(B["b_kln"], 1)
            act.wait_ge(B["b_kln"], t.upto(NB, b + 1))
            act.activation(krs[:], krs[:], ACT.Exp, scale=-0.5).then_inc(B["b_krs"], 1)

        def bd(t, b):
            act.wait_ge(B["b_max"], t.upto(NB, b + 1))
            for j in range(REP):
                ins = act.activation(p1[:, j], psB[:, j, 0:M], ACT.Exp, bias=p1max[:, j:j + 1], scale=HD1 ** -0.5,
                                     accum_out=p1sum[:, j:j + 1])
            ins.then_inc(B["b_probs"], 1)

        def be(t, b):
            act.wait_ge(B["b_probsT_mm"], t.upto(3 * NB, 3 * b + 1))
            act.copy(p1T[:, 0:512], psB[:, 0, :]).then_inc(B["b_probsT_act"], 1)
            act.wait_ge(B["b_probsT_mm"], t.upto(3 * NB, 3 * b + 3))
            act.copy(p1T_last[:], psB[0:NB, 2, :]).then_inc(B["b_probsT_act"], 1)

        def bg(t, n):
            if n == 0:
                act.wait_ge(B["b_oT_mm"], t.upto(1, 1))
                for h in range(REP):
                    ins = act.activation(o1T[:, h], psB[0:64, 0, :].rearrange("p (b h q) -> p b h q", b=NB, h=REP)[:, :, h],
                                         ACT.Identity, bias=bv1[:, h:h + 1])
                ins.then_inc(B["b_oT"], 1)
            if n == 2:
                ynT_copy(t, 2, 2)
            if n == 4:
                act.wait_ge(B["b_rot2T_mm"], t.upto(1, 1))
                act.copy(q2T.rearrange("p b j q -> p j b q"),
                         psB[0:64, 0, :].rearrange("p (j b q) -> p j b q", j=REP, b=NB)).then_inc(B["b_q2T"], 1)
            if n == 5:
                act.wait_ge(B["b_centred2"], t.upto(1, 1))
                act.activation(att2, att2, ACT.Exp, scale=float(1 / np.sqrt(np.float32(HD2)))).then_inc(B["b_exp2"], 1)
            if n == 6:
                act.wait_ge(B["b_att2T_mm"], t.upto(2, 1))
                act.copy(att2T[:, 0:512], psB[:, 0, :]).then_inc(B["b_att2T_act"], 1)
            if n == 8:
                act.wait_ge(B["b_o2T_mm"], t.upto(1, 1))
                act.copy(o2T[:].rearrange("p j b q -> p b j q"),
                         psB[0:64, 3, :].rearrange("p (b j q) -> p b j q", b=NB, j=REP)).then_inc(B["b_o2T"], 1)

        run(act, dict(a01=a01, a02=a02, a03=a03, a05=a05, a06=a06, a07=a07, a08=a08, a09=a09, a10=a10, a12=a12, a13=a13,
                      a14=a14), dict(ba=ba, bb=bb, bc=bc, bd=bd, be=be, bg=bg))

    @block.vector
    def _(dve):
        dve.wait_ge(const_in, 16 * len(loads))
        dve.memset(ones[:], 1.0)
        dve.memset(p1_last[:], 0.0).then_inc(setup_chain, 1)
        for c in range(KC):
            ins = dve.tensor_scalar(gk_rows[:, c], head_rows[:], gk1[:, c:c + 1], None, ALU.mult)
        ins.then_inc(setup_chain, 1)
        dve.wait_ge(setup_chain, 2)
        dve.memset(small[:, 7:8], 0.0).then_inc(setup_done, 1)
        ca = Chain(dve, dve_a, CHAIN_A)
        cb = Chain(dve, dve_b, CHAIN_B)

        def norm(chain, x, y, stats, mv):
            return layer_norm(dve, chain, x, y[:], stats[:], mv)

        def a01(t):
            ca.open(t)
            wait_loaded(dve, t)
            norm(ca, x_in[:, t.slot], xn, stats, mv).then_inc(A["xn"], 1)
            m8 = mask_u8[:, t.slot]
            dve.tensor_scalar(maskadd[:, 0:MC * P].rearrange("p (c r) -> p c r", c=MC),
                              m8[:, 0:MC * P].rearrange("p (r c) -> p c r", c=MC), 1.0, -NEG, ALU.subtract, ALU.mult)
            dve.tensor_scalar(maskadd[:, M - 1:M], m8[:, M - 1:M], 1.0, -NEG, ALU.subtract, ALU.mult)
            ca.done(dve.tensor_reduce(small[:, 0:1], m8, AX.X, ALU.max))
            for b in (1, 3):
                dve.wait_ge(A["ctxT_mm"], t.upto(NB, b + 1))
                dve.tensor_copy(ctxT[:, t.slot, :, b, 0:MC * P],
                                psA[:, (b + 1) % 4, :].rearrange("p (k m) -> p k m", k=KC)).then_inc(A["ctxT_dve"], 1)

        def a02(t):
            dve.wait_ge(A["scores_mm"], t.upto(1, 1))
            ca.done(dve.scalar_tensor_tensor(sc0[:], psA[:, 1, 0:M], D ** -0.5, maskadd[:], ALU.mult, ALU.add))
            ca.done(dve.tensor_reduce(small[:, 3:4], sc0[:], AX.X, ALU.max))
            dve.tensor_scalar(small[:, 1:2], small[:, 3:4], -1.0, None, ALU.mult).then_inc(A["scores"], 1)
            dve.wait_ge(A["probs"], t.upto(1, 1))
            dve.tensor_scalar(p0_last[:], own_batch[:], p0[:, M - 1:M], None, ALU.mult).then_inc(A["probs_last"], 1)
            ca.done(dve.reciprocal(small[:, 4:5], small[:, 2:3]))
            ca.done(dve.tensor_tensor(small[:, 5:6], small[:, 4:5], small[:, 0:1], ALU.mult))

        def a04(t):
            dve.wait_ge(A["read_mm"], t.upto(1, 1))
            ca.done(dve.scalar_tensor_tensor(x1[:], psA[:, 3, 0:D], small[:, 5:6], x_in[:, t.slot], ALU.mult, ALU.add))
            norm(ca, x1[:], xn, stats, mv).then_inc(A["xn"], 1)

        def rope(t, n, mm, bank):
            if n >= 2:
                dve.wait_ge(A["rotT_mm"], t.upto(5, n - 1))
            dve.wait_ge(A["qkv_mm"], t.upto(6, mm))
            v = psA[:, bank, :].rearrange("p (h d) -> p h d", d=HD0)
            c3, s3 = (r.rearrange("p (h d) -> p h d", d=HD0) for r in (rope_c, rope_s))
            h = HD0 // 2
            dve.tensor_tensor(c3, v, cos0[:].unsqueeze(1).broadcast_to([P, 8, HD0]), ALU.mult)
            dve.tensor_tensor(s3[:, :, 0:h], v[:, :, h:], sin0[:, 0:h].unsqueeze(1).broadcast_to([P, 8, h]), ALU.mult)
            ca.done(dve.tensor_tensor(s3[:, :, h:], v[:, :, 0:h], sin0[:, h:].unsqueeze(1).broadcast_to([P, 8, h]), ALU.mult))
            dve.tensor_tensor(rot[:, n % 2], rope_c, rope_s, ALU.add).then_inc(A["rot"], 1)
            dve.wait_ge(A["rot"], t.upto(5, n + 1))

        def a06(t):
            rope(t, 0, 1, 2)
            rope(t, 1, 3, 0)

        def a07(t):
            rope(t, 2, 4, 1)
            rope(t, 3, 5, 0)
            rope(t, 4, 6, 1)

        def segments(x, n=32):
            return x.rearrange("p (g k) -> p g k", g=n)

        def a08(t):
            dve.wait_ge(A["att_mm"], t.upto(1, 1))
            s3 = segments(att[:])
            ca.done(dve.scalar_tensor_tensor(s3, psA[:, 0:2, :].rearrange("p a (g k) -> p (a g) k", k=S), HD0 ** -0.5,
                                             causal[:].unsqueeze(1).broadcast_to([P, 32, S]), ALU.mult, ALU.add))
            ca.done(dve.tensor_reduce(att_max[:], s3, AX.X, ALU.max))
            dve.tensor_tensor(s3, s3, att_max[:].unsqueeze(2).broadcast_to([P, 32, S]), ALU.subtract
                              ).then_inc(A["att_centred"], 1)
            dve.wait_ge(A["att_exp"], t.upto(1, 1))
            ca.done(dve.tensor_reduce(att_sum[:], s3, AX.X, ALU.add))
            ca.done(dve.reciprocal(att_sum[:], att_sum[:]))
            dve.tensor_tensor(s3, s3, att_sum[:].unsqueeze(2).broadcast_to([P, 32, S]), ALU.mult).then_inc(A["att"], 1)

        def a09(t):
            dve.wait_ge(A["attT_mm"], t.upto(2, 2))
            dve.tensor_copy(attT[:, 1], psA[:, 3, :]).then_inc(A["attT_dve"], 1)

        def a10(t):
            for b in (1, 3):
                dve.wait_ge(A["pv_mm"], t.upto(NB, b + 1))
                dve.tensor_copy(oT[:, :, :, b], psA[:, b, :].rearrange("p (c j q) -> p c j q", c=4, j=REP)
                                ).then_inc(A["oT_dve"], 1)

        def a11(t):
            dve.wait_ge(A["wo_mm"], t.upto(1, 1))
            ca.done(dve.tensor_tensor(x2[:], psA[:, 0, 0:D], x1[:], ALU.add))
            norm(ca, x2[:], xn, stats, mv).then_inc(A["xn"], 1)

        def a13(t):
            dve.wait_ge(A["exp_gate"], t.upto(1, 1))
            ca.done(dve.tensor_scalar(th, th, 1.0, None, ALU.add))
            ca.done(dve.reciprocal(th, th))
            ca.done(dve.tensor_tensor(hid, psA[:, 2:4, :].rearrange("p a n -> p (a n)"), th, ALU.mult))
            dve.wait_ge(A["up_mm"], t.upto(1, 1))
            dve.tensor_tensor(hid, hid, psA[:, 0:2, :].rearrange("p a n -> p (a n)"), ALU.mult).then_inc(A["hid"], 1)

        def a14(t):
            dve.wait_ge(A["hT_mm"], t.upto(2, 2))
            dve.tensor_copy(hT[:, 512:1024], psA[:, 3, :]).then_inc(A["hT_dve"], 1)

        def a15(t):
            dve.wait_ge(A["down_mm"], t.upto(1, 1))
            dve.scalar_tensor_tensor(x3[:, t.slot], psA[:, 0, 0:D], 1.0, x2[:], ALU.mult, ALU.add).then_inc(A["x3"], 1)
            ca.close()

        def ba(t, n):
            if n == 0:
                cb.open(t)
                dve.wait_ge(A["x3"], t.upto(1, 1))
                norm(cb, x3[:, t.slot], yn, stats_b, mv_b).then_inc(B["b_yn"], 1)
                dve.tensor_tensor(x3b[:], x3[:, t.slot], bo1[:], ALU.add)
            if n == 1:
                dve.wait_ge(B["b_q_mm"], t.upto(1, 1))
                cb.done(dve.tensor_tensor(q1[:], psB[:, 1, 0:D], bq1[:], ALU.add))
                cb.done(dve.tensor_tensor(q1sq[:], q1[:], q1[:], ALU.mult))
                cb.done(dve.tensor_reduce(q1ss[:, 0:1], q1sq[:], AX.X, ALU.add))
                cb.done(dve.tensor_scalar(q1ss[:, 0:1], q1ss[:, 0:1], 1.0 / D, 1e-6, ALU.mult, ALU.add))
                inverse_root(dve, cb, q1ss[:, 0:1], q1ss[:, 1:2], q1ss[:, 2:3])
                dve.scalar_tensor_tensor(q1[:], q1[:], q1ss[:, 1:2], gq1[:], ALU.mult, ALU.mult).then_inc(B["b_q"], 1)
            if n == 2:
                dve.wait_ge(B["b_qT_mm"], t.upto(1, 1))
                for c in range(KC):
                    ins = dve.tensor_tensor(
                        qbd[:, c],
                        psB[:, 2, c * P:(c + 1) * P].rearrange("p (b q) -> p b q", b=NB).unsqueeze(2).broadcast_to([P, NB, REP, S]),
                        gk_rows[:, c].unsqueeze(1).unsqueeze(3).broadcast_to([P, NB, REP, S]), ALU.mult)
                ins.then_inc(B["b_qbd"], 1)

        def bc(t, b):
            dve.wait_ge(B["b_kss_mm"], t.upto(NB, b + 1))
            dve.tensor_scalar(kms[:], psB[:, 3, 0:M], 1.0 / D, 1e-6, ALU.mult, ALU.add).then_inc(B["b_kms"], 1)
            dve.wait_ge(B["b_krs"], t.upto(NB, b + 1))
            cb.done(dve.tensor_tensor(kms[:], kms[:], krs[:], ALU.mult))
            cb.done(dve.tensor_tensor(kms[:], kms[:], krs[:], ALU.mult))
            cb.done(dve.tensor_scalar(kms[:], kms[:], -0.5, 1.5, ALU.mult, ALU.add))
            cb.done(dve.tensor_tensor(krs[:], kms[:], krs[:], ALU.mult))
            for m in range(KC):
                ins = dve.scalar_tensor_tensor(k1n[:, m], psB[:, m, 0:M], bk1[:, m:m + 1], krs[:], ALU.add, ALU.mult)
            ins.then_inc(B["b_kn"], 1)

        def bd(t, b):
            dve.wait_ge(B["b_scores_mm"], t.upto(NB, b + 1))
            cb.done(dve.tensor_reduce(p1max[:], psB[:, :, 0:M], AX.X, ALU.max))
            dve.tensor_scalar(p1max[:], p1max[:], -HD1 ** -0.5, None, ALU.mult).then_inc(B["b_max"], 1)
            dve.wait_ge(B["b_probs"], t.upto(NB, b + 1))
            dve.tensor_copy(p1_last[:, b, :, b], p1[:, :, M - 1]).then_inc(B["b_probs_last"], 1)
            cb.done(dve.reciprocal(p1rec[:], p1sum[:]))

        def be(t, b):
            dve.wait_ge(B["b_probsT_mm"], t.upto(3 * NB, 3 * b + 2))
            dve.tensor_copy(p1T[:, 512:1024], psB[:, 1, :]).then_inc(B["b_probsT_dve"], 1)

        def bf(t, b):
            dve.wait_ge(B["b_pv_mm"], t.upto(NB, b + 1))
            for h in range(REP):
                r = slice(S * h, S * h + S)
                ins = dve.tensor_tensor(o1[r, b], psB[r, 3, 0:D].rearrange("p (j h d) -> p j h d", j=REP, h=REP)[:, :, h],
                                        p1rec[r].unsqueeze(2).broadcast_to([S, REP, HD1]), ALU.mult)
            ins.then_inc(B["b_o"], 1)

        def bg(t, n):
            if n == 1:
                dve.wait_ge(B["b_wo_mm"], t.upto(1, 1))
                cb.done(dve.tensor_tensor(x4[:], psB[:, 1, 0:D], x3b[:], ALU.add))
                norm(cb, x4[:], yn, stats_b, mv_b).then_inc(B["b_yn"], 1)
                dve.tensor_tensor(x4b[:], x4[:], bo2[:], ALU.add)
            if n == 3:
                dve.wait_ge(B["b_qkv2_mm"], t.upto(1, 1))
                cb.done(dve.tensor_tensor(qkv[:], psB[:, 3, 0:384], bqkv2[:], ALU.add))
                v = qkv[:, 0:320].rearrange("p (h d) -> p h d", d=HD2)
                c3, s3 = (r[:].rearrange("p (h d) -> p h d", d=HD2) for r in (rc2, rs2))
                h, n_h = HD2 // 2, 320 // HD2
                dve.tensor_tensor(c3, v, cos2[:].unsqueeze(1).broadcast_to([P, n_h, HD2]), ALU.mult)
                dve.tensor_tensor(s3[:, :, 0:h], v[:, :, h:], sin2[:, 0:h].unsqueeze(1).broadcast_to([P, n_h, h]), ALU.mult)
                cb.done(dve.tensor_tensor(s3[:, :, h:], v[:, :, 0:h], sin2[:, h:].unsqueeze(1).broadcast_to([P, n_h, h]), ALU.mult))
                dve.tensor_tensor(rc2[:], rc2[:], rs2[:], ALU.add).then_inc(B["b_rot2"], 1)
                dve.tensor_tensor(v2bd, qkv[:, 320:384].rearrange("p (g d) -> p g d", g=G2).unsqueeze(2).broadcast_to([P, G2, NB, HD2]),
                                  own_batch[:].unsqueeze(1).unsqueeze(3).broadcast_to([P, G2, NB, HD2]), ALU.mult)
            if n == 4:
                dve.wait_ge(B["b_rot2T_mm"], t.upto(1, 1))
                dve.tensor_tensor(k2bd, psB[0:64, 1, 0:P].rearrange("p (b k) -> p b k", b=NB).unsqueeze(2).broadcast_to([64, NB, G2, S]),
                                  group_rows[:].unsqueeze(1).unsqueeze(3).broadcast_to([64, NB, G2, S]), ALU.mult).then_inc(B["b_k2bd"], 1)
            if n == 5:
                dve.wait_ge(B["b_att2_mm"], t.upto(1, 1))
                ps = psB[:, 2:4, :].rearrange("p a (g k) -> p (a g) k", k=S)
                s3 = segments(att2)
                cb.done(dve.tensor_reduce(att2_max[:], ps, AX.X, ALU.max))
                dve.tensor_tensor(s3, ps, att2_max[:].unsqueeze(2).broadcast_to([P, 32, S]), ALU.subtract).then_inc(B["b_centred2"], 1)
                dve.wait_ge(B["b_exp2"], t.upto(1, 1))
                cb.done(dve.tensor_reduce(att2_sum[:], s3, AX.X, ALU.add))
                cb.done(dve.reciprocal(att2_sum[:], att2_sum[:]))
            if n == 6:
                dve.wait_ge(B["b_att2T_mm"], t.upto(2, 2))
                dve.tensor_copy(att2T[:, 512:1024], psB[:, 1, :]).then_inc(B["b_att2T_dve"], 1)
            if n == 7:
                dve.wait_ge(B["b_pv2_mm"], t.upto(1, 1))
                dve.tensor_tensor(o2.rearrange("p b g d -> p g b d"), psB[:, 2, 0:D].rearrange("p (g b d) -> p g b d", g=G2, b=NB),
                                  att2_sum[:].rearrange("p (g b) -> p g b", g=G2).unsqueeze(3).broadcast_to([P, G2, NB, HD2]), ALU.mult
                                  ).then_inc(B["b_o2"], 1)
            if n == 9:
                dve.wait_ge(B["b_wo2_mm"], t.upto(1, 1))
                if not t.slot_first:
                    dve.wait_ge(stored[t.slot], 16 * t.n)
                dve.tensor_tensor(x5[:, t.slot], psB[:, 0, 0:D], x4b[:], ALU.add).then_inc(B["b_x5"], 1)
                cb.close()

        run(dve, dict(a01=a01, a02=a02, a04=a04, a06=a06, a07=a07, a08=a08, a09=a09, a10=a10, a11=a11, a13=a13, a14=a14,
                      a15=a15), dict(ba=ba, bb=lambda t, b: None, bc=bc, bd=bd, be=be, bf=bf, bg=bg))


def mixture_of_experts(nc, ctx, a, ident, x5_dram, out):
    def sb(name, shape, dt=F32):
        return ctx.enter_context(nc.sbuf_tensor(name, shape, dt))

    def sem(name):
        return ctx.enter_context(nc.semaphore(name))

    def sems(*names):
        return {n: sem(n) for n in names}

    wg = sb("wg", [P, EXPERTS, KC, F])
    wu = sb("wu", [P, EXPERTS, KC, F])
    wd = sb("wd", [P, EXPERTS, FC, D])
    wr = sb("wr", [P, KC, EXPERTS])
    br = sb("br", [P, EXPERTS])
    rank = sb("rank", [P, EXPERTS])
    x5 = sb("x5m", [P, 2, D])
    xn = sb("xnm", [P, D])
    xnT = sb("xnTm", [P, 2, KC, P])
    stats = sb("stats_m", [P, 6])
    mv = sb("mv_m", [P, 4])
    lg = sb("lg", [P, EXPERTS])
    pr = sb("pr", [P, EXPERTS])
    r = sb("router", [P, 8])
    sel = sb("sel", [P, 2, EXPERTS])
    th = sb("th_m", [P, 2, F])
    hid = sb("hid_m", [P, 2, F])
    hT = sb("hT_m", [P, F])
    y = sb("y", [P, 2, D])

    ps_g = ctx.enter_context(nc.psum_tensor("ps_g", [P, 2, 512], F32))
    ps_u = ctx.enter_context(nc.psum_tensor("ps_u", [P, 2, 512], F32))
    ps_t = ctx.enter_context(nc.psum_tensor("ps_t", [P, 2, 512], F32))
    ps_y = ctx.enter_context(nc.psum_tensor("ps_y", [P, 512], F32))
    ps_x = ctx.enter_context(nc.psum_tensor("ps_x", [P, 512], F32))

    weights_in = [sem(f"expert_in{e}") for e in range(EXPERTS)]
    router_in = sem("router_in")
    loaded = [sem("m_loaded0"), sem("m_loaded1")]
    stored = [sem("m_stored0"), sem("m_stored1")]
    dve_m = sem("dve_own_m")
    C = sems("m_xn", "m_xnT_mm", "m_xnT", "m_logits_mm", "m_logits", "m_exp", "m_sel", "m_gate_mm", "m_up_mm", "m_exp_gate", "m_hid",
             "m_hT_mm", "m_hT_act", "m_hT_dve", "m_down_mm", "m_y")

    block = ctx.enter_context(nc.Block())

    def run(eng, norm, first, second):
        def tile(t, before):
            norm(t)
            for e in range(EXPERTS):
                first(t, e)
                if e > 0:
                    second(t, e - 1)
                elif before is not None:
                    second(before, EXPERTS - 1)

        tile(Tile(0, 0, 0), None)
        tile(Tile(1, 1, 0), Tile(0, 0, 0))
        tile(Tile(2, 0, 1), Tile(1, 1, 0))
        with eng.Fori(1, TILES // 2 - 1) as k:
            tile(Tile(2 * k + 1, 1, k), Tile(2 * k, 0, k))
            tile(Tile(2 * k + 2, 0, k + 1), Tile(2 * k + 1, 1, k))
        last = Tile(TILES - 1, 1, TILES // 2 - 1)
        tile(last, Tile(TILES - 2, 0, TILES // 2 - 1))
        second(last, EXPERTS - 1)

    @block.sync
    def _(sp):
        for dst, src in ((wr, "wr"), (br, "br"), (rank, "rank")):
            sp.dma_start(dst[:], a[src]).then_inc(router_in, 16)

        def load(t):
            if not t.slot_first:
                sp.wait_ge(C["m_y"], t.upto(1, -1))
            sp.dma_start(x5[:, t.slot], x5_dram[ds(t.i * P, P)]).then_inc(loaded[t.slot], 16)

        load(Tile(0, 0, 0))
        load(Tile(1, 1, 0))
        for e in range(EXPERTS):
            for dst, src in ((wg, "wg"), (wu, "wu"), (wd, "wd")):
                sp.dma_start(dst[:, e], a[src][:, e]).then_inc(weights_in[e], 16)
        with sp.Fori(1, TILES // 2) as k:
            load(Tile(2 * k, 0, k))
            load(Tile(2 * k + 1, 1, k))

    @block.gpsimd
    def _(pool):
        def store(t):
            pool.wait_ge(C["m_y"], t.upto(1, 1))
            pool.dma_start(out[ds(t.i * P, P)], y[:, t.slot]).then_inc(stored[t.slot], 16)

        with pool.Fori(0, TILES // 2) as k:
            store(Tile(2 * k, 0, k))
            store(Tile(2 * k + 1, 1, k))
        for s in stored:
            pool.wait_ge(s, 16 * (TILES // 2))

    @block.tensor
    def _(pe):
        pe.wait_ge(router_in, 48)

        def norm(t):
            pe.wait_ge(C["m_xn"], t.upto(1, 1))
            for c in range(KC):
                mm = pe.transpose(ps_x[:, c * P:(c + 1) * P], xn[:, c * P:(c + 1) * P], ident[:])
            mm.then_inc(C["m_xnT_mm"], 1)
            pe.wait_ge(C["m_xnT"], t.upto(1, 1))
            for c in range(KC):
                mm = pe.matmul(ps_x[:, 256:256 + EXPERTS], xnT[:, t.slot, c], wr[:, c], start=(c == 0), stop=(c == KC - 1))
            mm.then_inc(C["m_logits_mm"], 1)

        def first(t, e):
            if t.first:
                pe.wait_ge(weights_in[e], 48)
            if not (t.first and e == 0):
                pe.wait_ge(C["m_hid"], t.upto(EXPERTS, e))
            for ps, w, done in ((ps_g, wg, C["m_gate_mm"]), (ps_u, wu, C["m_up_mm"])):
                for h in range(2):
                    for c in range(KC):
                        mm = pe.matmul(ps[:, h], xnT[:, t.slot, c], w[:, e, c, h * 512:(h + 1) * 512], start=(c == 0),
                                       stop=(c == KC - 1))
                mm.then_inc(done, 1)

        def second(t, e):
            pe.wait_ge(C["m_hid"], t.upto(EXPERTS, e + 1))
            for h in range(2):
                for c in range(4):
                    at = h * 512 + c * P
                    mm = pe.transpose(ps_t[:, h, c * P:(c + 1) * P], hid[:, e % 2, at:at + P], ident[:])
                mm.then_inc(C["m_hT_mm"], 1)
            if e == 0 and not t.first:
                pe.wait_ge(C["m_y"], t.upto(1, 0))
            pe.wait_ge(C["m_hT_act"], t.upto(EXPERTS, e + 1))
            pe.wait_ge(C["m_hT_dve"], t.upto(EXPERTS, e + 1))
            for c in range(FC):
                mm = pe.matmul(ps_y[:, 0:D], hT[:, c * P:(c + 1) * P], wd[:, e, c], start=(e == 0 and c == 0),
                               stop=(e == EXPERTS - 1 and c == FC - 1))
            mm.then_inc(C["m_down_mm"], 1)

        run(pe, norm, first, second)

    @block.scalar
    def _(act):
        def norm(t):
            act.wait_ge(C["m_xnT_mm"], t.upto(1, 1))
            act.copy(xnT[:, t.slot].rearrange("p c q -> p (c q)"), ps_x[:, 0:D]).then_inc(C["m_xnT"], 1)
            act.wait_ge(C["m_logits"], t.upto(1, 1))
            act.activation(pr[:], lg[:], ACT.Exp, bias=r[:, 1:2], accum_out=r[:, 2:3]).then_inc(C["m_exp"], 1)

        def first(t, e):
            act.wait_ge(C["m_gate_mm"], t.upto(EXPERTS, e + 1))
            act.activation(th[:, e % 2], ps_g[:].rearrange("p a n -> p (a n)"), ACT.Exp, scale=-1.0).then_inc(C["m_exp_gate"], 1)

        def second(t, e):
            act.wait_ge(C["m_hT_mm"], t.upto(2 * EXPERTS, 2 * e + 1))
            act.copy(hT[:, 0:512], ps_t[:, 0]).then_inc(C["m_hT_act"], 1)

        run(act, norm, first, second)

    @block.vector
    def _(dve):
        dve.wait_ge(router_in, 48)
        cm = Chain(dve, dve_m, CHAIN_M)

        def norm(t):
            cm.open(t)
            dve.wait_ge(loaded[t.slot], t.n * 16 + 16)
            layer_norm(dve, cm, x5[:, t.slot], xn[:], stats[:], mv).then_inc(C["m_xn"], 1)
            dve.wait_ge(C["m_logits_mm"], t.upto(1, 1))
            cm.done(dve.tensor_tensor(lg[:], ps_x[:, 256:256 + EXPERTS], br[:], ALU.add))
            cm.done(dve.tensor_reduce(r[:, 0:1], lg[:], AX.X, ALU.max))
            dve.tensor_scalar(r[:, 1:2], r[:, 0:1], -1.0, None, ALU.mult).then_inc(C["m_logits"], 1)
            dve.wait_ge(C["m_exp"], t.upto(1, 1))
            cm.done(dve.reciprocal(r[:, 3:4], r[:, 2:3]))
            cm.done(dve.tensor_reduce(r[:, 4:5], pr[:], AX.X, ALU.max))
            cm.done(dve.scalar_tensor_tensor(lg[:], pr[:], r[:, 4:5], rank[:], ALU.is_equal, ALU.mult))
            cm.done(dve.tensor_tensor(r[:, 3:4], r[:, 3:4], r[:, 4:5], ALU.mult))
            cm.done(dve.tensor_reduce(r[:, 5:6], lg[:], AX.X, ALU.max))
            cm.done(dve.tensor_scalar(sel[:, t.slot], lg[:], r[:, 5:6], r[:, 3:4], ALU.is_equal, ALU.mult))

        def first(t, e):
            dve.wait_ge(C["m_exp_gate"], t.upto(EXPERTS, e + 1))
            cm.done(dve.tensor_scalar(th[:, e % 2], th[:, e % 2], 1.0, None, ALU.add))
            cm.done(dve.reciprocal(th[:, e % 2], th[:, e % 2]))
            cm.done(dve.tensor_tensor(th[:, e % 2], ps_g[:].rearrange("p a n -> p (a n)"), th[:, e % 2], ALU.mult))
            dve.wait_ge(C["m_up_mm"], t.upto(EXPERTS, e + 1))
            dve.scalar_tensor_tensor(hid[:, e % 2], th[:, e % 2], sel[:, t.slot, e:e + 1], ps_u[:].rearrange("p a n -> p (a n)"),
                                     ALU.mult, ALU.mult).then_inc(C["m_hid"], 1)
            if e == EXPERTS - 1:
                cm.close()

        def second(t, e):
            dve.wait_ge(C["m_hT_mm"], t.upto(2 * EXPERTS, 2 * e + 2))
            dve.tensor_copy(hT[:, 512:1024], ps_t[:, 1]).then_inc(C["m_hT_dve"], 1)
            if e == EXPERTS - 1:
                dve.wait_ge(C["m_down_mm"], t.upto(EXPERTS, EXPERTS))
                if not t.slot_first:
                    dve.wait_ge(stored[t.slot], 16 * t.n)
                dve.scalar_tensor_tensor(y[:, t.slot], ps_y[:, 0:D], 1.0, x5[:, t.slot], ALU.mult, ALU.add).then_inc(C["m_y"], 1)

        run(dve, norm, first, second)


def rope_tables(width, base=10000.0):
    inv = (np.float32(base) ** (-np.arange(0, width, 2, dtype=np.float32) / np.float32(width))).astype(np.float32)
    th = np.outer(np.arange(S, dtype=np.float32), inv).astype(np.float32)
    cos, sin = np.cos(th), np.sin(th)
    return (np.tile(np.concatenate([cos, cos], 1), (NB, 1)).astype(np.float32),
            np.tile(np.concatenate([-sin, sin], 1), (NB, 1)).astype(np.float32))


def lay_out(i):
    f = {n: np.asarray(v) for n, v in i.items()}

    def chunks(w):
        return w.reshape(-1, P, w.shape[-1]).transpose(1, 0, 2)

    def rep(v, n=P):
        return np.broadcast_to(v[None], (n, v.shape[0]))

    a = {}
    a["x"] = f["x"].reshape(TILES, P, D)
    a["ctx"] = f["ctx_2048"]
    a["mask"] = np.repeat(f["mask_BxS2_bk0"], S, axis=0).reshape(TILES, P, M)
    a["wkv0"] = chunks(np.concatenate([f["L0_attn_wk"], f["L0_attn_wv"]], 1))
    a["wq0"] = chunks(f["L0_attn_wq"].reshape(D, 4, 2, REP, HD0).transpose(0, 1, 3, 2, 4).reshape(D, -1))
    a["wo0"] = f["L0_attn_wo"].reshape(4, 2, REP, HD0, D).transpose(0, 2, 1, 3, 4).reshape(16, P, D).transpose(1, 0, 2)
    a["wgate0"] = chunks(f["L0_ffn_w_gate"].T)
    a["wup0"] = chunks(f["L0_ffn_w_up"].T)
    a["wdown0"] = chunks(f["L0_ffn_w_down"].T)
    a["wq1"] = chunks(f["L1_xattn_Wq"])
    a["wk1"] = chunks(f["L1_xattn_Wk_img"])
    a["wv1"] = chunks(f["L1_xattn_Wv_img"])
    a["wo1"] = f["L1_xattn_Wo"].reshape(4, REP, HD1, D).transpose(0, 2, 1, 3).reshape(64, REP, D)
    a["bv1"] = f["L1_xattn_bv_img"].reshape(4, REP, HD1).transpose(0, 2, 1).reshape(64, REP)
    a["bq1"], a["gq1"], a["bo1"] = (rep(f["L1_xattn_" + n]) for n in ("bq", "gq", "bo"))
    a["bk1"], a["gk1"] = (f["L1_xattn_" + n].reshape(KC, P).T for n in ("bk_img", "gk_img"))
    wq2 = f["L1_attn_Wq"].T.reshape(D, G2, REP, HD2).transpose(0, 2, 1, 3).reshape(D, D)
    bq2 = f["L1_attn_bq"].reshape(G2, REP, HD2).transpose(1, 0, 2).reshape(D)
    a["wqkv2"] = chunks(np.concatenate([wq2, f["L1_attn_Wk"].T, f["L1_attn_Wv"].T], 1))
    a["bqkv2"] = rep(np.concatenate([bq2, f["L1_attn_bk"], f["L1_attn_bv"]]))
    a["wo2"] = f["L1_attn_Wo"].T.reshape(G2, REP, HD2, D).transpose(0, 2, 1, 3).reshape(64, REP, D)
    a["bo2"] = rep(f["L1_attn_bo"])
    a["wr"] = chunks(f["L1_ffn_Wr"])
    a["br"] = rep(f["L1_ffn_br"])
    a["wg"], a["wu"], a["wd"] = (f["L1_ffn_" + n].reshape(EXPERTS, -1, P, m).transpose(2, 0, 1, 3)
                                 for n, m in (("Wg", F), ("Wu", F), ("Wd", D)))
    a["ident"] = np.eye(P, dtype=np.float32)
    a["cos0"], a["sin0"] = rope_tables(HD0)
    a["cos2"], a["sin2"] = rope_tables(HD2)
    q = np.arange(P)
    a["causal"] = np.where(np.arange(S)[None] <= (q % S)[:, None], 0.0, NEG).astype(np.float32)
    a["own_batch"] = (q[:, None] // S == np.arange(NB)[None]).astype(np.float32)
    a["head_rows"] = ((q[:, None] // HD1) % REP == np.arange(REP)[None]).astype(np.float32)
    a["group_rows"] = (np.arange(64)[:, None] // HD2 == np.arange(G2)[None]).astype(np.float32)
    a["rank"] = rep(np.arange(EXPERTS, 0, -1).astype(np.float32))
    return {n: np.ascontiguousarray(v) for n, v in a.items()}


def kernel(**inputs):
    import concourse.bacc as _bacc
    from concourse.bass_utils import run_bass_kernel_spmd as _run

    nc = _bacc.Bacc("TRN2", target_bir_lowering=False, num_devices=1)
    arrays = lay_out(inputs)
    a = {n: nc.dram_tensor("in_" + n, v.shape, mybir.dt.from_np(v.dtype), kind="ExternalInput").ap() for n, v in arrays.items()}
    out = nc.dram_tensor("out", [TOKENS, D], F32, kind="ExternalOutput").ap()
    build(nc, a, out)
    r = _run(nc, [{"in_" + n: v for n, v in arrays.items()}], core_ids=[0])
    return r.results[0]["out"].reshape(BATCHES, S, D)
```

```python
from contextlib import ExitStack

import numpy as np

import concourse.bass as bass
from concourse import mybir

F32 = mybir.dt.float32
U8 = mybir.dt.uint8
I32 = mybir.dt.int32
ALU = mybir.AluOpType
ACT = mybir.ActivationFunctionType
AX = mybir.AxisListType

P = 128
S = 32
NB = P // S
D = 256
KC = D // P
M = 257
MC = 2
BATCHES = 128
TILES = BATCHES // NB
TOKENS = BATCHES * S
F = 1024
FC = F // P
EXPERTS = 4
H0, G0, HD0 = 32, 8, 64
KV0 = G0 * HD0
H1, HD1 = 16, 16
G2, HD2 = 8, 8
REP = 4
NEG = -1e30
ROW = D + 1
SORTED_TILES = TILES + EXPERTS - 1
LOADS = 4
RSQRT_SEED = 0x5F3759DF
CHAIN_A, CHAIN_B, CHAIN_M = 59, 93, 15
B_STEPS = ["ba0", "ba1", "ba2"] + [s + str(b) for b in range(NB) for s in ("bb", "bc", "bd", "be", "bf")] + [
    f"bg{n}" for n in range(12)]
A_STEPS = [f"a{n:02d}" for n in range(1, 16)]
ORDER = [s for n, s_a in enumerate(A_STEPS) for s in [s_a] + B_STEPS[n * len(B_STEPS) // 15:(n + 1) * len(B_STEPS) // 15]]
ds = bass.ds


class Tile:

    def __init__(self, i, slot, n):
        self.i, self.slot, self.n = i, slot, n
        self.first = isinstance(i, int) and i == 0
        self.slot_first = isinstance(n, int) and n == 0

    def upto(self, per, k):
        return self.i * per + k


class Chain:

    def __init__(self, eng, sem, per):
        self.eng, self.sem, self.per, self.t, self.n = eng, sem, per, None, 0

    def open(self, t):
        self.t, self.n = t, 0

    def close(self):
        assert self.n == self.per, ("CHAIN", self.n, self.per)

    def done(self, ins):
        self.n += 1
        ins.then_inc(self.sem, 1)
        self.eng.wait_ge(self.sem, self.t.upto(self.per, self.n))


def inverse_root(dve, chain, v, y, w):
    chain.done(dve.tensor_scalar(y.bitcast(I32), v.bitcast(I32), 1, None, ALU.logical_shift_right))
    chain.done(dve.tensor_scalar(y.bitcast(I32), y.bitcast(I32), -1.0, float(RSQRT_SEED), ALU.mult, ALU.add))
    for _ in range(3):
        chain.done(dve.scalar_tensor_tensor(w, v, y, y, ALU.mult, ALU.mult))
        chain.done(dve.tensor_scalar(w, w, -0.5, 1.5, ALU.mult, ALU.add))
        chain.done(dve.tensor_tensor(y, y, w, ALU.mult))


def layer_norm(dve, chain, x, y, stats, mv):
    chain.done(dve.bn_stats(stats, x))
    dve.memset(mv[:, 3:4], 0.0)
    chain.done(dve.bn_aggr(mv[:, 0:2], stats))
    chain.done(dve.tensor_scalar(mv[:, 1:2], mv[:, 1:2], 1e-5, None, ALU.add))
    inverse_root(dve, chain, mv[:, 1:2], mv[:, 2:3], mv[:, 3:4])
    return dve.tensor_scalar(y, x, mv[:, 0:1], mv[:, 2:3], ALU.subtract, ALU.mult)


def build(nc, a, out):
    x5_dram = nc.dram_tensor("x5_scratch", [TOKENS, ROW], F32, kind="Internal").ap()
    sorted_dram = nc.dram_tensor("sorted_scratch", [SORTED_TILES * P, ROW], F32, kind="Internal").ap()
    y_dram = nc.dram_tensor("y_scratch", [SORTED_TILES * P, D], F32, kind="Internal").ap()
    with ExitStack() as both:
        ident = both.enter_context(nc.sbuf_tensor("ident", [P, P], F32))
        chosen = both.enter_context(nc.sbuf_tensor("chosen", [P, TILES, EXPERTS], F32))
        with ExitStack() as ctx:
            layers_0_to_attention_1(nc, ctx, a, ident, chosen, x5_dram, sorted_dram)
        with ExitStack() as ctx:
            mixture_of_experts(nc, ctx, a, ident, chosen, x5_dram, sorted_dram, y_dram, out)


def layers_0_to_attention_1(nc, ctx, a, ident, chosen, x5_dram, sorted_dram):
    def sb(name, shape, dt=F32):
        return ctx.enter_context(nc.sbuf_tensor(name, shape, dt))

    def sem(name):
        return ctx.enter_context(nc.semaphore(name))

    loads = []

    def const(name, shape, src=None, dt=F32):
        t = sb("c_" + name, shape, dt)
        loads.append((t, a[src or name]))
        return t

    loads.append((ident, a["ident"]))
    wkv0 = const("wkv0", [P, KC, 2 * KV0])
    wq0 = const("wq0", [P, KC, H0 * HD0])
    wo0 = const("wo0", [P, H0 * HD0 // P, D])
    wgate0 = const("wgate0", [P, KC, F])
    wup0 = const("wup0", [P, KC, F])
    wdown0 = const("wdown0", [P, FC, D])
    wq1 = const("wq1", [P, KC, D])
    wk1 = const("wk1", [P, KC, D])
    wv1 = const("wv1", [P, KC, D])
    wo1 = const("wo1", [64, REP, D])
    wqkv2 = const("wqkv2", [P, KC, 384])
    wo2 = const("wo2", [64, REP, D])
    cos0 = const("cos0", [P, HD0])
    sin0 = const("sin0", [P, HD0])
    cos2 = const("cos2", [P, HD2])
    sin2 = const("sin2", [P, HD2])
    causal = const("causal", [P, S])
    own_batch = const("own_batch", [P, NB])
    head_rows = const("head_rows", [P, REP])
    group_rows = const("group_rows", [64, G2])
    bq1 = const("bq1", [P, D])
    gq1 = const("gq1", [P, D])
    bk1 = const("bk1", [P, KC])
    gk1 = const("gk1", [P, KC])
    bv1 = const("bv1", [64, REP])
    bo1 = const("bo1", [P, D])
    bqkv2 = const("bqkv2", [P, 384])
    bo2 = const("bo2", [P, D])
    wr = const("wr", [P, KC, EXPERTS])
    br = const("br", [P, EXPERTS])
    rank = const("rank", [P, EXPERTS])

    x_in = sb("x_in", [P, 2, D])
    rows = sb("ctx_rows", [P, 2, NB, MC, D])
    last_row = sb("ctx_last_row", [NB, 2, D])
    mask_u8 = sb("mask_u8", [P, 2, M], U8)
    ctxT = sb("ctxT", [P, 2, KC, NB, M])
    xn = sb("xn", [P, D])
    xnT_sb = sb("xnT_sb", [P, KC, P])
    stats = sb("stats", [P, 6])
    mv = sb("mv", [P, 4])
    maskadd = sb("maskadd", [P, M])
    sc0 = sb("sc0", [P, M])
    p0 = sb("p0", [P, M])
    small = sb("small", [P, 8])
    p0_last = sb("p0_last", [P, NB])
    p0T = sb("p0T", [P, MC, P])
    p0T_last = sb("p0T_last", [NB, P])
    x1 = sb("x1", [P, D])
    v0 = sb("v0", [P, KV0])
    qT = sb("qT", [P, 4, NB, REP, S])
    kT = sb("kT", [P, 4, P])
    att = sb("att", [P, 2 * 512])
    rope_c, rope_s = att[:, 0:512], att[:, 512:1024]
    att_max = sb("att_max", [P, 32])
    att_sum = sb("att_sum", [P, 32])
    attT = sb("attT", [P, 2, 512])
    rot = attT
    oT = sb("oT", [P, 4, REP, NB, S])
    x2 = sb("x2", [P, D])
    th = qT[:].rearrange("p c b j q -> p (c b j q)")[:, 0:F]
    hid = qT[:].rearrange("p c b j q -> p (c b j q)")[:, F:2 * F]
    hT = oT[:].rearrange("p c j b q -> p (c j b q)")[:, 0:F]
    x3 = sb("x3", [P, 2, D])

    yn = sb("yn", [P, D])
    ynT = sb("ynT", [P, KC, P])
    stats_b = sb("stats_b", [P, 6])
    mv_b = sb("mv_b", [P, 4])
    ones = sb("ones", [P, P])
    gk_rows = sb("gk_rows", [P, KC, REP])
    q1 = sb("q1", [P, D])
    q1sq = sb("q1sq", [P, D])
    q1ss = sb("q1ss", [P, 3])
    qbd = sb("qbd", [P, KC, NB, REP, S])
    ksq = sb("ksq", [P, KC, M])
    krs = sb("krs", [P, M])
    kms = sb("kms", [P, M])
    k1n = sb("k1n", [P, KC, M])
    v1 = sb("v1", [P, MC, D])
    v1_last = sb("v1_last", [NB, D])
    p1 = sb("p1", [P, REP, M])
    p1max = sb("p1max", [P, REP])
    p1sum = sb("p1sum", [P, REP])
    p1rec = sb("p1rec", [P, REP])
    p1_last = sb("p1_last", [P, NB, REP, NB])
    p1T = sb("p1T", [P, 1024])
    p1T_last = sb("p1T_last", [NB, 512])
    o1 = sb("o1", [P, NB, REP, HD1])
    o1T = sb("o1T", [64, REP, NB, S])
    x3b = sb("x3b", [P, D])
    x4 = sb("x4", [P, D])
    x4b = sb("x4b", [P, D])
    qkv = sb("qkv", [P, 384])
    rc2 = sb("rc2", [P, 320])
    rs2 = sb("rs2", [P, 320])
    q2T = v1[0:64].rearrange("p c d -> p (c d)").rearrange("p (b j q) -> p b j q", b=NB, j=REP)
    k2bd = p1[0:64].rearrange("p j m -> p (j m)")[:, 0:NB * G2 * S].rearrange("p (b g k) -> p b g k", b=NB, g=G2)
    v2bd = ksq[:].rearrange("p c m -> p (c m)")[:, 0:D].rearrange("p (g b d) -> p g b d", g=G2, b=NB)
    att2 = qbd[:].rearrange("p c b h q -> p (c b h q)")
    att2_max = sb("att2_max", [P, 32])
    att2_sum = sb("att2_sum", [P, 32])
    att2T = p1T
    o2 = o1[:].rearrange("p b j d -> p (b j d)").rearrange("p (b g d) -> p b g d", b=NB, g=G2)
    o2T = o1T
    x5 = sb("x5", [P, 2, ROW])
    lg = sb("lg", [P, EXPERTS])
    pr = sb("pr", [P, EXPERTS])
    rt = sb("router", [P, 6])
    zero_row = sb("zero_row", [P, ROW])

    psA = ctx.enter_context(nc.psum_tensor("psA", [P, 4, 512], F32))
    psB = ctx.enter_context(nc.psum_tensor("psB", [P, 4, 512], F32))

    def sems(*names):
        return {n: sem(n) for n in names}

    const_in = sem("const_in")
    loaded = [sem("tile_loaded_slot0"), sem("tile_loaded_slot1")]
    stored = [sem("x5_stored_slot0"), sem("x5_stored_slot1")]
    dve_a, dve_b = sem("dve_own_results_a"), sem("dve_own_results_b")
    setup_done = sem("setup_done")
    setup_chain = sem("setup_chain")
    A = sems("xn", "xnT_mm", "xnT", "ctxT_mm", "ctxT_act", "ctxT_dve", "scores_mm", "scores", "probs", "probs_last",
             "probsT_mm", "probsT", "read_mm", "qkv_mm", "v", "rot", "rotT_mm", "rotT", "att_mm", "att_centred",
             "att_exp", "att", "attT_mm", "attT_act", "attT_dve", "pv_mm", "oT_act", "oT_dve", "wo_mm", "gate_mm",
             "up_mm", "tanh", "hid", "hT_mm", "hT_act", "hT_dve", "down_mm", "x3")
    B = sems("b_yn", "b_ynT_mm", "b_ynT", "b_q_mm", "b_q", "b_qT_mm", "b_qbd", "b_vlast_mm", "b_vlast",
             "b_k_mm", "b_v_mm", "b_ksq", "b_kss_mm", "b_kms", "b_kln", "b_krs", "b_kn", "b_v", "b_scores_mm", "b_max", "b_probs", "b_probs_last",
             "b_probsT_mm", "b_probsT_act", "b_probsT_dve", "b_pv_mm", "b_o", "b_oT_mm", "b_oT", "b_wo_mm",
             "b_qkv2_mm", "b_rot2", "b_rot2T_mm", "b_q2T", "b_k2bd", "b_att2_mm", "b_centred2", "b_exp2", "b_sum2",
             "b_att2T_mm", "b_att2T_act", "b_att2T_dve", "b_pv2_mm", "b_o2", "b_o2T_mm", "b_o2T", "b_wo2_mm", "b_logits_mm", "b_logits", "b_pexp", "b_x5")
    zeroed = sem("sorted_rows_zeroed")

    def run(eng, stage_a, stage_b):
        weave(stage_a, Tile(0, 0, 0), None, None)
        weave(stage_a, Tile(1, 1, 0), stage_b, Tile(0, 0, 0))
        weave(stage_a, Tile(2, 0, 1), stage_b, Tile(1, 1, 0))
        with eng.Fori(1, TILES // 2 - 1) as k:
            weave(stage_a, Tile(2 * k + 1, 1, k), stage_b, Tile(2 * k, 0, k))
            weave(stage_a, Tile(2 * k + 2, 0, k + 1), stage_b, Tile(2 * k + 1, 1, k))
        weave(stage_a, Tile(TILES - 1, 1, TILES // 2 - 1), stage_b, Tile(TILES - 2, 0, TILES // 2 - 1))
        weave(None, None, stage_b, Tile(TILES - 1, 1, TILES // 2 - 1))

    def weave(stage_a, ta, stage_b, tb):
        for name in ORDER:
            if name[0] == "a" and ta is not None and name in stage_a:
                stage_a[name](ta)
            if name[0] == "b" and tb is not None and name[:2] in stage_b:
                stage_b[name[:2]](tb, int(name[2:]))

    block = ctx.enter_context(nc.Block())

    @block.sync
    def _(sp):
        for dst, src in loads:
            sp.dma_start(dst[:], src).then_inc(const_in, 16)

        def load(t):
            if not t.slot_first:
                sp.wait_ge(A["xn"], t.upto(3, 2 - 6))
            done = loaded[t.slot]
            sp.dma_start(x_in[:, t.slot], a["x"][ds(t.i, 1)].rearrange("t p d -> (t p) d")).then_inc(done, 16)
            sp.dma_start(rows[:, t.slot].rearrange("p b c d -> p b (c d)"),
                         a["ctx"][ds(t.i * NB, NB), 0:MC * P].rearrange("b (p c) d -> p b (c d)", c=MC)).then_inc(done, 16)
            sp.dma_start(last_row[:, t.slot], a["ctx"][ds(t.i * NB, NB), M - 1]).then_inc(done, 16)
            sp.dma_start(mask_u8[:, t.slot], a["mask"][ds(t.i, 1)].rearrange("t p m -> (t p) m")).then_inc(done, 16)

        load(Tile(0, 0, 0))
        load(Tile(1, 1, 0))
        with sp.Fori(1, TILES // 2) as k:
            load(Tile(2 * k, 0, k))
            load(Tile(2 * k + 1, 1, k))

    @block.gpsimd
    def _(pool):
        def store(t):
            pool.wait_ge(B["b_x5"], t.upto(1, 1))
            pool.dma_start(x5_dram[ds(t.i * P, P)], x5[:, t.slot]).then_inc(stored[t.slot], 16)

        pool.wait_ge(setup_done, 1)
        pool.dma_start(sorted_dram.rearrange("(t p) d -> p t d", p=P),
                       zero_row[:].unsqueeze(1).broadcast_to([P, SORTED_TILES, ROW])).then_inc(zeroed, 16)
        with pool.Fori(0, TILES // 2) as k:
            store(Tile(2 * k, 0, k))
            store(Tile(2 * k + 1, 1, k))
        for s in stored:
            pool.wait_ge(s, 16 * (TILES // 2))
        pool.wait_ge(zeroed, 16)

    def wait_loaded(eng, t):
        eng.wait_ge(loaded[t.slot], t.n * 16 * LOADS + 16 * LOADS)

    @block.tensor
    def _(pe):
        pe.wait_ge(const_in, 16 * len(loads))
        pe.wait_ge(setup_done, 1)

        def transpose(out, in_):
            return pe.transpose(out, in_, ident[0:in_.shape[0], 0:in_.shape[0]])

        def xnT(t, k, bank):
            pe.wait_ge(A["xn"], t.upto(3, k))
            for c in range(KC):
                mm = transpose(psA[:, bank, c * P:(c + 1) * P], xn[:, c * P:(c + 1) * P])
            return mm

        def a01(t):
            wait_loaded(pe, t)
            if not t.first:
                pe.wait_ge(A["x3"], t.upto(1, 0))
            xnT(t, 1, 0)
            for c in range(KC):
                mm = transpose(psA[:, 0, 2 * P + c * NB:2 * P + (c + 1) * NB], last_row[:, t.slot, c * P:(c + 1) * P])
            mm.then_inc(A["xnT_mm"], 1)
            for b in range(NB):
                if b == NB - 1:
                    pe.wait_ge(A["xnT"], t.upto(3, 1))
                for kc in range(KC):
                    for c in range(MC):
                        at = (kc * MC + c) * P
                        mm = transpose(psA[:, (b + 1) % 4, at:at + P], rows[:, t.slot, b, c, kc * P:(kc + 1) * P])
                mm.then_inc(A["ctxT_mm"], 1)

        def a02(t):
            pe.wait_ge(A["xnT"], t.upto(3, 1))
            pe.wait_ge(A["ctxT_act"], t.upto(2, 2))
            pe.wait_ge(A["ctxT_dve"], t.upto(2, 2))
            for b in range(NB):
                for kc in range(KC):
                    mm = pe.matmul(psA[S * b:S * b + S, 1, 0:M], xnT_sb[:, kc, S * b:S * b + S],
                                   ctxT[:, t.slot, kc, b], start=(kc == 0), stop=(kc == KC - 1), tile_position=(0, S * b))
            mm.then_inc(A["scores_mm"], 1)

        def a03(t):
            pe.wait_ge(A["probs"], t.upto(1, 1))
            for c in range(MC):
                transpose(psA[:, 2, c * P:(c + 1) * P], p0[:, c * P:(c + 1) * P])
            pe.wait_ge(A["probs_last"], t.upto(1, 1))
            transpose(psA[0:NB, 2, 2 * P:3 * P], p0_last[:]).then_inc(A["probsT_mm"], 1)

        def a04(t):
            pe.wait_ge(A["probsT"], t.upto(1, 1))
            pe.matmul(psA[:, 3, 0:D], p0T_last[:], last_row[:, t.slot], start=True, stop=False, skip_group_check=True)
            for b in range(NB):
                for c in range(MC):
                    mm = pe.matmul(psA[S * b:S * b + S, 3, 0:D], p0T[:, c, S * b:S * b + S], rows[:, t.slot, b, c],
                                   start=False, stop=(c == MC - 1), tile_position=(0, S * b), skip_group_check=True)
            mm.then_inc(A["read_mm"], 1)

        def a05(t):
            xnT(t, 2, 0).then_inc(A["xnT_mm"], 1)

        def project(bank, w, lo, n):
            for kc in range(KC):
                mm = pe.matmul(psA[:, bank, 0:n], xnT_sb[:, kc], w[:, kc, lo:lo + n], start=(kc == 0), stop=(kc == KC - 1))
            return mm

        def a06(t):
            pe.wait_ge(A["xnT"], t.upto(3, 2))
            project(2, wkv0, 0, KV0).then_inc(A["qkv_mm"], 1)
            project(3, wkv0, KV0, KV0).then_inc(A["qkv_mm"], 1)
            project(0, wq0, 0, 512).then_inc(A["qkv_mm"], 1)
            project(1, wq0, 512, 512).then_inc(A["qkv_mm"], 1)

        def rotT(t, n, bank):
            pe.wait_ge(A["rot"], t.upto(5, n + 1))
            for c in range(4):
                mm = transpose(psA[:, bank, c * P:(c + 1) * P], rot[:, n % 2, c * P:(c + 1) * P])
            mm.then_inc(A["rotT_mm"], 1)

        def a07(t):
            rotT(t, 0, 2)
            pe.wait_ge(A["v"], t.upto(1, 1))
            rotT(t, 1, 3)
            project(0, wq0, 1024, 512).then_inc(A["qkv_mm"], 1)
            pe.wait_ge(A["rotT"], t.upto(5, 1))
            rotT(t, 2, 2)
            project(1, wq0, 1536, 512).then_inc(A["qkv_mm"], 1)
            pe.wait_ge(A["rotT"], t.upto(5, 2))
            rotT(t, 3, 3)
            pe.wait_ge(A["rotT"], t.upto(5, 3))
            rotT(t, 4, 2)

        def a08(t):
            pe.wait_ge(A["rotT"], t.upto(5, 5))
            for c in range(4):
                for b in range(NB):
                    for s in range(2):
                        mm = pe.matmul(psA[:, s, (c * NB + b) * S:(c * NB + b + 1) * S],
                                       qT[64 * s:64 * s + 64, c, b].rearrange("p j q -> p (j q)"),
                                       kT[64 * s:64 * s + 64, c, S * b:S * b + S], start=True, stop=True,
                                       tile_position=(64 * s, 0))
            mm.then_inc(A["att_mm"], 1)

        def a09(t):
            pe.wait_ge(A["att"], t.upto(1, 1))
            for s in range(2):
                for c in range(4):
                    at = s * 512 + c * P
                    mm = transpose(psA[:, 2 + s, c * P:(c + 1) * P], att[:, at:at + P])
                mm.then_inc(A["attT_mm"], 1)

        def a10(t):
            pe.wait_ge(A["attT_act"], t.upto(1, 1))
            pe.wait_ge(A["attT_dve"], t.upto(1, 1))
            for b in range(NB):
                for c in range(4):
                    for s in range(2):
                        g = 2 * c + s
                        mm = pe.matmul(psA[64 * s:64 * s + 64, b, c * P:(c + 1) * P], v0[S * b:S * b + S, g * HD0:(g + 1) * HD0],
                                       attT[S * b:S * b + S, s, c * P:(c + 1) * P], start=True, stop=True,
                                       tile_position=(S * b, 64 * s))
                mm.then_inc(A["pv_mm"], 1)

        def a11(t):
            pe.wait_ge(A["oT_act"], t.upto(2, 2))
            pe.wait_ge(A["oT_dve"], t.upto(2, 2))
            for c in range(16):
                mm = pe.matmul(psA[:, 0, 0:D], oT[:, c // 4, c % 4].rearrange("p b q -> p (b q)"), wo0[:, c],
                               start=(c == 0), stop=(c == 15))
            mm.then_inc(A["wo_mm"], 1)

        def a12(t):
            xnT(t, 3, 1).then_inc(A["xnT_mm"], 1)

        def a13(t):
            pe.wait_ge(A["xnT"], t.upto(3, 3))
            project(2, wgate0, 0, 512)
            project(3, wgate0, 512, 512).then_inc(A["gate_mm"], 1)
            project(0, wup0, 0, 512)
            project(1, wup0, 512, 512).then_inc(A["up_mm"], 1)

        def a14(t):
            pe.wait_ge(A["hid"], t.upto(1, 1))
            for h in range(2):
                for c in range(4):
                    at = h * 512 + c * P
                    mm = transpose(psA[:, 2 + h, c * P:(c + 1) * P], hid[:, at:at + P])
                mm.then_inc(A["hT_mm"], 1)

        def a15(t):
            pe.wait_ge(A["hT_act"], t.upto(1, 1))
            pe.wait_ge(A["hT_dve"], t.upto(1, 1))
            for c in range(FC):
                mm = pe.matmul(psA[:, 0, 0:D], hT[:, c * P:(c + 1) * P], wdown0[:, c], start=(c == 0), stop=(c == FC - 1))
            mm.then_inc(A["down_mm"], 1)

        def ynT_step(t, k, bank):
            pe.wait_ge(B["b_yn"], t.upto(3, k))
            for c in range(KC):
                mm = transpose(psB[:, bank, c * P:(c + 1) * P], yn[:, c * P:(c + 1) * P])
            mm.then_inc(B["b_ynT_mm"], 1)

        def ba(t, n):
            if n == 0:
                if not t.first:
                    pe.wait_ge(B["b_x5"], t.upto(1, 0))
                ynT_step(t, 1, 0)
            if n == 1:
                pe.wait_ge(B["b_ynT"], t.upto(3, 1))
                for kc in range(KC):
                    mm = pe.matmul(psB[:, 1, 0:D], ynT[:, kc], wq1[:, kc], start=(kc == 0), stop=(kc == KC - 1))
                mm.then_inc(B["b_q_mm"], 1)
                for kc in range(KC):
                    mm = pe.matmul(psB[0:NB, 3, 0:D], ctxT[:, t.slot, kc, :, M - 1], wv1[:, kc], start=(kc == 0),
                                   stop=(kc == KC - 1))
                mm.then_inc(B["b_vlast_mm"], 1)
            if n == 2:
                pe.wait_ge(B["b_q"], t.upto(1, 1))
                for c in range(KC):
                    mm = transpose(psB[:, 2, c * P:(c + 1) * P], q1[:, c * P:(c + 1) * P])
                mm.then_inc(B["b_qT_mm"], 1)

        def bb(t, b):
            if b == 0:
                pe.wait_ge(B["b_q"], t.upto(1, 1))
                pe.wait_ge(B["b_vlast"], t.upto(1, 1))
                pe.wait_ge(B["b_qbd"], t.upto(1, 1))
            else:
                pe.wait_ge(B["b_o"], t.upto(NB, b))
            for m in range(KC):
                for kc in range(KC):
                    mm = pe.matmul(psB[:, m, 0:M], wk1[:, kc, m * P:(m + 1) * P], ctxT[:, t.slot, kc, b],
                                   start=(kc == 0), stop=(kc == KC - 1))
            mm.then_inc(B["b_k_mm"], 1)
            for c in range(MC):
                for kc in range(KC):
                    mm = pe.matmul(psB[:, 2, c * D:(c + 1) * D], ctxT[:, t.slot, kc, b, c * P:(c + 1) * P], wv1[:, kc],
                                   start=(kc == 0), stop=(kc == KC - 1))
            mm.then_inc(B["b_v_mm"], 1)

        def bc(t, b):
            pe.wait_ge(B["b_ksq"], t.upto(NB, b + 1))
            for m in range(KC):
                mm = pe.matmul(psB[:, 3, 0:M], ones[:], ksq[:, m], start=(m == 0), stop=(m == KC - 1))
            mm.then_inc(B["b_kss_mm"], 1)

        def bd(t, b):
            pe.wait_ge(B["b_kn"], t.upto(NB, b + 1))
            pe.wait_ge(B["b_v"], t.upto(NB, b + 1))
            for j in range(REP):
                r = 64 * (j % 2)
                mm = pe.matmul(psB[:, j, 0:M], qbd[r:r + 64, j // 2, b].rearrange("p h q -> p (h q)"),
                               k1n[r:r + 64, j // 2], start=True, stop=True, tile_position=(r, 0))
            mm.then_inc(B["b_scores_mm"], 1)

        def be(t, b):
            pe.wait_ge(B["b_probs"], t.upto(NB, b + 1))
            for j in range(REP):
                for c in range(MC):
                    mm = transpose(psB[:, j // 2, ((j % 2) * MC + c) * P:((j % 2) * MC + c + 1) * P],
                                   p1[:, j, c * P:(c + 1) * P])
                if j % 2 == 1:
                    mm.then_inc(B["b_probsT_mm"], 1)
            pe.wait_ge(B["b_probs_last"], t.upto(NB, b + 1))
            for j in range(REP):
                mm = transpose(psB[0:NB, 2, j * P:(j + 1) * P], p1_last[:, b, j])
            mm.then_inc(B["b_probsT_mm"], 1)

        def bf(t, b):
            pe.wait_ge(B["b_probsT_act"], t.upto(2 * NB, 2 * b + 2))
            pe.wait_ge(B["b_probsT_dve"], t.upto(NB, b + 1))
            for j in range(REP):
                for c in range(MC):
                    at = (j * MC + c) * P
                    pe.matmul(psB[:, 3, j * 64:(j + 1) * 64], p1T[:, at:at + P], v1[:, c, j * 64:(j + 1) * 64],
                              start=(c == 0), stop=False)
                mm = pe.matmul(psB[:, 3, j * 64:(j + 1) * 64], p1T_last[:, j * P:(j + 1) * P],
                               v1_last[:, j * 64:(j + 1) * 64], start=False, stop=True)
            mm.then_inc(B["b_pv_mm"], 1)

        def out_T(src, bank):
            for b in range(NB):
                mm = transpose(psB[0:64, bank, b * P:(b + 1) * P], src[:, b].rearrange("p h d -> p (h d)"))
            return mm

        def out_w(srcT, w, bank):
            for h in range(REP):
                mm = pe.matmul(psB[:, bank, 0:D], srcT[:, h].rearrange("p b q -> p (b q)"), w[:, h], start=(h == 0),
                               stop=(h == REP - 1))
            return mm

        def bg(t, n):
            if n == 0:
                pe.wait_ge(setup_done, 1)
                pe.wait_ge(B["b_o"], t.upto(NB, NB))
                out_T(o1, 0).then_inc(B["b_oT_mm"], 1)
            if n == 1:
                pe.wait_ge(B["b_oT"], t.upto(1, 1))
                out_w(o1T, wo1, 1).then_inc(B["b_wo_mm"], 1)
            if n == 2:
                ynT_step(t, 2, 2)
            if n == 3:
                pe.wait_ge(B["b_ynT"], t.upto(3, 2))
                for kc in range(KC):
                    mm = pe.matmul(psB[:, 3, 0:384], ynT[:, kc], wqkv2[:, kc], start=(kc == 0), stop=(kc == KC - 1))
                mm.then_inc(B["b_qkv2_mm"], 1)
            if n == 4:
                pe.wait_ge(setup_done, 1)
                pe.wait_ge(B["b_rot2"], t.upto(1, 1))
                for j in range(REP):
                    transpose(psB[0:64, 0, j * P:(j + 1) * P], rc2[:, j * 64:(j + 1) * 64])
                transpose(psB[0:64, 1, 0:P], rc2[:, 256:320]).then_inc(B["b_rot2T_mm"], 1)
            if n == 5:
                pe.wait_ge(B["b_q2T"], t.upto(1, 1))
                pe.wait_ge(B["b_k2bd"], t.upto(1, 1))
                for b in range(NB):
                    for h in range(2):
                        o = psB[:, 2 + h].rearrange("p (g b k) -> p g b k", g=4, b=NB)[:, :, b]
                        mm = pe.matmul(o, q2T[:, b].rearrange("p j q -> p (j q)"), k2bd[:, b, 4 * h:4 * h + 4],
                                       start=True, stop=True)
                mm.then_inc(B["b_att2_mm"], 1)
            if n == 6:
                pe.wait_ge(B["b_exp2"], t.upto(1, 1))
                for h in range(2):
                    for g in range(4):
                        at = (4 * h + g) * P
                        mm = transpose(psB[:, h, g * P:(g + 1) * P], att2[:, at:at + P])
                    mm.then_inc(B["b_att2T_mm"], 1)
            if n == 7:
                pe.wait_ge(B["b_att2T_act"], t.upto(1, 1))
                pe.wait_ge(B["b_att2T_dve"], t.upto(1, 1))
                for g in range(G2):
                    mm = pe.matmul(psB[:, 2, g * 32:(g + 1) * 32], att2T[:, g * P:(g + 1) * P],
                                   v2bd[:, g].rearrange("p b d -> p (b d)"), start=True, stop=True)
                mm.then_inc(B["b_pv2_mm"], 1)
            if n == 8:
                pe.wait_ge(setup_done, 1)
                pe.wait_ge(B["b_o2"], t.upto(1, 1))
                out_T(o2, 3).then_inc(B["b_o2T_mm"], 1)
            if n == 9:
                pe.wait_ge(B["b_o2T"], t.upto(1, 1))
                out_w(o2T, wo2, 0).then_inc(B["b_wo2_mm"], 1)
            if n == 10:
                ynT_step(t, 3, 1)
            if n == 11:
                pe.wait_ge(B["b_ynT"], t.upto(3, 3))
                for kc in range(KC):
                    mm = pe.matmul(psB[:, 2, 0:EXPERTS], ynT[:, kc], wr[:, kc], start=(kc == 0), stop=(kc == KC - 1))
                mm.then_inc(B["b_logits_mm"], 1)

        run(pe, dict(a01=a01, a02=a02, a03=a03, a04=a04, a05=a05, a06=a06, a07=a07, a08=a08, a09=a09, a10=a10, a11=a11,
                     a12=a12, a13=a13, a14=a14, a15=a15), dict(ba=ba, bb=bb, bc=bc, bd=bd, be=be, bf=bf, bg=bg))

    @block.scalar
    def _(act):
        act.wait_ge(const_in, 16 * len(loads))
        nc.scalar.preload_act_table_set("natural_log_exp_and_others")

        def xnT_copy(t, k, bank):
            act.wait_ge(A["xnT_mm"], t.upto(3, k))
            return act.copy(xnT_sb[:].rearrange("p c q -> p (c q)"), psA[:, bank, 0:D])

        def a01(t):
            ins = xnT_copy(t, 1, 0)
            act.copy(ctxT[:, t.slot, :, :, M - 1], psA[:, 0, D:D + KC * NB].rearrange("p (c b) -> p c b", c=KC)
                     ).then_inc(A["xnT"], 1)
            for b in (0, 2):
                act.wait_ge(A["ctxT_mm"], t.upto(NB, b + 1))
                act.copy(ctxT[:, t.slot, :, b, 0:MC * P], psA[:, b + 1, :].rearrange("p (k m) -> p k m", k=KC)
                         ).then_inc(A["ctxT_act"], 1)

        def a02(t):
            act.wait_ge(A["scores"], t.upto(1, 1))
            act.activation(p0[:], sc0[:], ACT.Exp, bias=small[:, 1:2], accum_out=small[:, 2:3]).then_inc(A["probs"], 1)

        def a03(t):
            act.wait_ge(A["probsT_mm"], t.upto(1, 1))
            act.copy(p0T[:].rearrange("p c q -> p (c q)"), psA[:, 2, 0:MC * P])
            act.copy(p0T_last[:], psA[0:NB, 2, MC * P:(MC + 1) * P]).then_inc(A["probsT"], 1)

        def a05(t):
            xnT_copy(t, 2, 0).then_inc(A["xnT"], 1)

        def a06(t):
            act.wait_ge(A["qkv_mm"], t.upto(6, 2))
            act.copy(v0[:], psA[:, 3, :]).then_inc(A["v"], 1)

        def a07(t):
            act.wait_ge(A["rotT_mm"], t.upto(5, 1))
            act.copy(kT[:].rearrange("p c q -> p (c q)"), psA[:, 2, :]).then_inc(A["rotT"], 1)
            for c in range(4):
                act.wait_ge(A["rotT_mm"], t.upto(5, c + 2))
                act.copy(qT[:, c].rearrange("p b j q -> p j b q"),
                         psA[:, 3 - c % 2, :].rearrange("p (j b q) -> p j b q", j=REP, b=NB)).then_inc(A["rotT"], 1)

        def a08(t):
            act.wait_ge(A["att_centred"], t.upto(1, 1))
            act.activation(att[:], att[:], ACT.Exp).then_inc(A["att_exp"], 1)

        def a09(t):
            act.wait_ge(A["attT_mm"], t.upto(2, 1))
            act.copy(attT[:, 0], psA[:, 2, :]).then_inc(A["attT_act"], 1)

        def a10(t):
            for b in (0, 2):
                act.wait_ge(A["pv_mm"], t.upto(NB, b + 1))
                act.copy(oT[:, :, :, b], psA[:, b, :].rearrange("p (c j q) -> p c j q", c=4, j=REP)).then_inc(A["oT_act"], 1)

        def a12(t):
            xnT_copy(t, 3, 1).then_inc(A["xnT"], 1)

        def a13(t):
            nc.scalar.preload_act_table_set("exp_and_others")
            act.wait_ge(A["gate_mm"], t.upto(1, 1))
            act.activation(th, psA[:, 2:4, :].rearrange("p a n -> p (a n)"), ACT.Tanh, scale=0.5).then_inc(A["tanh"], 1)

        def a14(t):
            act.wait_ge(A["hT_mm"], t.upto(2, 1))
            act.copy(hT[:, 0:512], psA[:, 2, :]).then_inc(A["hT_act"], 1)

        def ynT_copy(t, k, bank):
            act.wait_ge(B["b_ynT_mm"], t.upto(3, k))
            act.copy(ynT[:].rearrange("p c q -> p (c q)"), psB[:, bank, 0:D]).then_inc(B["b_ynT"], 1)

        def ba(t, n):
            if n == 0:
                ynT_copy(t, 1, 0)
            if n == 1:
                act.wait_ge(B["b_vlast_mm"], t.upto(1, 1))
                act.copy(v1_last[:], psB[0:NB, 3, 0:D]).then_inc(B["b_vlast"], 1)

        def bb(t, b):
            act.wait_ge(B["b_k_mm"], t.upto(NB, b + 1))
            for m in range(KC):
                ins = act.activation(ksq[:, m], psB[:, m, 0:M], ACT.Square, bias=bk1[:, m:m + 1])
            ins.then_inc(B["b_ksq"], 1)
            act.wait_ge(B["b_v_mm"], t.upto(NB, b + 1))
            act.copy(v1[:].rearrange("p c d -> p (c d)"), psB[:, 2, :]).then_inc(B["b_v"], 1)

        def bc(t, b):
            if b == 0:
                nc.scalar.preload_act_table_set("natural_log_exp_and_others")
            act.wait_ge(B["b_kms"], t.upto(NB, b + 1))
            act.activation(krs[:], kms[:], ACT.Ln).then_inc(B["b_kln"], 1)
            act.wait_ge(B["b_kln"], t.upto(NB, b + 1))
            act.activation(krs[:], krs[:], ACT.Exp, scale=-0.5).then_inc(B["b_krs"], 1)

        def bd(t, b):
            act.wait_ge(B["b_max"], t.upto(NB, b + 1))
            for j in range(REP):
                ins = act.activation(p1[:, j], psB[:, j, 0:M], ACT.Exp, bias=p1max[:, j:j + 1], scale=HD1 ** -0.5,
                                     accum_out=p1sum[:, j:j + 1])
            ins.then_inc(B["b_probs"], 1)

        def be(t, b):
            act.wait_ge(B["b_probsT_mm"], t.upto(3 * NB, 3 * b + 1))
            act.copy(p1T[:, 0:512], psB[:, 0, :]).then_inc(B["b_probsT_act"], 1)
            act.wait_ge(B["b_probsT_mm"], t.upto(3 * NB, 3 * b + 3))
            act.copy(p1T_last[:], psB[0:NB, 2, :]).then_inc(B["b_probsT_act"], 1)

        def bg(t, n):
            if n == 0:
                act.wait_ge(B["b_oT_mm"], t.upto(1, 1))
                for h in range(REP):
                    ins = act.activation(o1T[:, h], psB[0:64, 0, :].rearrange("p (b h q) -> p b h q", b=NB, h=REP)[:, :, h],
                                         ACT.Identity, bias=bv1[:, h:h + 1])
                ins.then_inc(B["b_oT"], 1)
            if n == 2:
                ynT_copy(t, 2, 2)
            if n == 4:
                act.wait_ge(B["b_rot2T_mm"], t.upto(1, 1))
                act.copy(q2T.rearrange("p b j q -> p j b q"),
                         psB[0:64, 0, :].rearrange("p (j b q) -> p j b q", j=REP, b=NB)).then_inc(B["b_q2T"], 1)
            if n == 5:
                act.wait_ge(B["b_centred2"], t.upto(1, 1))
                act.activation(att2, att2, ACT.Exp, scale=float(1 / np.sqrt(np.float32(HD2)))).then_inc(B["b_exp2"], 1)
            if n == 6:
                act.wait_ge(B["b_att2T_mm"], t.upto(2, 1))
                act.copy(att2T[:, 0:512], psB[:, 0, :]).then_inc(B["b_att2T_act"], 1)
            if n == 8:
                act.wait_ge(B["b_o2T_mm"], t.upto(1, 1))
                act.copy(o2T[:].rearrange("p j b q -> p b j q"),
                         psB[0:64, 3, :].rearrange("p (b j q) -> p b j q", b=NB, j=REP)).then_inc(B["b_o2T"], 1)

            if n == 10:
                ynT_copy(t, 3, 1)
            if n == 11:
                act.wait_ge(B["b_logits"], t.upto(1, 1))
                act.activation(pr[:], lg[:], ACT.Exp, bias=rt[:, 1:2], accum_out=rt[:, 2:3]).then_inc(B["b_pexp"], 1)

        run(act, dict(a01=a01, a02=a02, a03=a03, a05=a05, a06=a06, a07=a07, a08=a08, a09=a09, a10=a10, a12=a12, a13=a13,
                      a14=a14), dict(ba=ba, bb=bb, bc=bc, bd=bd, be=be, bg=bg))

    @block.vector
    def _(dve):
        dve.wait_ge(const_in, 16 * len(loads))
        dve.memset(ones[:], 1.0)
        dve.memset(zero_row[:], 0.0)
        dve.memset(p1_last[:], 0.0).then_inc(setup_chain, 1)
        for c in range(KC):
            ins = dve.tensor_scalar(gk_rows[:, c], head_rows[:], gk1[:, c:c + 1], None, ALU.mult)
        ins.then_inc(setup_chain, 1)
        dve.wait_ge(setup_chain, 2)
        dve.memset(small[:, 7:8], 0.0).then_inc(setup_done, 1)
        ca = Chain(dve, dve_a, CHAIN_A)
        cb = Chain(dve, dve_b, CHAIN_B)

        def norm(chain, x, y, stats, mv):
            return layer_norm(dve, chain, x, y[:], stats[:], mv)

        def a01(t):
            ca.open(t)
            wait_loaded(dve, t)
            norm(ca, x_in[:, t.slot], xn, stats, mv).then_inc(A["xn"], 1)
            m8 = mask_u8[:, t.slot]
            dve.tensor_scalar(maskadd[:, 0:MC * P].rearrange("p (c r) -> p c r", c=MC),
                              m8[:, 0:MC * P].rearrange("p (r c) -> p c r", c=MC), 1.0, -NEG, ALU.subtract, ALU.mult)
            dve.tensor_scalar(maskadd[:, M - 1:M], m8[:, M - 1:M], 1.0, -NEG, ALU.subtract, ALU.mult)
            ca.done(dve.tensor_reduce(small[:, 0:1], m8, AX.X, ALU.max))
            for b in (1, 3):
                dve.wait_ge(A["ctxT_mm"], t.upto(NB, b + 1))
                dve.tensor_copy(ctxT[:, t.slot, :, b, 0:MC * P],
                                psA[:, (b + 1) % 4, :].rearrange("p (k m) -> p k m", k=KC)).then_inc(A["ctxT_dve"], 1)

        def a02(t):
            dve.wait_ge(A["scores_mm"], t.upto(1, 1))
            ca.done(dve.scalar_tensor_tensor(sc0[:], psA[:, 1, 0:M], D ** -0.5, maskadd[:], ALU.mult, ALU.add))
            ca.done(dve.tensor_reduce(small[:, 3:4], sc0[:], AX.X, ALU.max))
            dve.tensor_scalar(small[:, 1:2], small[:, 3:4], -1.0, None, ALU.mult).then_inc(A["scores"], 1)
            dve.wait_ge(A["probs"], t.upto(1, 1))
            dve.tensor_scalar(p0_last[:], own_batch[:], p0[:, M - 1:M], None, ALU.mult).then_inc(A["probs_last"], 1)
            ca.done(dve.reciprocal(small[:, 4:5], small[:, 2:3]))
            ca.done(dve.tensor_tensor(small[:, 5:6], small[:, 4:5], small[:, 0:1], ALU.mult))

        def a04(t):
            dve.wait_ge(A["read_mm"], t.upto(1, 1))
            ca.done(dve.scalar_tensor_tensor(x1[:], psA[:, 3, 0:D], small[:, 5:6], x_in[:, t.slot], ALU.mult, ALU.add))
            norm(ca, x1[:], xn, stats, mv).then_inc(A["xn"], 1)

        def rope(t, n, mm, bank):
            if n >= 2:
                dve.wait_ge(A["rotT_mm"], t.upto(5, n - 1))
            dve.wait_ge(A["qkv_mm"], t.upto(6, mm))
            v = psA[:, bank, :].rearrange("p (h d) -> p h d", d=HD0)
            c3, s3 = (r.rearrange("p (h d) -> p h d", d=HD0) for r in (rope_c, rope_s))
            h = HD0 // 2
            dve.tensor_tensor(c3, v, cos0[:].unsqueeze(1).broadcast_to([P, 8, HD0]), ALU.mult)
            dve.tensor_tensor(s3[:, :, 0:h], v[:, :, h:], sin0[:, 0:h].unsqueeze(1).broadcast_to([P, 8, h]), ALU.mult)
            ca.done(dve.tensor_tensor(s3[:, :, h:], v[:, :, 0:h], sin0[:, h:].unsqueeze(1).broadcast_to([P, 8, h]), ALU.mult))
            dve.tensor_tensor(rot[:, n % 2], rope_c, rope_s, ALU.add).then_inc(A["rot"], 1)
            dve.wait_ge(A["rot"], t.upto(5, n + 1))

        def a06(t):
            rope(t, 0, 1, 2)
            rope(t, 1, 3, 0)

        def a07(t):
            rope(t, 2, 4, 1)
            rope(t, 3, 5, 0)
            rope(t, 4, 6, 1)

        def segments(x, n=32):
            return x.rearrange("p (g k) -> p g k", g=n)

        def a08(t):
            dve.wait_ge(A["att_mm"], t.upto(1, 1))
            s3 = segments(att[:])
            ca.done(dve.scalar_tensor_tensor(s3, psA[:, 0:2, :].rearrange("p a (g k) -> p (a g) k", k=S), HD0 ** -0.5,
                                             causal[:].unsqueeze(1).broadcast_to([P, 32, S]), ALU.mult, ALU.add))
            ca.done(dve.tensor_reduce(att_max[:], s3, AX.X, ALU.max))
            dve.tensor_tensor(s3, s3, att_max[:].unsqueeze(2).broadcast_to([P, 32, S]), ALU.subtract
                              ).then_inc(A["att_centred"], 1)
            dve.wait_ge(A["att_exp"], t.upto(1, 1))
            ca.done(dve.tensor_reduce(att_sum[:], s3, AX.X, ALU.add))
            ca.done(dve.reciprocal(att_sum[:], att_sum[:]))
            dve.tensor_tensor(s3, s3, att_sum[:].unsqueeze(2).broadcast_to([P, 32, S]), ALU.mult).then_inc(A["att"], 1)

        def a09(t):
            dve.wait_ge(A["attT_mm"], t.upto(2, 2))
            dve.tensor_copy(attT[:, 1], psA[:, 3, :]).then_inc(A["attT_dve"], 1)

        def a10(t):
            for b in (1, 3):
                dve.wait_ge(A["pv_mm"], t.upto(NB, b + 1))
                dve.tensor_copy(oT[:, :, :, b], psA[:, b, :].rearrange("p (c j q) -> p c j q", c=4, j=REP)
                                ).then_inc(A["oT_dve"], 1)

        def a11(t):
            dve.wait_ge(A["wo_mm"], t.upto(1, 1))
            ca.done(dve.tensor_tensor(x2[:], psA[:, 0, 0:D], x1[:], ALU.add))
            norm(ca, x2[:], xn, stats, mv).then_inc(A["xn"], 1)

        def a13(t):
            dve.wait_ge(A["tanh"], t.upto(1, 1))
            ca.done(dve.scalar_tensor_tensor(hid, th, 1.0, psA[:, 2:4, :].rearrange("p a n -> p (a n)"), ALU.add, ALU.mult))
            dve.wait_ge(A["up_mm"], t.upto(1, 1))
            dve.tensor_tensor(hid, hid, psA[:, 0:2, :].rearrange("p a n -> p (a n)"), ALU.mult).then_inc(A["hid"], 1)

        def a14(t):
            dve.wait_ge(A["hT_mm"], t.upto(2, 2))
            dve.tensor_copy(hT[:, 512:1024], psA[:, 3, :]).then_inc(A["hT_dve"], 1)

        def a15(t):
            dve.wait_ge(A["down_mm"], t.upto(1, 1))
            dve.scalar_tensor_tensor(x3[:, t.slot], psA[:, 0, 0:D], 0.5, x2[:], ALU.mult, ALU.add).then_inc(A["x3"], 1)
            ca.close()

        def ba(t, n):
            if n == 0:
                cb.open(t)
                dve.wait_ge(A["x3"], t.upto(1, 1))
                norm(cb, x3[:, t.slot], yn, stats_b, mv_b).then_inc(B["b_yn"], 1)
                dve.tensor_tensor(x3b[:], x3[:, t.slot], bo1[:], ALU.add)
            if n == 1:
                dve.wait_ge(B["b_q_mm"], t.upto(1, 1))
                cb.done(dve.tensor_tensor(q1[:], psB[:, 1, 0:D], bq1[:], ALU.add))
                cb.done(dve.tensor_tensor(q1sq[:], q1[:], q1[:], ALU.mult))
                cb.done(dve.tensor_reduce(q1ss[:, 0:1], q1sq[:], AX.X, ALU.add))
                cb.done(dve.tensor_scalar(q1ss[:, 0:1], q1ss[:, 0:1], 1.0 / D, 1e-6, ALU.mult, ALU.add))
                inverse_root(dve, cb, q1ss[:, 0:1], q1ss[:, 1:2], q1ss[:, 2:3])
                dve.scalar_tensor_tensor(q1[:], q1[:], q1ss[:, 1:2], gq1[:], ALU.mult, ALU.mult).then_inc(B["b_q"], 1)
            if n == 2:
                dve.wait_ge(B["b_qT_mm"], t.upto(1, 1))
                for c in range(KC):
                    ins = dve.tensor_tensor(
                        qbd[:, c],
                        psB[:, 2, c * P:(c + 1) * P].rearrange("p (b q) -> p b q", b=NB).unsqueeze(2).broadcast_to([P, NB, REP, S]),
                        gk_rows[:, c].unsqueeze(1).unsqueeze(3).broadcast_to([P, NB, REP, S]), ALU.mult)
                ins.then_inc(B["b_qbd"], 1)

        def bc(t, b):
            dve.wait_ge(B["b_kss_mm"], t.upto(NB, b + 1))
            dve.tensor_scalar(kms[:], psB[:, 3, 0:M], 1.0 / D, 1e-6, ALU.mult, ALU.add).then_inc(B["b_kms"], 1)
            dve.wait_ge(B["b_krs"], t.upto(NB, b + 1))
            cb.done(dve.tensor_tensor(kms[:], kms[:], krs[:], ALU.mult))
            cb.done(dve.tensor_tensor(kms[:], kms[:], krs[:], ALU.mult))
            cb.done(dve.tensor_scalar(kms[:], kms[:], -0.5, 1.5, ALU.mult, ALU.add))
            cb.done(dve.tensor_tensor(krs[:], kms[:], krs[:], ALU.mult))
            for m in range(KC):
                ins = dve.scalar_tensor_tensor(k1n[:, m], psB[:, m, 0:M], bk1[:, m:m + 1], krs[:], ALU.add, ALU.mult)
            ins.then_inc(B["b_kn"], 1)

        def bd(t, b):
            dve.wait_ge(B["b_scores_mm"], t.upto(NB, b + 1))
            cb.done(dve.tensor_reduce(p1max[:], psB[:, :, 0:M], AX.X, ALU.max))
            dve.tensor_scalar(p1max[:], p1max[:], -HD1 ** -0.5, None, ALU.mult).then_inc(B["b_max"], 1)
            dve.wait_ge(B["b_probs"], t.upto(NB, b + 1))
            dve.tensor_copy(p1_last[:, b, :, b], p1[:, :, M - 1]).then_inc(B["b_probs_last"], 1)
            cb.done(dve.reciprocal(p1rec[:], p1sum[:]))

        def be(t, b):
            dve.wait_ge(B["b_probsT_mm"], t.upto(3 * NB, 3 * b + 2))
            dve.tensor_copy(p1T[:, 512:1024], psB[:, 1, :]).then_inc(B["b_probsT_dve"], 1)

        def bf(t, b):
            dve.wait_ge(B["b_pv_mm"], t.upto(NB, b + 1))
            for h in range(REP):
                r = slice(S * h, S * h + S)
                ins = dve.tensor_tensor(o1[r, b], psB[r, 3, 0:D].rearrange("p (j h d) -> p j h d", j=REP, h=REP)[:, :, h],
                                        p1rec[r].unsqueeze(2).broadcast_to([S, REP, HD1]), ALU.mult)
            ins.then_inc(B["b_o"], 1)

        def bg(t, n):
            if n == 1:
                dve.wait_ge(B["b_wo_mm"], t.upto(1, 1))
                cb.done(dve.tensor_tensor(x4[:], psB[:, 1, 0:D], x3b[:], ALU.add))
                norm(cb, x4[:], yn, stats_b, mv_b).then_inc(B["b_yn"], 1)
                dve.tensor_tensor(x4b[:], x4[:], bo2[:], ALU.add)
            if n == 3:
                dve.wait_ge(B["b_qkv2_mm"], t.upto(1, 1))
                cb.done(dve.tensor_tensor(qkv[:], psB[:, 3, 0:384], bqkv2[:], ALU.add))
                v = qkv[:, 0:320].rearrange("p (h d) -> p h d", d=HD2)
                c3, s3 = (r[:].rearrange("p (h d) -> p h d", d=HD2) for r in (rc2, rs2))
                h, n_h = HD2 // 2, 320 // HD2
                dve.tensor_tensor(c3, v, cos2[:].unsqueeze(1).broadcast_to([P, n_h, HD2]), ALU.mult)
                dve.tensor_tensor(s3[:, :, 0:h], v[:, :, h:], sin2[:, 0:h].unsqueeze(1).broadcast_to([P, n_h, h]), ALU.mult)
                cb.done(dve.tensor_tensor(s3[:, :, h:], v[:, :, 0:h], sin2[:, h:].unsqueeze(1).broadcast_to([P, n_h, h]), ALU.mult))
                dve.tensor_tensor(rc2[:], rc2[:], rs2[:], ALU.add).then_inc(B["b_rot2"], 1)
                dve.tensor_tensor(v2bd, qkv[:, 320:384].rearrange("p (g d) -> p g d", g=G2).unsqueeze(2).broadcast_to([P, G2, NB, HD2]),
                                  own_batch[:].unsqueeze(1).unsqueeze(3).broadcast_to([P, G2, NB, HD2]), ALU.mult)
            if n == 4:
                dve.wait_ge(B["b_rot2T_mm"], t.upto(1, 1))
                dve.tensor_tensor(k2bd, psB[0:64, 1, 0:P].rearrange("p (b k) -> p b k", b=NB).unsqueeze(2).broadcast_to([64, NB, G2, S]),
                                  group_rows[:].unsqueeze(1).unsqueeze(3).broadcast_to([64, NB, G2, S]), ALU.mult).then_inc(B["b_k2bd"], 1)
            if n == 5:
                dve.wait_ge(B["b_att2_mm"], t.upto(1, 1))
                ps = psB[:, 2:4, :].rearrange("p a (g k) -> p (a g) k", k=S)
                s3 = segments(att2)
                cb.done(dve.tensor_reduce(att2_max[:], ps, AX.X, ALU.max))
                dve.tensor_tensor(s3, ps, att2_max[:].unsqueeze(2).broadcast_to([P, 32, S]), ALU.subtract).then_inc(B["b_centred2"], 1)
                dve.wait_ge(B["b_exp2"], t.upto(1, 1))
                cb.done(dve.tensor_reduce(att2_sum[:], s3, AX.X, ALU.add))
                cb.done(dve.reciprocal(att2_sum[:], att2_sum[:]))
            if n == 6:
                dve.wait_ge(B["b_att2T_mm"], t.upto(2, 2))
                dve.tensor_copy(att2T[:, 512:1024], psB[:, 1, :]).then_inc(B["b_att2T_dve"], 1)
            if n == 7:
                dve.wait_ge(B["b_pv2_mm"], t.upto(1, 1))
                dve.tensor_tensor(o2.rearrange("p b g d -> p g b d"), psB[:, 2, 0:D].rearrange("p (g b d) -> p g b d", g=G2, b=NB),
                                  att2_sum[:].rearrange("p (g b) -> p g b", g=G2).unsqueeze(3).broadcast_to([P, G2, NB, HD2]), ALU.mult
                                  ).then_inc(B["b_o2"], 1)
            if n == 9:
                dve.wait_ge(B["b_wo2_mm"], t.upto(1, 1))
                if not t.slot_first:
                    dve.wait_ge(stored[t.slot], 16 * t.n)
                cb.done(dve.tensor_tensor(x5[:, t.slot, 0:D], psB[:, 0, 0:D], x4b[:], ALU.add))
                norm(cb, x5[:, t.slot, 0:D], yn, stats_b, mv_b).then_inc(B["b_yn"], 1)
            if n == 11:
                dve.wait_ge(B["b_logits_mm"], t.upto(1, 1))
                cb.done(dve.tensor_tensor(lg[:], psB[:, 2, 0:EXPERTS], br[:], ALU.add))
                cb.done(dve.tensor_reduce(rt[:, 0:1], lg[:], AX.X, ALU.max))
                dve.tensor_scalar(rt[:, 1:2], rt[:, 0:1], -1.0, None, ALU.mult).then_inc(B["b_logits"], 1)
                dve.wait_ge(B["b_pexp"], t.upto(1, 1))
                dve.reciprocal(rt[:, 3:4], rt[:, 2:3])
                cb.done(dve.tensor_reduce(rt[:, 4:5], pr[:], AX.X, ALU.max))
                cb.done(dve.scalar_tensor_tensor(lg[:], pr[:], rt[:, 4:5], rank[:], ALU.is_equal, ALU.mult))
                cb.done(dve.tensor_reduce(rt[:, 5:6], lg[:], AX.X, ALU.max))
                dve.tensor_scalar(chosen[:, ds(t.i, 1), :].rearrange("p t e -> p (t e)"), lg[:], rt[:, 5:6], None, ALU.is_equal)
                dve.tensor_tensor(x5[:, t.slot, D:ROW], rt[:, 3:4], rt[:, 4:5], ALU.mult).then_inc(B["b_x5"], 1)
                cb.close()

        run(dve, dict(a01=a01, a02=a02, a04=a04, a06=a06, a07=a07, a08=a08, a09=a09, a10=a10, a11=a11, a13=a13, a14=a14,
                      a15=a15), dict(ba=ba, bb=lambda t, b: None, bc=bc, bd=bd, be=be, bf=bf, bg=bg))


def mixture_of_experts(nc, ctx, a, ident, chosen, x5_dram, sorted_dram, y_dram, out):
    def sb(name, shape, dt=F32):
        return ctx.enter_context(nc.sbuf_tensor(name, shape, dt))

    def sem(name):
        return ctx.enter_context(nc.semaphore(name))

    def sems(*names):
        return {n: sem(n) for n in names}

    GATHERS = 4
    wg = sb("wg", [P, EXPERTS, KC, F])
    wu = sb("wu", [P, EXPERTS, KC, F])
    wd = sb("wd", [P, EXPERTS, FC, D])
    x_all = sb("x_all", [P, TILES, ROW])
    before = sb("before", [P, P])
    tile_start = sb("tile_start", [P, TILES])
    tile_number = sb("tile_number", [P, SORTED_TILES])
    ones = sb("ones_m", [P, P])
    total = sb("total", [P, TILES, EXPERTS])
    sums = sb("sums", [P, 2, TILES, EXPERTS])
    place = sb("place", [P, TILES, EXPERTS])
    over = sb("over", [P, EXPERTS, TILES])
    tiles_of = sb("tiles_of", [P, EXPERTS])
    first_tile = sb("first_tile", [P, EXPERTS])
    first_row = sb("first_row", [P, EXPERTS])
    pos_f = sb("pos_f", [P, TILES])
    pos = sb("pos", [P, TILES], I32)
    expert_f = sb("expert_f", [P, SORTED_TILES])
    expert = sb("expert", [P, SORTED_TILES], I32)
    xs = sb("xs", [P, 2, ROW])
    xn = sb("xnm", [P, D])
    xnT = sb("xnTm", [P, 2, KC, P])
    stats = sb("stats_m", [P, 6])
    mv = sb("mv_m", [P, 4])
    th = sb("th_m", [P, F])
    hid = sb("hid_m", [P, 2, F])
    hT = sb("hT_m", [P, F])
    y = sb("y", [P, 2, D])
    back = sb("back", [P, GATHERS, D])
    fin = sb("fin", [P, 2, D])

    ps_g = ctx.enter_context(nc.psum_tensor("ps_g", [P, 2, 512], F32))
    ps_u = ctx.enter_context(nc.psum_tensor("ps_u", [P, 2, 512], F32))
    ps_t = ctx.enter_context(nc.psum_tensor("ps_t", [P, 2, 512], F32))
    ps_y = ctx.enter_context(nc.psum_tensor("ps_y", [P, 512], F32))
    ps_x = ctx.enter_context(nc.psum_tensor("ps_x", [P, 512], F32))

    weights_in, routing_in, all_in = sem("expert_weights_in"), sem("routing_constants_in"), sem("x_all_in")
    loaded = [sem("sorted_loaded0"), sem("sorted_loaded1")]
    y_stored = [sem("y_stored0"), sem("y_stored1")]
    scattered = sem("rows_scattered")
    gathered = [sem(f"rows_gathered{g}") for g in range(GATHERS)]
    out_stored = [sem("out_stored0"), sem("out_stored1")]
    dve_route, dve_m = sem("dve_own_routing"), sem("dve_own_m")
    C = sems("counted_mm", "ones_set", "placed", "m_xn", "m_xnT_mm", "m_xnT", "m_gate_mm", "m_up_mm", "m_tanh", "m_hid",
             "m_hT_mm", "m_hT_act", "m_hT_dve", "m_down_mm", "m_y", "m_fin")

    block = ctx.enter_context(nc.Block())

    def run(eng, norm, first, second):
        def tile(t, last):
            norm(t)
            first(t)
            if last is not None:
                second(last)

        tile(Tile(0, 0, 0), None)
        tile(Tile(1, 1, 0), Tile(0, 0, 0))
        tile(Tile(2, 0, 1), Tile(1, 1, 0))
        with eng.Fori(1, SORTED_TILES // 2) as k:
            tile(Tile(2 * k + 1, 1, k), Tile(2 * k, 0, k))
            tile(Tile(2 * k + 2, 0, k + 1), Tile(2 * k + 1, 1, k))
        second(Tile(SORTED_TILES - 1, 0, SORTED_TILES // 2))

    @block.sync
    def _(sp):
        for dst, src in ((before, "before"), (tile_start, "tile_start"), (tile_number, "tile_number")):
            sp.dma_start(dst[:], a[src]).then_inc(routing_in, 16)
        sp.dma_start(x_all[:], x5_dram.rearrange("(t p) d -> p t d", p=P)).then_inc(all_in, 16)
        for dst, src in ((wg, "wg"), (wu, "wu"), (wd, "wd")):
            sp.dma_start(dst[:], a[src]).then_inc(weights_in, 16)
        sp.wait_ge(scattered, 16 * TILES)

        def load(t):
            if not t.slot_first:
                sp.wait_ge(C["m_y"], t.upto(1, -1))
            sp.dma_start(xs[:, t.slot], sorted_dram[ds(t.i * P, P)]).then_inc(loaded[t.slot], 16)

        load(Tile(0, 0, 0))
        load(Tile(1, 1, 0))
        with sp.Fori(1, SORTED_TILES // 2) as k:
            load(Tile(2 * k, 0, k))
            load(Tile(2 * k + 1, 1, k))
        load(Tile(SORTED_TILES - 1, 0, SORTED_TILES // 2))
        for i in range(TILES):
            sp.wait_ge(C["m_fin"], i + 1)
            sp.dma_start(out[i * P:(i + 1) * P], fin[:, i % 2]).then_inc(out_stored[i % 2], 16)
        for s in out_stored:
            sp.wait_ge(s, 16 * (TILES // 2))

    @block.gpsimd
    def _(pool):
        pool.wait_ge(all_in, 16)
        pool.wait_ge(C["placed"], 1)
        for i in range(TILES):
            pool.indirect_dma_start(out=sorted_dram, out_offset=bass.IndirectOffsetOnAxis(ap=pos[:, i:i + 1], axis=0),
                                    in_=x_all[:, i], in_offset=None).then_inc(scattered, 16)
        for i in range(TILES):
            if i == 0:
                for s, n in zip(y_stored, (SORTED_TILES // 2 + 1, SORTED_TILES // 2)):
                    pool.wait_ge(s, 16 * n)
            if i >= GATHERS:
                pool.wait_ge(C["m_fin"], i - GATHERS + 1)
            pool.indirect_dma_start(out=back[:, i % GATHERS], out_offset=None, in_=y_dram,
                                    in_offset=bass.IndirectOffsetOnAxis(ap=pos[:, i:i + 1], axis=0)
                                    ).then_inc(gathered[i % GATHERS], 16)

    @block.tensor
    def _(pe):
        pe.wait_ge(routing_in, 48)
        pe.wait_ge(C["ones_set"], 1)
        flat = chosen[:].rearrange("p t e -> p (t e)")
        pe.matmul(ps_x[:, 0:P], before[:], flat, start=True, stop=True)
        pe.matmul(ps_y[:, 0:P], ones[:], flat, start=True, stop=True).then_inc(C["counted_mm"], 1)
        pe.wait_ge(C["placed"], 1)
        pe.wait_ge(weights_in, 48)

        def norm(t):
            pe.wait_ge(C["m_xn"], t.upto(1, 1))
            for c in range(KC):
                mm = pe.transpose(ps_x[:, c * P:(c + 1) * P], xn[:, c * P:(c + 1) * P], ident[:])
            mm.then_inc(C["m_xnT_mm"], 1)

        def expert_of(t):
            return pe.value_load(expert[0:1, ds(t.i, 1)], min_val=0, max_val=EXPERTS - 1)

        def first(t):
            pe.wait_ge(C["m_xnT"], t.upto(1, 1))
            if not t.first:
                pe.wait_ge(C["m_hid"], t.upto(1, 0))
            e = expert_of(t)
            for ps, w, done in ((ps_g, wg, C["m_gate_mm"]), (ps_u, wu, C["m_up_mm"])):
                for h in range(2):
                    for c in range(KC):
                        mm = pe.matmul(ps[:, h], xnT[:, t.slot, c], w[:, ds(e, 1), c, h * 512:(h + 1) * 512],
                                       start=(c == 0), stop=(c == KC - 1))
                mm.then_inc(done, 1)

        def second(t):
            pe.wait_ge(C["m_hid"], t.upto(1, 1))
            for h in range(2):
                for c in range(4):
                    at = h * 512 + c * P
                    mm = pe.transpose(ps_t[:, h, c * P:(c + 1) * P], hid[:, t.slot, at:at + P], ident[:])
                mm.then_inc(C["m_hT_mm"], 1)
            e = expert_of(t)
            if not t.first:
                pe.wait_ge(C["m_y"], t.upto(1, 0))
            pe.wait_ge(C["m_hT_act"], t.upto(1, 1))
            pe.wait_ge(C["m_hT_dve"], t.upto(1, 1))
            for c in range(FC):
                mm = pe.matmul(ps_y[:, 0:D], hT[:, c * P:(c + 1) * P], wd[:, ds(e, 1), c], start=(c == 0), stop=(c == FC - 1))
            mm.then_inc(C["m_down_mm"], 1)

        run(pe, norm, first, second)

    @block.scalar
    def _(act):
        def norm(t):
            act.wait_ge(C["m_xnT_mm"], t.upto(1, 1))
            act.copy(xnT[:, t.slot].rearrange("p c q -> p (c q)"), ps_x[:, 0:D]).then_inc(C["m_xnT"], 1)

        def first(t):
            act.wait_ge(C["m_gate_mm"], t.upto(1, 1))
            act.activation(th[:], ps_g[:].rearrange("p a n -> p (a n)"), ACT.Tanh, scale=0.5).then_inc(C["m_tanh"], 1)

        def second(t):
            act.wait_ge(C["m_hT_mm"], t.upto(2, 1))
            act.copy(hT[:, 0:512], ps_t[:, 0]).then_inc(C["m_hT_act"], 1)
            act.wait_ge(C["m_y"], t.upto(1, 1))
            act.dma_start(y_dram[ds(t.i * P, P)], y[:, t.slot]).then_inc(y_stored[t.slot], 16)

        run(act, norm, first, second)

    @block.vector
    def _(dve):
        dve.memset(ones[:], 1.0).then_inc(C["ones_set"], 1)
        dve.wait_ge(routing_in, 48)
        dve.wait_ge(C["counted_mm"], 1)
        rt = Tile(0, 0, 0)
        cr = Chain(dve, dve_route, 0)
        cr.open(rt)
        cr.done(dve.tensor_copy(total[:], ps_y[:, 0:P].rearrange("p (t e) -> p t e", e=EXPERTS)))
        old, step, n = total[:], 1, 0
        while step < TILES:
            new = sums[:, n % 2]
            dve.tensor_copy(new[:, 0:step], old[:, 0:step])
            cr.done(dve.tensor_tensor(new[:, step:], old[:, step:], old[:, 0:TILES - step], ALU.add))
            old, step, n = new, 2 * step, n + 1
        count = old[:, TILES - 1]
        cr.done(dve.tensor_tensor(over[:], count.unsqueeze(2).broadcast_to([P, EXPERTS, TILES]),
                                  tile_start[:].unsqueeze(1).broadcast_to([P, EXPERTS, TILES]), ALU.is_gt))
        cr.done(dve.tensor_reduce(tiles_of[:], over[:], AX.X, ALU.add))
        cr.done(dve.memset(first_tile[:, 0:1], 0.0))
        for e in range(1, EXPERTS):
            cr.done(dve.tensor_tensor(first_tile[:, e:e + 1], first_tile[:, e - 1:e], tiles_of[:, e - 1:e], ALU.add))
        cr.done(dve.tensor_scalar(first_row[:], first_tile[:], float(P), None, ALU.mult))
        cr.done(dve.tensor_tensor(place[:], old, total[:], ALU.subtract))
        cr.done(dve.tensor_tensor(place[:], place[:], ps_x[:, 0:P].rearrange("p (t e) -> p t e", e=EXPERTS), ALU.add))
        cr.done(dve.tensor_tensor(place[:], place[:], first_row[:].unsqueeze(1).broadcast_to([P, TILES, EXPERTS]), ALU.add))
        cr.done(dve.tensor_tensor(place[:], place[:], chosen[:], ALU.mult))
        cr.done(dve.tensor_reduce(pos_f[:], place[:], AX.X, ALU.add))
        dve.tensor_copy(pos[:], pos_f[:])
        cr.done(dve.tensor_scalar(expert_f[:], tile_number[:], first_tile[:, 1:2], None, ALU.is_ge))
        for e in range(2, EXPERTS):
            cr.done(dve.scalar_tensor_tensor(expert_f[:], tile_number[:], first_tile[:, e:e + 1], expert_f[:], ALU.is_ge, ALU.add))
        dve.tensor_copy(expert[:], expert_f[:]).then_inc(C["placed"], 1)

        cm = Chain(dve, dve_m, CHAIN_M)

        def norm(t):
            cm.open(t)
            dve.wait_ge(loaded[t.slot], t.n * 16 + 16)
            layer_norm(dve, cm, xs[:, t.slot, 0:D], xn[:], stats[:], mv).then_inc(C["m_xn"], 1)

        def first(t):
            dve.wait_ge(C["m_tanh"], t.upto(1, 1))
            cm.done(dve.scalar_tensor_tensor(hid[:, t.slot], th[:], 1.0, ps_g[:].rearrange("p a n -> p (a n)"), ALU.add, ALU.mult))
            dve.wait_ge(C["m_up_mm"], t.upto(1, 1))
            dve.tensor_tensor(hid[:, t.slot], hid[:, t.slot], ps_u[:].rearrange("p a n -> p (a n)"), ALU.mult
                              ).then_inc(C["m_hid"], 1)
            cm.close()

        def second(t):
            dve.wait_ge(C["m_hT_mm"], t.upto(2, 2))
            dve.tensor_copy(hT[:, 512:1024], ps_t[:, 1]).then_inc(C["m_hT_dve"], 1)
            dve.wait_ge(C["m_down_mm"], t.upto(1, 1))
            if not t.slot_first:
                dve.wait_ge(y_stored[t.slot], 16 * t.n)
            dve.tensor_scalar(y[:, t.slot], ps_y[:, 0:D], xs[:, t.slot, D:ROW], 0.5, ALU.mult, ALU.mult).then_inc(C["m_y"], 1)

        run(dve, norm, first, second)
        for i in range(TILES):
            dve.wait_ge(gathered[i % GATHERS], 16 * (i // GATHERS + 1))
            if i >= 2:
                dve.wait_ge(out_stored[i % 2], 16 * (i // 2))
            dve.tensor_tensor(fin[:, i % 2], back[:, i % GATHERS], x_all[:, i, 0:D], ALU.add).then_inc(C["m_fin"], 1)


def rope_tables(width, base=10000.0):
    inv = (np.float32(base) ** (-np.arange(0, width, 2, dtype=np.float32) / np.float32(width))).astype(np.float32)
    th = np.outer(np.arange(S, dtype=np.float32), inv).astype(np.float32)
    cos, sin = np.cos(th), np.sin(th)
    return (np.tile(np.concatenate([cos, cos], 1), (NB, 1)).astype(np.float32),
            np.tile(np.concatenate([-sin, sin], 1), (NB, 1)).astype(np.float32))


def lay_out(i):
    f = {n: np.asarray(v) for n, v in i.items()}

    def chunks(w):
        return w.reshape(-1, P, w.shape[-1]).transpose(1, 0, 2)

    def rep(v, n=P):
        return np.broadcast_to(v[None], (n, v.shape[0]))

    a = {}
    a["x"] = f["x"].reshape(TILES, P, D)
    a["ctx"] = f["ctx_2048"]
    a["mask"] = np.repeat(f["mask_BxS2_bk0"], S, axis=0).reshape(TILES, P, M)
    a["wkv0"] = chunks(np.concatenate([f["L0_attn_wk"], f["L0_attn_wv"]], 1))
    a["wq0"] = chunks(f["L0_attn_wq"].reshape(D, 4, 2, REP, HD0).transpose(0, 1, 3, 2, 4).reshape(D, -1))
    a["wo0"] = f["L0_attn_wo"].reshape(4, 2, REP, HD0, D).transpose(0, 2, 1, 3, 4).reshape(16, P, D).transpose(1, 0, 2)
    a["wgate0"] = chunks(f["L0_ffn_w_gate"].T)
    a["wup0"] = chunks(f["L0_ffn_w_up"].T)
    a["wdown0"] = chunks(f["L0_ffn_w_down"].T)
    a["wq1"] = chunks(f["L1_xattn_Wq"])
    a["wk1"] = chunks(f["L1_xattn_Wk_img"])
    a["wv1"] = chunks(f["L1_xattn_Wv_img"])
    a["wo1"] = f["L1_xattn_Wo"].reshape(4, REP, HD1, D).transpose(0, 2, 1, 3).reshape(64, REP, D)
    a["bv1"] = f["L1_xattn_bv_img"].reshape(4, REP, HD1).transpose(0, 2, 1).reshape(64, REP)
    a["bq1"], a["gq1"], a["bo1"] = (rep(f["L1_xattn_" + n]) for n in ("bq", "gq", "bo"))
    a["bk1"], a["gk1"] = (f["L1_xattn_" + n].reshape(KC, P).T for n in ("bk_img", "gk_img"))
    wq2 = f["L1_attn_Wq"].T.reshape(D, G2, REP, HD2).transpose(0, 2, 1, 3).reshape(D, D)
    bq2 = f["L1_attn_bq"].reshape(G2, REP, HD2).transpose(1, 0, 2).reshape(D)
    a["wqkv2"] = chunks(np.concatenate([wq2, f["L1_attn_Wk"].T, f["L1_attn_Wv"].T], 1))
    a["bqkv2"] = rep(np.concatenate([bq2, f["L1_attn_bk"], f["L1_attn_bv"]]))
    a["wo2"] = f["L1_attn_Wo"].T.reshape(G2, REP, HD2, D).transpose(0, 2, 1, 3).reshape(64, REP, D)
    a["bo2"] = rep(f["L1_attn_bo"])
    a["wr"] = chunks(f["L1_ffn_Wr"])
    a["br"] = rep(f["L1_ffn_br"])
    a["wg"], a["wu"], a["wd"] = (f["L1_ffn_" + n].reshape(EXPERTS, -1, P, m).transpose(2, 0, 1, 3)
                                 for n, m in (("Wg", F), ("Wu", F), ("Wd", D)))
    a["ident"] = np.eye(P, dtype=np.float32)
    a["cos0"], a["sin0"] = rope_tables(HD0)
    a["cos2"], a["sin2"] = rope_tables(HD2)
    q = np.arange(P)
    a["causal"] = np.where(np.arange(S)[None] <= (q % S)[:, None], 0.0, NEG).astype(np.float32)
    a["own_batch"] = (q[:, None] // S == np.arange(NB)[None]).astype(np.float32)
    a["head_rows"] = ((q[:, None] // HD1) % REP == np.arange(REP)[None]).astype(np.float32)
    a["group_rows"] = (np.arange(64)[:, None] // HD2 == np.arange(G2)[None]).astype(np.float32)
    a["before"] = (q[:, None] < q[None]).astype(np.float32)
    a["tile_start"] = rep(np.arange(TILES, dtype=np.float32) * P)
    a["tile_number"] = rep(np.arange(SORTED_TILES, dtype=np.float32))
    a["rank"] = rep(np.arange(EXPERTS, 0, -1).astype(np.float32))
    return {n: np.ascontiguousarray(v) for n, v in a.items()}


def kernel(**inputs):
    import concourse.bacc as _bacc
    from concourse.bass_utils import run_bass_kernel_spmd as _run

    nc = _bacc.Bacc("TRN2", target_bir_lowering=False, num_devices=1)
    arrays = lay_out(inputs)
    a = {n: nc.dram_tensor("in_" + n, v.shape, mybir.dt.from_np(v.dtype), kind="ExternalInput").ap() for n, v in arrays.items()}
    out = nc.dram_tensor("out", [TOKENS, D], F32, kind="ExternalOutput").ap()
    build(nc, a, out)
    r = _run(nc, [{"in_" + n: v for n, v in arrays.items()}], core_ids=[0])
    return r.results[0]["out"].reshape(BATCHES, S, D)
```

```python
from contextlib import ExitStack

import numpy as np

import concourse.bass as bass
from concourse import mybir

F32 = mybir.dt.float32
U8 = mybir.dt.uint8
I32 = mybir.dt.int32
ALU = mybir.AluOpType
ACT = mybir.ActivationFunctionType
AX = mybir.AxisListType

P = 128
S = 32
NB = P // S
D = 256
KC = D // P
M = 257
MC = 2
BATCHES = 128
TILES = BATCHES // NB
TOKENS = BATCHES * S
F = 1024
FC = F // P
EXPERTS = 4
H0, G0, HD0 = 32, 8, 64
KV0 = G0 * HD0
H1, HD1 = 16, 16
G2, HD2 = 8, 8
REP = 4
NEG = -1e30
ROW = D + 1
SORTED_TILES = TILES + EXPERTS - 1
LOADS = 4
RSQRT_SEED = 0x5F3759DF + 0x40000000 - 0x00400000
CHAIN_N, CHAIN_K = 11, 4
CHAIN_A, CHAIN_B, CHAIN_M = 50, 54, 11
ORDER = """
    bb.0 a01.0 bc.0 a01.1 ba.0 a01.2 bn.0 ba.1 a01.3 a01.4 a02.0 ba.2 bs.0 a02.20 a03.0 bd.0 a04.0 be.0 a04.40
    bb.1 a05.0 bc.1 bn.1 bf.0 a06.0 ar.0 bs.1 bd.1 a06.1 a06.2 be.1 ar.1
    bb.2 a07.0 bc.2 bn.2 bf.1 a06.3 ar.2 bs.2 bd.2 a07.5 a07.1 a07.2 be.2 a07.3 ar.3 ar.4
    bb.3 bc.3 bn.3 bf.2 a07.4 bs.3 bd.3 a08.0 a08.1 a08.2 a08.3 be.3 a08.30 bf.3 bg.0 a08.31 bg.1 a09.0 bg.15
    a10.0 a10.1 a10.2 a10.3 bg.2 a11.0 bg.3 a11.1 a11.2 a11.3 bg.4 a11.30
    bg.5 a12.0 bg.55 a13.0 a13.1 bg.56 bg.6 a00.0 a13.2 bg.7 a13.3 bg.8 bg.9 a14.0 bg.90
    a15.0 a15.1 bg.10 bg.11
""".split()
ds = bass.ds


class Tile:

    def __init__(self, i, slot, n):
        self.i, self.slot, self.n = i, slot, n
        self.first = isinstance(i, int) and i == 0
        self.slot_first = isinstance(n, int) and n == 0

    def upto(self, per, k):
        return self.i * per + k


class Chain:

    def __init__(self, eng, sem, per):
        self.eng, self.sem, self.per, self.t, self.n = eng, sem, per, None, 0

    def open(self, t, n=0):
        self.t, self.n = t, n

    def close(self):
        assert self.n == self.per, ("CHAIN", self.n, self.per)

    def done(self, ins):
        self.n += 1
        ins.then_inc(self.sem, 1)
        self.eng.wait_ge(self.sem, self.t.upto(self.per, self.n))


def inverse_root(dve, chain, v, scale, eps, h, y):
    chain.done(dve.tensor_scalar(h, v, -0.5 * scale, -0.5 * eps, ALU.mult, ALU.add))
    chain.done(dve.tensor_scalar(y.bitcast(I32), h.bitcast(I32), 1, None, ALU.logical_shift_right))
    chain.done(dve.tensor_scalar(y.bitcast(I32), y.bitcast(I32), -1.0, float(RSQRT_SEED), ALU.mult, ALU.add))
    for _ in range(3):
        chain.done(dve.scalar_tensor_tensor(v, h, y, y, ALU.mult, ALU.mult))
        chain.done(dve.scalar_tensor_tensor(y, v, 1.5, y, ALU.add, ALU.mult))


def layer_norm(dve, chain, x, y, stats, mv):
    chain.done(dve.bn_stats(stats, x))
    dve.memset(mv[:, 3:4], 0.0)
    chain.done(dve.bn_aggr(mv[:, 0:2], stats))
    inverse_root(dve, chain, mv[:, 1:2], 1.0, 1e-5, mv[:, 2:3], mv[:, 3:4])
    return dve.tensor_scalar(y, x, mv[:, 0:1], mv[:, 3:4], ALU.subtract, ALU.mult)


def build(nc, a, out):
    x5_dram = nc.dram_tensor("x5_scratch", [TOKENS, ROW], F32, kind="Internal").ap()
    sorted_dram = nc.dram_tensor("sorted_scratch", [SORTED_TILES * P, ROW], F32, kind="Internal").ap()
    y_dram = nc.dram_tensor("y_scratch", [SORTED_TILES * P, D], F32, kind="Internal").ap()
    with ExitStack() as both:
        ident = both.enter_context(nc.sbuf_tensor("ident", [P, P], F32))
        chosen = both.enter_context(nc.sbuf_tensor("chosen", [P, TILES, EXPERTS], F32))
        with ExitStack() as ctx:
            layers_0_to_attention_1(nc, ctx, a, ident, chosen, x5_dram, sorted_dram)
        with ExitStack() as ctx:
            mixture_of_experts(nc, ctx, a, ident, chosen, x5_dram, sorted_dram, y_dram, out)


def layers_0_to_attention_1(nc, ctx, a, ident, chosen, x5_dram, sorted_dram):
    def sb(name, shape, dt=F32):
        return ctx.enter_context(nc.sbuf_tensor(name, shape, dt))

    def sem(name):
        return ctx.enter_context(nc.semaphore(name))

    loads = []

    def const(name, shape, src=None, dt=F32):
        t = sb("c_" + name, shape, dt)
        loads.append((t, a[src or name]))
        return t

    loads.append((ident, a["ident"]))
    wkv0 = const("wkv0", [P, KC, 2 * KV0])
    wq0 = const("wq0", [P, KC, H0 * HD0])
    wo0 = const("wo0", [P, H0 * HD0 // P, D])
    wgate0 = const("wgate0", [P, KC, F])
    wup0 = const("wup0", [P, KC, F])
    wdown0 = const("wdown0", [P, FC, D])
    wq1 = const("wq1", [P, KC, D])
    wk1 = const("wk1", [P, KC, D])
    wv1 = const("wv1", [P, KC, D])
    wo1 = const("wo1", [64, REP, D])
    wqkv2 = const("wqkv2", [P, KC, 384])
    wo2 = const("wo2", [64, REP, D])
    cos0 = const("cos0", [P, HD0])
    sin0 = const("sin0", [P, HD0])
    cos2 = const("cos2", [P, HD2])
    sin2 = const("sin2", [P, HD2])
    causal = const("causal", [P, S])
    own_batch = const("own_batch", [P, NB])
    head_rows = const("head_rows", [P, REP])
    group_rows = const("group_rows", [64, G2])
    bq1 = const("bq1", [P, D])
    gq1 = const("gq1", [P, D])
    bk1 = const("bk1", [P, KC])
    gk1 = const("gk1", [P, KC])
    bv1 = const("bv1", [64, REP])
    bo1 = const("bo1", [P, D])
    bqkv2 = const("bqkv2", [P, 384])
    bo2 = const("bo2", [P, D])
    wr = const("wr", [P, KC, EXPERTS])
    br = const("br", [P, EXPERTS])
    rank = const("rank", [P, EXPERTS])

    x_in = sb("x_in", [P, 2, D])
    rows = sb("ctx_rows", [P, 2, NB, MC, D])
    last_row = sb("ctx_last_row", [NB, 2, D])
    mask_u8 = sb("mask_u8", [P, 2, M], U8)
    ctxT = sb("ctxT", [P, 2, KC, NB, M])
    xn = sb("xn", [P, D])
    xnT_sb = sb("xnT_sb", [P, KC, P])
    stats = sb("stats", [P, 6])
    mv = sb("mv", [P, 4])
    small = sb("small", [P, 8])
    p0_last = sb("p0_last", [P, NB])
    p0T = sb("p0T", [P, MC, P])
    p0T_last = sb("p0T_last", [NB, P])
    x1 = sb("x1", [P, D])
    v0 = sb("v0", [P, KV0])
    qT = sb("qT", [P, 4, NB, REP, S])
    kT = sb("kT", [P, 4, NB, 2, S])
    att = sb("att", [P, 2 * 512])
    rope_c, rope_s = att[:, 0:512], att[:, 512:1024]
    maskadd, sc0, p0 = (att[:, k * M:(k + 1) * M] for k in range(3))
    att_max = sb("att_max", [P, 32])
    att_sum = sb("att_sum", [P, 32])
    attT = sb("attT", [P, 2, 512])
    rot = attT
    oT = sb("oT", [P, 4, REP, NB, S])
    x2 = sb("x2", [P, D])
    th = qT[:].rearrange("p c b j q -> p (c b j q)")[:, 0:F]
    hid = qT[:].rearrange("p c b j q -> p (c b j q)")[:, F:2 * F]
    hT = oT[:].rearrange("p c j b q -> p (c j b q)")[:, 0:F]
    x3 = sb("x3", [P, 2, D])

    yn = sb("yn", [P, D])
    yn1 = sb("yn1", [P, D])
    ynT = sb("ynT", [P, KC, P])
    stats_b = sb("stats_b", [P, 6])
    mv_b = sb("mv_b", [P, 4])
    ones = sb("ones", [P, P])
    gk_rows = sb("gk_rows", [P, KC, REP])
    q1 = sb("q1", [P, D])
    q1sq = yn
    q1ss = sb("q1ss", [P, 3])
    qbd = sb("qbd", [P, KC, NB, REP, S])
    ksq = sb("ksq", [P, KC, M])
    krs = sb("krs", [P, M])
    kms = sb("kms", [P, M])
    k1n = sb("k1n", [P, KC, M])
    v1 = sb("v1", [P, 2, MC, D])
    v1_last = sb("v1_last", [NB, D])
    p1 = sb("p1", [P, REP, M])
    p1max = sb("p1max", [P, REP])
    p1sum = sb("p1sum", [P, REP])
    p1rec = sb("p1rec", [P, REP])
    p1_last = sb("p1_last", [P, NB, REP, NB])
    p1T = sb("p1T", [P, 1024])
    p1T_last = sb("p1T_last", [NB, 512])
    o1 = sb("o1", [P, NB, REP, HD1])
    o1T = sb("o1T", [64, REP, NB, S])
    x3b = sb("x3b", [P, D])
    x4 = sb("x4", [P, D])
    x4b = sb("x4b", [P, D])
    qkv = sb("qkv", [P, 384])
    rc2 = sb("rc2", [P, 320])
    rs2 = sb("rs2", [P, 320])
    q2T = v1[0:64, 0].rearrange("p c d -> p (c d)").rearrange("p (b j q) -> p b j q", b=NB, j=REP)
    k2bd = p1[0:64].rearrange("p j m -> p (j m)")[:, 0:NB * G2 * S].rearrange("p (b g k) -> p b g k", b=NB, g=G2)
    v2bd = ksq[:].rearrange("p c m -> p (c m)")[:, 0:D].rearrange("p (g b d) -> p g b d", g=G2, b=NB)
    att2 = qbd[:].rearrange("p c b h q -> p (c b h q)")
    att2_max = sb("att2_max", [P, 32])
    att2_sum = sb("att2_sum", [P, 32])
    att2T = p1T
    o2 = o1[:].rearrange("p b j d -> p (b j d)").rearrange("p (b g d) -> p b g d", b=NB, g=G2)
    o2T = o1T
    x5 = sb("x5", [P, 2, ROW])
    lg = sb("lg", [P, EXPERTS])
    pr = sb("pr", [P, EXPERTS])
    rt = sb("router", [P, 6])
    zero_row = x5[:, 1]

    psA = ctx.enter_context(nc.psum_tensor("psA", [P, 4, 512], F32))
    psB = ctx.enter_context(nc.psum_tensor("psB", [P, 4, 512], F32))

    def sems(*names):
        return {n: sem(n) for n in names}

    const_in = sem("const_in")
    loaded = [sem("tile_loaded_slot0"), sem("tile_loaded_slot1")]
    stored = [sem("x5_stored_slot0"), sem("x5_stored_slot1")]
    dve_n, dve_k = sem("dve_own_results_norm1"), sem("dve_own_results_keys")
    dve_a, dve_b = sem("dve_own_results_a"), sem("dve_own_results_b")
    setup_done = sem("setup_done")
    setup_chain = sem("setup_chain")
    A = sems("xn1", "xn", "xnT_mm", "xnT", "ctxT_mm", "ctxT", "scores_mm", "scores", "probs", "probs_last",
             "probsT_mm", "probsT", "read_mm", "qkv_mm", "v", "rot", "rotT_mm", "rotT", "att_mm", "att_centred",
             "att_exp", "att", "attT_mm", "attT_act", "attT_dve", "pv_mm", "oT_act", "oT_dve", "wo_mm", "gate_mm",
             "up_mm", "tanh", "hid", "hT_mm", "hT_act", "hT_dve", "down_mm", "x3", "yn1")
    B = sems("b_yn", "b_ynT_mm", "b_ynT", "b_q_mm", "b_q", "b_qT_mm", "b_qbd", 
             "b_k_mm", "b_v_mm", "b_ksq", "b_kss_mm", "b_kms", "b_kln", "b_krs", "b_kn", "b_v", "b_scores_mm", "b_max", "b_probs", "b_probs_last",
             "b_probsT_mm", "b_probsT_act", "b_probsT_dve", "b_pv_mm", "b_o", "b_oT_mm", "b_oT", "b_wo_mm",
             "b_qkv2_mm", "b_rot2", "b_rot2T_mm", "b_q2T", "b_k2bd", "b_att2_mm", "b_centred2", "b_exp2", "b_sum2",
             "b_att2T_mm", "b_att2T_act", "b_att2T_dve", "b_pv2_mm", "b_o2", "b_o2T_mm", "b_o2T", "b_wo2_mm", "b_logits_mm", "b_logits", "b_pexp", "b_x5")
    zeroed = sem("sorted_rows_zeroed")

    def run(eng, stage_a, stage_b):
        if "a00" in stage_a:
            stage_a["a00"](Tile(0, 0, 0), 0)
        weave(stage_a, Tile(0, 0, 0), stage_b, None, Tile(1, 1, 0))
        weave(stage_a, Tile(1, 1, 0), stage_b, Tile(0, 0, 0), Tile(2, 0, 1))
        weave(stage_a, Tile(2, 0, 1), stage_b, Tile(1, 1, 0), Tile(3, 1, 1))
        with eng.Fori(1, TILES // 2 - 1) as k:
            weave(stage_a, Tile(2 * k + 1, 1, k), stage_b, Tile(2 * k, 0, k), Tile(2 * k + 2, 0, k + 1))
            weave(stage_a, Tile(2 * k + 2, 0, k + 1), stage_b, Tile(2 * k + 1, 1, k), Tile(2 * k + 3, 1, k + 1))
        weave(stage_a, Tile(TILES - 1, 1, TILES // 2 - 1), stage_b, Tile(TILES - 2, 0, TILES // 2 - 1), None)
        weave(stage_a, None, stage_b, Tile(TILES - 1, 1, TILES // 2 - 1), None)

    def weave(stage_a, ta, stage_b, tb, after):
        for name, part in (s.split(".") for s in ORDER):
            if name == "a00":
                if ta is not None and after is not None and name in stage_a:
                    stage_a[name](after, 0)
            elif name[0] == "a":
                if ta is not None and name in stage_a:
                    stage_a[name](ta, int(part))
            elif tb is not None and name in stage_b:
                stage_b[name](tb, int(part))

    block = ctx.enter_context(nc.Block())

    @block.sync
    def _(sp):
        for dst, src in loads:
            sp.dma_start(dst[:], src).then_inc(const_in, 16)

        def load(t):
            if not t.slot_first:
                sp.wait_ge(A["xn"], t.upto(2, 1 - 4))
            done = loaded[t.slot]
            sp.dma_start(x_in[:, t.slot], a["x"][ds(t.i, 1)].rearrange("t p d -> (t p) d")).then_inc(done, 16)
            sp.dma_start(rows[:, t.slot].rearrange("p b c d -> p b (c d)"),
                         a["ctx"][ds(t.i * NB, NB), 0:MC * P].rearrange("b (p c) d -> p b (c d)", c=MC)).then_inc(done, 16)
            sp.dma_start(last_row[:, t.slot], a["ctx"][ds(t.i * NB, NB), M - 1]).then_inc(done, 16)
            sp.dma_start(mask_u8[:, t.slot], a["mask"][ds(t.i, 1)].rearrange("t p m -> (t p) m")).then_inc(done, 16)

        load(Tile(0, 0, 0))
        load(Tile(1, 1, 0))
        with sp.Fori(1, TILES // 2) as k:
            load(Tile(2 * k, 0, k))
            load(Tile(2 * k + 1, 1, k))

    @block.gpsimd
    def _(pool):
        def store(t):
            pool.wait_ge(B["b_x5"], t.upto(1, 1))
            pool.dma_start(x5_dram[ds(t.i * P, P)], x5[:, t.slot]).then_inc(stored[t.slot], 16)

        pool.wait_ge(setup_done, 1)
        pool.dma_start(sorted_dram.rearrange("(t p) d -> p t d", p=P),
                       zero_row.unsqueeze(1).broadcast_to([P, SORTED_TILES, ROW])).then_inc(zeroed, 16)
        with pool.Fori(0, TILES // 2) as k:
            store(Tile(2 * k, 0, k))
            store(Tile(2 * k + 1, 1, k))
        for s in stored:
            pool.wait_ge(s, 16 * (TILES // 2))
        pool.wait_ge(zeroed, 16)

    def wait_loaded(eng, t):
        eng.wait_ge(loaded[t.slot], t.n * 16 * LOADS + 16 * LOADS)

    @block.tensor
    def _(pe):
        pe.wait_ge(const_in, 16 * len(loads))
        pe.wait_ge(setup_done, 1)

        def transpose(out, in_):
            return pe.transpose(out, in_, ident[0:in_.shape[0], 0:in_.shape[0]])

        def xnT(t, k, bank):
            if k == 1:
                pe.wait_ge(A["xn1"], t.upto(1, 1))
            else:
                pe.wait_ge(A["xn"], t.upto(2, k - 1))
            for c in range(KC):
                mm = transpose(psA[:, bank, c * P:(c + 1) * P], xn[:, c * P:(c + 1) * P])
            return mm

        def a01(t, n):
            if n == 0:
                wait_loaded(pe, t)
                if not t.first:
                    pe.wait_ge(A["x3"], t.upto(1, 0))
                xnT(t, 1, 0)
                for c in range(KC):
                    mm = transpose(psA[:, 0, 2 * P + c * NB:2 * P + (c + 1) * NB], last_row[:, t.slot, c * P:(c + 1) * P])
                mm.then_inc(A["xnT_mm"], 1)
                return
            b = n - 1
            if b == NB - 1:
                pe.wait_ge(A["xnT"], t.upto(3, 1))
            for kc in range(KC):
                for c in range(MC):
                    at = (kc * MC + c) * P
                    mm = transpose(psA[:, (b + 1) % 4, at:at + P], rows[:, t.slot, b, c, kc * P:(kc + 1) * P])
            mm.then_inc(A["ctxT_mm"], 1)

        def a02(t, n):
            if n != 0:
                return
            pe.wait_ge(A["xnT"], t.upto(3, 1))
            pe.wait_ge(A["ctxT"], t.upto(NB, NB))
            for b in range(NB):
                for kc in range(KC):
                    mm = pe.matmul(psA[S * b:S * b + S, 1, 0:M], xnT_sb[:, kc, S * b:S * b + S],
                                   ctxT[:, t.slot, kc, b], start=(kc == 0), stop=(kc == KC - 1), tile_position=(0, S * b))
            mm.then_inc(A["scores_mm"], 1)

        def a03(t, n):
            pe.wait_ge(A["probs"], t.upto(1, 1))
            for c in range(MC):
                transpose(psA[:, 2, c * P:(c + 1) * P], p0[:, c * P:(c + 1) * P])
            pe.wait_ge(A["probs_last"], t.upto(1, 1))
            transpose(psA[0:NB, 2, 2 * P:3 * P], p0_last[:]).then_inc(A["probsT_mm"], 1)

        def a04(t, n):
            if n != 0:
                return
            pe.wait_ge(A["probsT"], t.upto(1, 1))
            pe.matmul(psA[:, 3, 0:D], p0T_last[:], last_row[:, t.slot], start=True, stop=False, skip_group_check=True)
            for b in range(NB):
                for c in range(MC):
                    mm = pe.matmul(psA[S * b:S * b + S, 3, 0:D], p0T[:, c, S * b:S * b + S], rows[:, t.slot, b, c],
                                   start=False, stop=(c == MC - 1), tile_position=(0, S * b), skip_group_check=True)
            mm.then_inc(A["read_mm"], 1)

        def a05(t, n):
            xnT(t, 2, 0).then_inc(A["xnT_mm"], 1)

        def project(bank, w, lo, n):
            for kc in range(KC):
                mm = pe.matmul(psA[:, bank, 0:n], xnT_sb[:, kc], w[:, kc, lo:lo + n], start=(kc == 0), stop=(kc == KC - 1))
            return mm

        def a06(t, n):
            if n == 0:
                pe.wait_ge(A["xnT"], t.upto(3, 2))
            bank, w, lo = ((2, wkv0, 0), (3, wkv0, KV0), (0, wq0, 0), (1, wq0, 512))[n]
            project(bank, w, lo, 512).then_inc(A["qkv_mm"], 1)

        def rotT(t, n, bank):
            pe.wait_ge(A["rot"], t.upto(5, n + 1))
            for c in range(4):
                mm = transpose(psA[:, bank, c * P:(c + 1) * P], rot[:, n % 2, c * P:(c + 1) * P])
            mm.then_inc(A["rotT_mm"], 1)

        def a07(t, n):
            if n == 0:
                rotT(t, 0, 2)
            if n == 5:
                pe.wait_ge(A["v"], t.upto(1, 1))
                rotT(t, 1, 3)
            if n == 1:
                project(0, wq0, 1024, 512).then_inc(A["qkv_mm"], 1)
            if n == 2:
                pe.wait_ge(A["rotT"], t.upto(5, 1))
                rotT(t, 2, 2)
            if n == 3:
                project(1, wq0, 1536, 512).then_inc(A["qkv_mm"], 1)
            if n == 4:
                pe.wait_ge(A["rotT"], t.upto(5, 2))
                rotT(t, 3, 3)
                pe.wait_ge(A["rotT"], t.upto(5, 3))
                rotT(t, 4, 2)

        def a08(t, c):
            if c > 3:
                return
            if c == 0:
                pe.wait_ge(A["rotT"], t.upto(5, 5))
            for b in range(NB):
                o = psA[:, c // 2].rearrange("p (c s b k) -> p c s b k", c=2, s=2, b=NB)[:, c % 2, :, b]
                mm = pe.matmul(o, qT[:, c, b].rearrange("p j q -> p (j q)"), kT[:, c, b], start=True, stop=True)
            if c == 3:
                mm.then_inc(A["att_mm"], 1)

        def a09(t, n):
            pe.wait_ge(A["att"], t.upto(1, 1))
            for s in range(2):
                for c in range(4):
                    at = (2 * c + s) * P
                    mm = transpose(psA[:, 2 + s, c * P:(c + 1) * P], att[:, at:at + P])
                mm.then_inc(A["attT_mm"], 1)

        def a10(t, b):
            if b == 0:
                pe.wait_ge(A["attT_act"], t.upto(1, 1))
                pe.wait_ge(A["attT_dve"], t.upto(1, 1))
            for c in range(4):
                for s in range(2):
                    g = 2 * c + s
                    mm = pe.matmul(psA[64 * s:64 * s + 64, b, c * P:(c + 1) * P], v0[S * b:S * b + S, g * HD0:(g + 1) * HD0],
                                   attT[S * b:S * b + S, s, c * P:(c + 1) * P], start=True, stop=True,
                                   tile_position=(S * b, 64 * s))
            mm.then_inc(A["pv_mm"], 1)

        def a11(t, n):
            if n > 3:
                return
            if n == 0:
                pe.wait_ge(A["oT_act"], t.upto(2, 2))
                pe.wait_ge(A["oT_dve"], t.upto(2, 2))
            for c in range(4 * n, 4 * n + 4):
                mm = pe.matmul(psA[:, 0, 0:D], oT[:, c // 4, c % 4].rearrange("p b q -> p (b q)"), wo0[:, c],
                               start=(c == 0), stop=(c == 15))
            if n == 3:
                mm.then_inc(A["wo_mm"], 1)

        def a12(t, n):
            xnT(t, 3, 1).then_inc(A["xnT_mm"], 1)

        def a13(t, n):
            if n == 0:
                pe.wait_ge(A["xnT"], t.upto(3, 3))
            bank, w, lo, done = ((2, wgate0, 0, None), (3, wgate0, 512, "gate_mm"), (0, wup0, 0, None),
                                 (1, wup0, 512, "up_mm"))[n]
            mm = project(bank, w, lo, 512)
            if done is not None:
                mm.then_inc(A[done], 1)

        def a14(t, n):
            pe.wait_ge(A["hid"], t.upto(1, 1))
            for h in range(2):
                for c in range(4):
                    at = h * 512 + c * P
                    mm = transpose(psA[:, 2 + h, c * P:(c + 1) * P], hid[:, at:at + P])
                mm.then_inc(A["hT_mm"], 1)

        def a15(t, n):
            if n == 0:
                pe.wait_ge(A["hT_act"], t.upto(1, 1))
                pe.wait_ge(A["hT_dve"], t.upto(1, 1))
            for c in range(4 * n, 4 * n + 4):
                mm = pe.matmul(psA[:, 0, 0:D], hT[:, c * P:(c + 1) * P], wdown0[:, c], start=(c == 0), stop=(c == FC - 1))
            if n == 1:
                mm.then_inc(A["down_mm"], 1)

        def ynT_step(t, k, bank):
            if k > 1:
                pe.wait_ge(B["b_yn"], t.upto(2, k - 1))
            src = yn1 if k == 1 else yn
            for c in range(KC):
                mm = transpose(psB[:, bank, c * P:(c + 1) * P], src[:, c * P:(c + 1) * P])
            mm.then_inc(B["b_ynT_mm"], 1)

        def ba(t, n):
            if n == 0:
                pe.wait_ge(A["yn1"], t.upto(1, 1))
                if not t.first:
                    pe.wait_ge(B["b_logits"], t.upto(1, 0))
                ynT_step(t, 1, 3)
            if n == 1:
                pe.wait_ge(B["b_ynT"], t.upto(3, 1))
                for kc in range(KC):
                    mm = pe.matmul(psB[:, 3, D:2 * D], ynT[:, kc], wq1[:, kc], start=(kc == 0), stop=(kc == KC - 1))
                mm.then_inc(B["b_q_mm"], 1)
            if n == 2:
                pe.wait_ge(B["b_q"], t.upto(1, 1))
                for c in range(KC):
                    mm = transpose(psB[:, 3, c * P:(c + 1) * P], q1[:, c * P:(c + 1) * P])
                mm.then_inc(B["b_qT_mm"], 1)

        def bb(t, b):
            if b > 0:
                pe.wait_ge(B["b_probsT_act"], t.upto(2 * NB, 2 * b))
                pe.wait_ge(B["b_probsT_dve"], t.upto(NB, b))
            for m in range(KC):
                for kc in range(KC):
                    mm = pe.matmul(psB[:, m, 0:M], wk1[:, kc, m * P:(m + 1) * P], ctxT[:, t.slot, kc, b],
                                   start=(kc == 0), stop=(kc == KC - 1))
                if b == 0:
                    for kc in range(KC):
                        mm = pe.matmul(psB[0:NB, m, 3 * P:4 * P], ctxT[:, t.slot, kc, :, M - 1],
                                       wv1[:, kc, m * P:(m + 1) * P], start=(kc == 0), stop=(kc == KC - 1))
            mm.then_inc(B["b_k_mm"], 1)
            for c in range(MC):
                for kc in range(KC):
                    mm = pe.matmul(psB[:, 2, c * D:(c + 1) * D], ctxT[:, t.slot, kc, b, c * P:(c + 1) * P], wv1[:, kc],
                                   start=(kc == 0), stop=(kc == KC - 1))
            mm.then_inc(B["b_v_mm"], 1)

        def bc(t, b):
            pe.wait_ge(B["b_v"], t.upto(NB, b + 1))
            pe.wait_ge(B["b_ksq"], t.upto(NB, b + 1))
            for m in range(KC):
                mm = pe.matmul(psB[:, 2, 0:M], ones[:], ksq[:, m], start=(m == 0), stop=(m == KC - 1))
            mm.then_inc(B["b_kss_mm"], 1)

        def bs(t, b):
            pe.wait_ge(B["b_kn"], t.upto(NB, b + 1))
            if b == 0:
                pe.wait_ge(B["b_qbd"], t.upto(1, 1))
            else:
                pe.wait_ge(B["b_o"], t.upto(NB, b))
            for j in range(REP):
                r = 64 * (j % 2)
                mm = pe.matmul(psB[:, j, 0:M], qbd[r:r + 64, j // 2, b].rearrange("p h q -> p (h q)"),
                               k1n[r:r + 64, j // 2], start=True, stop=True, tile_position=(r, 0))
            mm.then_inc(B["b_scores_mm"], 1)

        def be(t, b):
            pe.wait_ge(B["b_probs"], t.upto(NB, b + 1))
            for j in range(REP):
                for c in range(MC):
                    mm = transpose(psB[:, j // 2, ((j % 2) * MC + c) * P:((j % 2) * MC + c + 1) * P],
                                   p1[:, j, c * P:(c + 1) * P])
                if j % 2 == 1:
                    mm.then_inc(B["b_probsT_mm"], 1)
            pe.wait_ge(B["b_probs_last"], t.upto(NB, b + 1))
            for j in range(REP):
                mm = transpose(psB[0:NB, 2, j * P:(j + 1) * P], p1_last[:, b, j])
            mm.then_inc(B["b_probsT_mm"], 1)

        def bf(t, b):
            pe.wait_ge(B["b_probsT_act"], t.upto(2 * NB, 2 * b + 2))
            pe.wait_ge(B["b_probsT_dve"], t.upto(NB, b + 1))
            for j in range(REP):
                half = slice(j // 2 * P, (j // 2 + 1) * P)
                for c in range(MC):
                    at = (j * MC + c) * P
                    pe.matmul(psB[:, 3, j * P:(j + 1) * P], p1T[:, at:at + P], v1[:, b % 2, c, half], start=(c == 0), stop=False)
                mm = pe.matmul(psB[:, 3, j * P:(j + 1) * P], p1T_last[:, j * P:(j + 1) * P], v1_last[:, half],
                               start=False, stop=True)
            mm.then_inc(B["b_pv_mm"], 1)

        def out_T(src, bank):
            for b in range(NB):
                mm = transpose(psB[0:64, bank, b * P:(b + 1) * P], src[:, b].rearrange("p h d -> p (h d)"))
            return mm

        def out_w(srcT, w, bank):
            for h in range(REP):
                mm = pe.matmul(psB[:, bank, 0:D], srcT[:, h].rearrange("p b q -> p (b q)"), w[:, h], start=(h == 0),
                               stop=(h == REP - 1))
            return mm

        def bg(t, n):
            if n == 0:
                pe.wait_ge(setup_done, 1)
                pe.wait_ge(B["b_o"], t.upto(NB, NB))
                out_T(o1, 0).then_inc(B["b_oT_mm"], 1)
            if n == 1:
                pe.wait_ge(B["b_oT"], t.upto(1, 1))
                out_w(o1T, wo1, 1).then_inc(B["b_wo_mm"], 1)
            if n == 2:
                ynT_step(t, 2, 2)
            if n == 3:
                pe.wait_ge(B["b_ynT"], t.upto(3, 2))
                for kc in range(KC):
                    mm = pe.matmul(psB[:, 3, 0:384], ynT[:, kc], wqkv2[:, kc], start=(kc == 0), stop=(kc == KC - 1))
                mm.then_inc(B["b_qkv2_mm"], 1)
            if n == 4:
                pe.wait_ge(setup_done, 1)
                pe.wait_ge(B["b_rot2"], t.upto(1, 1))
                for j in range(REP):
                    transpose(psB[0:64, 0, j * P:(j + 1) * P], rc2[:, j * 64:(j + 1) * 64])
                transpose(psB[0:64, 1, 0:P], rc2[:, 256:320]).then_inc(B["b_rot2T_mm"], 1)
            if n == 5:
                pe.wait_ge(B["b_q2T"], t.upto(1, 1))
                pe.wait_ge(B["b_k2bd"], t.upto(1, 1))
                for b in range(NB):
                    for h in range(2):
                        o = psB[:, 2 + h].rearrange("p (g b k) -> p g b k", g=4, b=NB)[:, :, b]
                        mm = pe.matmul(o, q2T[:, b].rearrange("p j q -> p (j q)"), k2bd[:, b, 4 * h:4 * h + 4],
                                       start=True, stop=True)
                mm.then_inc(B["b_att2_mm"], 1)
            if n == 6:
                pe.wait_ge(B["b_exp2"], t.upto(1, 1))
                for h in range(2):
                    for g in range(4):
                        at = (4 * h + g) * P
                        mm = transpose(psB[:, h, g * P:(g + 1) * P], att2[:, at:at + P])
                    mm.then_inc(B["b_att2T_mm"], 1)
            if n == 7:
                pe.wait_ge(B["b_att2T_act"], t.upto(1, 1))
                pe.wait_ge(B["b_att2T_dve"], t.upto(1, 1))
                for g in range(G2):
                    mm = pe.matmul(psB[:, 2 + g // 4, g % 4 * P:(g % 4 + 1) * P], att2T[:, g * P:(g + 1) * P],
                                   v2bd[:, g // 4 * 4:g // 4 * 4 + 4].rearrange("p g b d -> p (g b d)"), start=True, stop=True)
                mm.then_inc(B["b_pv2_mm"], 1)
            if n == 8:
                pe.wait_ge(setup_done, 1)
                pe.wait_ge(B["b_o2"], t.upto(1, 1))
                out_T(o2, 3).then_inc(B["b_o2T_mm"], 1)
            if n == 9:
                pe.wait_ge(B["b_o2T"], t.upto(1, 1))
                out_w(o2T, wo2, 3).then_inc(B["b_wo2_mm"], 1)
            if n == 10:
                ynT_step(t, 3, 3)
            if n == 11:
                pe.wait_ge(B["b_ynT"], t.upto(3, 3))
                for kc in range(KC):
                    mm = pe.matmul(psB[:, 3, 0:EXPERTS], ynT[:, kc], wr[:, kc], start=(kc == 0), stop=(kc == KC - 1))
                mm.then_inc(B["b_logits_mm"], 1)

        run(pe, dict(a01=a01, a02=a02, a03=a03, a04=a04, a05=a05, a06=a06, a07=a07, a08=a08, a09=a09, a10=a10, a11=a11,
                     a12=a12, a13=a13, a14=a14, a15=a15), dict(ba=ba, bb=bb, bc=bc, bs=bs, be=be, bf=bf, bg=bg))

    @block.scalar
    def _(act):
        act.wait_ge(const_in, 16 * len(loads))
        nc.scalar.preload_act_table_set("natural_log_exp_and_others")

        def xnT_copy(t, k, bank):
            act.wait_ge(A["xnT_mm"], t.upto(3, k))
            return act.copy(xnT_sb[:].rearrange("p c q -> p (c q)"), psA[:, bank, 0:D])

        def a01(t, n):
            if n == 0:
                xnT_copy(t, 1, 0)
                act.copy(ctxT[:, t.slot, :, :, M - 1], psA[:, 0, D:D + KC * NB].rearrange("p (c b) -> p c b", c=KC)
                         ).then_inc(A["xnT"], 1)
            else:
                b = n - 1
                act.wait_ge(A["ctxT_mm"], t.upto(NB, b + 1))
                act.copy(ctxT[:, t.slot, :, b, 0:MC * P], psA[:, (b + 1) % 4, :].rearrange("p (k m) -> p k m", k=KC)
                         ).then_inc(A["ctxT"], 1)

        def a02(t, n):
            if n != 20:
                return
            act.wait_ge(A["scores"], t.upto(1, 1))
            act.activation(p0, sc0, ACT.Exp, bias=small[:, 1:2], accum_out=small[:, 2:3]).then_inc(A["probs"], 1)

        def a03(t, n):
            act.wait_ge(A["probsT_mm"], t.upto(1, 1))
            act.copy(p0T[:].rearrange("p c q -> p (c q)"), psA[:, 2, 0:MC * P])
            act.copy(p0T_last[:], psA[0:NB, 2, MC * P:(MC + 1) * P]).then_inc(A["probsT"], 1)

        def a05(t, n):
            xnT_copy(t, 2, 0).then_inc(A["xnT"], 1)

        def a06(t, n):
            if n == 1:
                act.wait_ge(A["qkv_mm"], t.upto(6, 2))
                act.copy(v0[:], psA[:, 3, :]).then_inc(A["v"], 1)

        def a07(t, n):
            if n == 0:
                act.wait_ge(A["rotT_mm"], t.upto(5, 1))
                for s in range(2):
                    r = slice(64 * s, 64 * s + 64)
                    ins = act.copy(kT[r, :, :, s], psA[r, 2, :].rearrange("p (c b k) -> p c b k", c=4, b=NB))
                ins.then_inc(A["rotT"], 1)
            for c in {5: (0,), 2: (1,), 4: (2, 3)}.get(n, ()):
                act.wait_ge(A["rotT_mm"], t.upto(5, c + 2))
                act.copy(qT[:, c].rearrange("p b j q -> p j b q"),
                         psA[:, 3 - c % 2, :].rearrange("p (j b q) -> p j b q", j=REP, b=NB)).then_inc(A["rotT"], 1)

        def a08(t, n):
            if n != 30:
                return
            act.wait_ge(A["att_centred"], t.upto(1, 1))
            act.activation(att[:], att[:], ACT.Exp).then_inc(A["att_exp"], 1)

        def a09(t, n):
            act.wait_ge(A["attT_mm"], t.upto(2, 1))
            act.copy(attT[:, 0], psA[:, 2, :]).then_inc(A["attT_act"], 1)

        def a10(t, n):
            b = n
            if b in (0, 2):
                act.wait_ge(A["pv_mm"], t.upto(NB, b + 1))
                act.copy(oT[:, :, :, b], psA[:, b, :].rearrange("p (c j q) -> p c j q", c=4, j=REP)).then_inc(A["oT_act"], 1)

        def a11(t, n):
            if n == 0:
                nc.scalar.preload_act_table_set("exp_and_others")

        def a12(t, n):
            xnT_copy(t, 3, 1).then_inc(A["xnT"], 1)

        def a13(t, n):
            if n != 1:
                return
            act.wait_ge(A["gate_mm"], t.upto(1, 1))
            act.activation(th, psA[:, 2:4, :].rearrange("p a n -> p (a n)"), ACT.Tanh, scale=0.5).then_inc(A["tanh"], 1)

        def a14(t, n):
            act.wait_ge(A["hT_mm"], t.upto(2, 1))
            act.copy(hT[:, 0:512], psA[:, 2, :]).then_inc(A["hT_act"], 1)

        def a15(t, n):
            if n == 0:
                nc.scalar.preload_act_table_set("natural_log_exp_and_others")

        def ynT_copy(t, k, bank):
            act.wait_ge(B["b_ynT_mm"], t.upto(3, k))
            act.copy(ynT[:].rearrange("p c q -> p (c q)"), psB[:, bank, 0:D]).then_inc(B["b_ynT"], 1)

        def ba(t, n):
            if n == 0:
                ynT_copy(t, 1, 3)

        def bb(t, b):
            act.wait_ge(B["b_k_mm"], t.upto(NB, b + 1))
            if b == 0:
                act.copy(v1_last[:].rearrange("p (m d) -> p m d", m=KC), psB[0:NB, 0:KC, 3 * P:4 * P])
            for m in range(KC):
                ins = act.activation(ksq[:, m], psB[:, m, 0:M], ACT.Square, bias=bk1[:, m:m + 1])
            ins.then_inc(B["b_ksq"], 1)
            act.wait_ge(B["b_v_mm"], t.upto(NB, b + 1))
            act.copy(v1[:, b % 2].rearrange("p c d -> p (c d)"), psB[:, 2, :]).then_inc(B["b_v"], 1)

        def bc(t, b):
            act.wait_ge(B["b_kms"], t.upto(NB, b + 1))
            act.activation(krs[:], kms[:], ACT.Ln).then_inc(B["b_kln"], 1)
            act.wait_ge(B["b_kln"], t.upto(NB, b + 1))
            act.activation(krs[:], krs[:], ACT.Exp, scale=-0.5).then_inc(B["b_krs"], 1)

        def bd(t, b):
            act.wait_ge(B["b_max"], t.upto(NB, b + 1))
            for j in range(REP):
                ins = act.activation(p1[:, j], psB[:, j, 0:M], ACT.Exp, bias=p1max[:, j:j + 1], scale=HD1 ** -0.5,
                                     accum_out=p1sum[:, j:j + 1])
            ins.then_inc(B["b_probs"], 1)

        def be(t, b):
            act.wait_ge(B["b_probsT_mm"], t.upto(3 * NB, 3 * b + 1))
            act.copy(p1T[:, 0:512], psB[:, 0, :]).then_inc(B["b_probsT_act"], 1)
            act.wait_ge(B["b_probsT_mm"], t.upto(3 * NB, 3 * b + 3))
            act.copy(p1T_last[:], psB[0:NB, 2, :]).then_inc(B["b_probsT_act"], 1)

        def bg(t, n):
            if n == 0:
                act.wait_ge(B["b_oT_mm"], t.upto(1, 1))
                for h in range(REP):
                    ins = act.activation(o1T[:, h], psB[0:64, 0, :].rearrange("p (b h q) -> p b h q", b=NB, h=REP)[:, :, h],
                                         ACT.Identity, bias=bv1[:, h:h + 1])
                ins.then_inc(B["b_oT"], 1)
            if n == 2:
                ynT_copy(t, 2, 2)
            if n == 4:
                act.wait_ge(B["b_rot2T_mm"], t.upto(1, 1))
                act.copy(q2T.rearrange("p b j q -> p j b q"),
                         psB[0:64, 0, :].rearrange("p (j b q) -> p j b q", j=REP, b=NB)).then_inc(B["b_q2T"], 1)
            if n == 55:
                act.wait_ge(B["b_centred2"], t.upto(1, 1))
                act.activation(att2, att2, ACT.Exp, scale=float(1 / np.sqrt(np.float32(HD2)))).then_inc(B["b_exp2"], 1)
            if n == 6:
                act.wait_ge(B["b_att2T_mm"], t.upto(2, 1))
                act.copy(att2T[:, 0:512], psB[:, 0, :]).then_inc(B["b_att2T_act"], 1)
            if n == 8:
                act.wait_ge(B["b_o2T_mm"], t.upto(1, 1))
                act.copy(o2T[:].rearrange("p j b q -> p b j q"),
                         psB[0:64, 3, :].rearrange("p (b j q) -> p b j q", b=NB, j=REP)).then_inc(B["b_o2T"], 1)

            if n == 10:
                ynT_copy(t, 3, 3)
            if n == 11:
                act.wait_ge(B["b_logits"], t.upto(1, 1))
                act.activation(pr[:], lg[:], ACT.Exp, bias=rt[:, 1:2], accum_out=rt[:, 2:3]).then_inc(B["b_pexp"], 1)

        run(act, dict(a01=a01, a02=a02, a03=a03, a05=a05, a06=a06, a07=a07, a08=a08, a09=a09, a10=a10, a11=a11, a12=a12, a13=a13,
                      a14=a14, a15=a15), dict(ba=ba, bb=bb, bc=bc, bd=bd, be=be, bg=bg))

    @block.vector
    def _(dve):
        dve.wait_ge(const_in, 16 * len(loads))
        dve.memset(ones[:], 1.0)
        dve.memset(zero_row, 0.0)
        dve.memset(kT[:], 0.0)
        dve.memset(p1_last[:], 0.0).then_inc(setup_chain, 1)
        for c in range(KC):
            ins = dve.tensor_scalar(gk_rows[:, c], head_rows[:], gk1[:, c:c + 1], None, ALU.mult)
        ins.then_inc(setup_chain, 1)
        dve.wait_ge(setup_chain, 2)
        dve.memset(small[:, 7:8], 0.0).then_inc(setup_done, 1)
        cn = Chain(dve, dve_n, CHAIN_N)
        ca = Chain(dve, dve_a, CHAIN_A)
        cb = Chain(dve, dve_b, CHAIN_B)
        ck = Chain(dve, dve_k, CHAIN_K * NB)

        def norm(chain, x, y, stats, mv):
            return layer_norm(dve, chain, x, y[:], stats[:], mv)

        def a00(t, n):
            cn.open(t)
            wait_loaded(dve, t)
            if not t.first:
                dve.wait_ge(A["xnT_mm"], t.upto(3, 0))
            norm(cn, x_in[:, t.slot], xn, stats, mv).then_inc(A["xn1"], 1)
            cn.close()

        def a01(t, n):
            if n == 0:
                ca.open(t)
                m8 = mask_u8[:, t.slot]
                dve.tensor_scalar(maskadd[:, 0:MC * P].rearrange("p (c r) -> p c r", c=MC),
                                  m8[:, 0:MC * P].rearrange("p (r c) -> p c r", c=MC), 1.0, -NEG, ALU.subtract, ALU.mult)
                dve.tensor_scalar(maskadd[:, M - 1:M], m8[:, M - 1:M], 1.0, -NEG, ALU.subtract, ALU.mult)
                ca.done(dve.tensor_reduce(small[:, 0:1], m8, AX.X, ALU.max))

        def a02(t, n):
            if n != 20:
                return
            dve.wait_ge(A["scores_mm"], t.upto(1, 1))
            ca.done(dve.scalar_tensor_tensor(sc0, psA[:, 1, 0:M], D ** -0.5, maskadd, ALU.mult, ALU.add))
            ca.done(dve.tensor_reduce(small[:, 3:4], sc0, AX.X, ALU.max))
            dve.tensor_scalar(small[:, 1:2], small[:, 3:4], -1.0, None, ALU.mult).then_inc(A["scores"], 1)
            dve.wait_ge(A["probs"], t.upto(1, 1))
            dve.tensor_scalar(p0_last[:], own_batch[:], p0[:, M - 1:M], None, ALU.mult).then_inc(A["probs_last"], 1)
            ca.done(dve.reciprocal(small[:, 4:5], small[:, 2:3]))
            ca.done(dve.tensor_tensor(small[:, 5:6], small[:, 4:5], small[:, 0:1], ALU.mult))

        def a04(t, n):
            if n != 40:
                return
            dve.wait_ge(A["read_mm"], t.upto(1, 1))
            ca.done(dve.scalar_tensor_tensor(x1[:], psA[:, 3, 0:D], small[:, 5:6], x_in[:, t.slot], ALU.mult, ALU.add))
            norm(ca, x1[:], xn, stats, mv).then_inc(A["xn"], 1)

        def rope(t, n, mm, bank):
            if n >= 2:
                dve.wait_ge(A["rotT_mm"], t.upto(5, n - 1))
            dve.wait_ge(A["qkv_mm"], t.upto(6, mm))
            v = psA[:, bank, :].rearrange("p (h d) -> p h d", d=HD0)
            c3, s3 = (r.rearrange("p (h d) -> p h d", d=HD0) for r in (rope_c, rope_s))
            h = HD0 // 2
            dve.tensor_tensor(c3, v, cos0[:].unsqueeze(1).broadcast_to([P, 8, HD0]), ALU.mult)
            dve.tensor_tensor(s3[:, :, 0:h], v[:, :, h:], sin0[:, 0:h].unsqueeze(1).broadcast_to([P, 8, h]), ALU.mult)
            ca.done(dve.tensor_tensor(s3[:, :, h:], v[:, :, 0:h], sin0[:, h:].unsqueeze(1).broadcast_to([P, 8, h]), ALU.mult))
            dve.tensor_tensor(rot[:, n % 2], rope_c, rope_s, ALU.add).then_inc(A["rot"], 1)
            dve.wait_ge(A["rot"], t.upto(5, n + 1))

        def ar(t, n):
            rope(t, n, *((1, 2), (3, 0), (4, 1), (5, 0), (6, 1))[n])

        def segments(x, n=32):
            return x.rearrange("p (g k) -> p g k", g=n)

        def a08(t, n):
            s3 = segments(att[:])
            if n == 30:
                dve.wait_ge(A["att_mm"], t.upto(1, 1))
                ca.done(dve.scalar_tensor_tensor(s3, psA[:, 0:2, :].rearrange("p a (g k) -> p (a g) k", k=S), HD0 ** -0.5,
                                                 causal[:].unsqueeze(1).broadcast_to([P, 32, S]), ALU.mult, ALU.add))
                ca.done(dve.tensor_reduce(att_max[:], s3, AX.X, ALU.max))
                dve.tensor_tensor(s3, s3, att_max[:].unsqueeze(2).broadcast_to([P, 32, S]), ALU.subtract
                                  ).then_inc(A["att_centred"], 1)
            if n == 31:
                dve.wait_ge(A["att_exp"], t.upto(1, 1))
                ca.done(dve.tensor_reduce(att_sum[:], s3, AX.X, ALU.add))
                ca.done(dve.reciprocal(att_sum[:], att_sum[:]))
                dve.tensor_tensor(s3, s3, att_sum[:].unsqueeze(2).broadcast_to([P, 32, S]), ALU.mult).then_inc(A["att"], 1)

        def a09(t, n):
            dve.wait_ge(A["attT_mm"], t.upto(2, 2))
            dve.tensor_copy(attT[:, 1], psA[:, 3, :]).then_inc(A["attT_dve"], 1)

        def a10(t, n):
            b = n
            if b in (1, 3):
                dve.wait_ge(A["pv_mm"], t.upto(NB, b + 1))
                dve.tensor_copy(oT[:, :, :, b], psA[:, b, :].rearrange("p (c j q) -> p c j q", c=4, j=REP)
                                ).then_inc(A["oT_dve"], 1)

        def a11(t, n):
            if n != 30:
                return
            dve.wait_ge(A["wo_mm"], t.upto(1, 1))
            ca.done(dve.tensor_tensor(x2[:], psA[:, 0, 0:D], x1[:], ALU.add))
            norm(ca, x2[:], xn, stats, mv).then_inc(A["xn"], 1)

        def a13(t, n):
            if n != 3:
                return
            dve.wait_ge(A["tanh"], t.upto(1, 1))
            ca.done(dve.scalar_tensor_tensor(hid, th, 1.0, psA[:, 2:4, :].rearrange("p a n -> p (a n)"), ALU.add, ALU.mult))
            dve.wait_ge(A["up_mm"], t.upto(1, 1))
            dve.tensor_tensor(hid, hid, psA[:, 0:2, :].rearrange("p a n -> p (a n)"), ALU.mult).then_inc(A["hid"], 1)

        def a14(t, n):
            dve.wait_ge(A["hT_mm"], t.upto(2, 2))
            dve.tensor_copy(hT[:, 512:1024], psA[:, 3, :]).then_inc(A["hT_dve"], 1)

        def a15(t, n):
            if n != 1:
                return
            dve.wait_ge(A["down_mm"], t.upto(1, 1))
            dve.scalar_tensor_tensor(x3[:, t.slot], psA[:, 0, 0:D], 0.5, x2[:], ALU.mult, ALU.add).then_inc(A["x3"], 1)
            dve.wait_ge(A["x3"], t.upto(1, 1))
            norm(ca, x3[:, t.slot], yn1, stats, mv).then_inc(A["yn1"], 1)
            ca.close()

        def ba(t, n):
            if n == 0:
                cb.open(t)
                dve.tensor_tensor(x3b[:], x3[:, t.slot], bo1[:], ALU.add)
            if n == 1:
                dve.wait_ge(B["b_q_mm"], t.upto(1, 1))
                cb.done(dve.tensor_tensor(q1[:], psB[:, 3, D:2 * D], bq1[:], ALU.add))
                cb.done(dve.tensor_tensor(q1sq[:], q1[:], q1[:], ALU.mult))
                cb.done(dve.tensor_reduce(q1ss[:, 0:1], q1sq[:], AX.X, ALU.add))
                inverse_root(dve, cb, q1ss[:, 0:1], 1.0 / D, 1e-6, q1ss[:, 1:2], q1ss[:, 2:3])
                dve.scalar_tensor_tensor(q1[:], q1[:], q1ss[:, 2:3], gq1[:], ALU.mult, ALU.mult).then_inc(B["b_q"], 1)
            if n == 2:
                dve.wait_ge(B["b_qT_mm"], t.upto(1, 1))
                for c in range(KC):
                    ins = dve.tensor_tensor(
                        qbd[:, c],
                        psB[:, 3, c * P:(c + 1) * P].rearrange("p (b q) -> p b q", b=NB).unsqueeze(2).broadcast_to([P, NB, REP, S]),
                        gk_rows[:, c].unsqueeze(1).unsqueeze(3).broadcast_to([P, NB, REP, S]), ALU.mult)
                ins.then_inc(B["b_qbd"], 1)

        def bc(t, b):
            dve.wait_ge(B["b_kss_mm"], t.upto(NB, b + 1))
            dve.tensor_scalar(kms[:], psB[:, 2, 0:M], 1.0 / D, 1e-6, ALU.mult, ALU.add).then_inc(B["b_kms"], 1)

        def bn(t, b):
            ck.open(t, CHAIN_K * b)
            dve.wait_ge(B["b_krs"], t.upto(NB, b + 1))
            ck.done(dve.tensor_tensor(kms[:], kms[:], krs[:], ALU.mult))
            ck.done(dve.tensor_tensor(kms[:], kms[:], krs[:], ALU.mult))
            ck.done(dve.tensor_scalar(kms[:], kms[:], -0.5, 1.5, ALU.mult, ALU.add))
            ck.done(dve.tensor_tensor(krs[:], kms[:], krs[:], ALU.mult))
            for m in range(KC):
                ins = dve.scalar_tensor_tensor(k1n[:, m], psB[:, m, 0:M], bk1[:, m:m + 1], krs[:], ALU.add, ALU.mult)
            ins.then_inc(B["b_kn"], 1)
            assert ck.n == CHAIN_K * (b + 1)

        def bd(t, b):
            dve.wait_ge(B["b_scores_mm"], t.upto(NB, b + 1))
            cb.done(dve.tensor_reduce(p1max[:], psB[:, :, 0:M], AX.X, ALU.max))
            dve.tensor_scalar(p1max[:], p1max[:], -HD1 ** -0.5, None, ALU.mult).then_inc(B["b_max"], 1)

        def be(t, b):
            dve.wait_ge(B["b_probs"], t.upto(NB, b + 1))
            dve.tensor_copy(p1_last[:, b, :, b], p1[:, :, M - 1]).then_inc(B["b_probs_last"], 1)
            cb.done(dve.reciprocal(p1rec[:], p1sum[:]))
            dve.wait_ge(B["b_probsT_mm"], t.upto(3 * NB, 3 * b + 2))
            dve.tensor_copy(p1T[:, 512:1024], psB[:, 1, :]).then_inc(B["b_probsT_dve"], 1)

        def bf(t, b):
            dve.wait_ge(B["b_pv_mm"], t.upto(NB, b + 1))
            for h in range(REP):
                r = slice(S * h, S * h + S)
                ps = psB[r, 3, :].rearrange("p (a x d) -> p a x d", a=2, x=4)[:, :, 0:4:3, h * HD1:(h + 1) * HD1]
                ins = dve.tensor_tensor(o1[r, b].rearrange("p (a x) d -> p a x d", a=2), ps,
                                        p1rec[r].rearrange("p (a x) -> p a x", a=2).unsqueeze(3).broadcast_to([S, 2, 2, HD1]),
                                        ALU.mult)
            ins.then_inc(B["b_o"], 1)

        def bg(t, n):
            if n == 15:
                dve.wait_ge(B["b_wo_mm"], t.upto(1, 1))
                cb.done(dve.tensor_tensor(x4[:], psB[:, 1, 0:D], x3b[:], ALU.add))
                norm(cb, x4[:], yn, stats_b, mv_b).then_inc(B["b_yn"], 1)
                dve.tensor_tensor(x4b[:], x4[:], bo2[:], ALU.add)
            if n == 3:
                dve.wait_ge(B["b_qkv2_mm"], t.upto(1, 1))
                cb.done(dve.tensor_tensor(qkv[:], psB[:, 3, 0:384], bqkv2[:], ALU.add))
                v = qkv[:, 0:320].rearrange("p (h d) -> p h d", d=HD2)
                c3, s3 = (r[:].rearrange("p (h d) -> p h d", d=HD2) for r in (rc2, rs2))
                h, n_h = HD2 // 2, 320 // HD2
                dve.tensor_tensor(c3, v, cos2[:].unsqueeze(1).broadcast_to([P, n_h, HD2]), ALU.mult)
                dve.tensor_tensor(s3[:, :, 0:h], v[:, :, h:], sin2[:, 0:h].unsqueeze(1).broadcast_to([P, n_h, h]), ALU.mult)
                cb.done(dve.tensor_tensor(s3[:, :, h:], v[:, :, 0:h], sin2[:, h:].unsqueeze(1).broadcast_to([P, n_h, h]), ALU.mult))
                dve.tensor_tensor(rc2[:], rc2[:], rs2[:], ALU.add).then_inc(B["b_rot2"], 1)
                dve.tensor_tensor(v2bd, qkv[:, 320:384].rearrange("p (g d) -> p g d", g=G2).unsqueeze(2).broadcast_to([P, G2, NB, HD2]),
                                  own_batch[:].unsqueeze(1).unsqueeze(3).broadcast_to([P, G2, NB, HD2]), ALU.mult)
            if n == 4:
                dve.wait_ge(B["b_rot2T_mm"], t.upto(1, 1))
                dve.tensor_tensor(k2bd, psB[0:64, 1, 0:P].rearrange("p (b k) -> p b k", b=NB).unsqueeze(2).broadcast_to([64, NB, G2, S]),
                                  group_rows[:].unsqueeze(1).unsqueeze(3).broadcast_to([64, NB, G2, S]), ALU.mult).then_inc(B["b_k2bd"], 1)
            if n == 5:
                dve.wait_ge(B["b_att2_mm"], t.upto(1, 1))
                ps = psB[:, 2:4, :].rearrange("p a (g k) -> p (a g) k", k=S)
                s3 = segments(att2)
                cb.done(dve.tensor_reduce(att2_max[:], ps, AX.X, ALU.max))
                dve.tensor_tensor(s3, ps, att2_max[:].unsqueeze(2).broadcast_to([P, 32, S]), ALU.subtract).then_inc(B["b_centred2"], 1)
            if n == 56:
                s3 = segments(att2)
                dve.wait_ge(B["b_exp2"], t.upto(1, 1))
                cb.done(dve.tensor_reduce(att2_sum[:], s3, AX.X, ALU.add))
                cb.done(dve.reciprocal(att2_sum[:], att2_sum[:]))
            if n == 6:
                dve.wait_ge(B["b_att2T_mm"], t.upto(2, 2))
                dve.tensor_copy(att2T[:, 512:1024], psB[:, 1, :]).then_inc(B["b_att2T_dve"], 1)
            if n == 7:
                dve.wait_ge(B["b_pv2_mm"], t.upto(1, 1))
                for h in range(2):
                    gs = slice(4 * h, 4 * h + 4)
                    ps = psB[:, 2 + h, :].rearrange("p (x b d) -> p x b d", x=16, b=NB)[:, 0:16:5]
                    ins = dve.tensor_tensor(o2.rearrange("p b g d -> p g b d")[:, gs], ps,
                                            att2_sum[:].rearrange("p (g b) -> p g b", g=G2)[:, gs].unsqueeze(3).broadcast_to([P, 4, NB, HD2]),
                                            ALU.mult)
                ins.then_inc(B["b_o2"], 1)
            if n == 90:
                dve.wait_ge(B["b_wo2_mm"], t.upto(1, 1))
                if not t.slot_first:
                    dve.wait_ge(stored[t.slot], 16 * t.n)
                elif t.first:
                    dve.wait_ge(zeroed, 16)
                cb.done(dve.tensor_tensor(x5[:, t.slot, 0:D], psB[:, 3, 0:D], x4b[:], ALU.add))
                norm(cb, x5[:, t.slot, 0:D], yn, stats_b, mv_b).then_inc(B["b_yn"], 1)
            if n == 11:
                dve.wait_ge(B["b_logits_mm"], t.upto(1, 1))
                cb.done(dve.tensor_tensor(lg[:], psB[:, 3, 0:EXPERTS], br[:], ALU.add))
                cb.done(dve.tensor_reduce(rt[:, 0:1], lg[:], AX.X, ALU.max))
                dve.tensor_scalar(rt[:, 1:2], rt[:, 0:1], -1.0, None, ALU.mult).then_inc(B["b_logits"], 1)
                dve.wait_ge(B["b_pexp"], t.upto(1, 1))
                dve.reciprocal(rt[:, 3:4], rt[:, 2:3])
                cb.done(dve.tensor_reduce(rt[:, 4:5], pr[:], AX.X, ALU.max))
                cb.done(dve.scalar_tensor_tensor(lg[:], pr[:], rt[:, 4:5], rank[:], ALU.is_equal, ALU.mult))
                cb.done(dve.tensor_reduce(rt[:, 5:6], lg[:], AX.X, ALU.max))
                dve.tensor_scalar(chosen[:, ds(t.i, 1), :].rearrange("p t e -> p (t e)"), lg[:], rt[:, 5:6], None, ALU.is_equal)
                dve.tensor_tensor(x5[:, t.slot, D:ROW], rt[:, 3:4], rt[:, 4:5], ALU.mult).then_inc(B["b_x5"], 1)
                cb.close()

        run(dve, dict(a00=a00, a01=a01, a02=a02, a04=a04, ar=ar, a08=a08, a09=a09, a10=a10, a11=a11, a13=a13, a14=a14,
                      a15=a15), dict(ba=ba, bc=bc, bn=bn, bd=bd, be=be, bf=bf, bg=bg))


def mixture_of_experts(nc, ctx, a, ident, chosen, x5_dram, sorted_dram, y_dram, out):
    def sb(name, shape, dt=F32):
        return ctx.enter_context(nc.sbuf_tensor(name, shape, dt))

    def sem(name):
        return ctx.enter_context(nc.semaphore(name))

    def sems(*names):
        return {n: sem(n) for n in names}

    GATHERS = 4
    wg = sb("wg", [P, EXPERTS, KC, F])
    wu = sb("wu", [P, EXPERTS, KC, F])
    wd = sb("wd", [P, EXPERTS, FC, D])
    x_all = sb("x_all", [P, TILES, ROW])
    before = sb("before", [P, P])
    tile_start = sb("tile_start", [P, TILES])
    tile_number = sb("tile_number", [P, SORTED_TILES])
    ones = sb("ones_m", [P, P])
    total = sb("total", [P, TILES, EXPERTS])
    sums = sb("sums", [P, 2, TILES, EXPERTS])
    place = sb("place", [P, TILES, EXPERTS])
    over = sb("over", [P, EXPERTS, TILES])
    tiles_of = sb("tiles_of", [P, EXPERTS])
    first_tile = sb("first_tile", [P, EXPERTS])
    first_row = sb("first_row", [P, EXPERTS])
    pos_f = sb("pos_f", [P, TILES])
    pos = sb("pos", [P, TILES], I32)
    expert_f = sb("expert_f", [P, SORTED_TILES])
    expert = sb("expert", [P, SORTED_TILES], I32)
    xs = sb("xs", [P, 2, ROW])
    xn = sb("xnm", [P, D])
    xnT = sb("xnTm", [P, 2, KC, P])
    stats = sb("stats_m", [P, 6])
    mv = sb("mv_m", [P, 4])
    th = sb("th_m", [P, F])
    hid = sb("hid_m", [P, 2, F])
    hT = sb("hT_m", [P, F])
    y = sb("y", [P, 2, D])
    back = sb("back", [P, GATHERS, D])
    fin = sb("fin", [P, 2, D])

    ps_g = ctx.enter_context(nc.psum_tensor("ps_g", [P, 2, 512], F32))
    ps_u = ctx.enter_context(nc.psum_tensor("ps_u", [P, 2, 512], F32))
    ps_t = ctx.enter_context(nc.psum_tensor("ps_t", [P, 2, 512], F32))
    ps_y = ctx.enter_context(nc.psum_tensor("ps_y", [P, 512], F32))
    ps_x = ctx.enter_context(nc.psum_tensor("ps_x", [P, 512], F32))

    weights_in, routing_in, all_in = sem("expert_weights_in"), sem("routing_constants_in"), sem("x_all_in")
    loaded = [sem("sorted_loaded0"), sem("sorted_loaded1")]
    y_stored = [sem("y_stored0"), sem("y_stored1")]
    scattered = sem("rows_scattered")
    gathered = [sem(f"rows_gathered{g}") for g in range(GATHERS)]
    out_stored = [sem("out_stored0"), sem("out_stored1")]
    dve_route, dve_m = sem("dve_own_routing"), sem("dve_own_m")
    C = sems("counted_mm", "ones_set", "placed", "m_xn", "m_xnT_mm", "m_xnT", "m_gate_mm", "m_up_mm", "m_tanh", "m_gated", "m_hid",
             "m_hT_mm", "m_hT_act", "m_hT_dve", "m_down_mm", "m_y", "m_fin")

    block = ctx.enter_context(nc.Block())

    def run(eng, steps):
        def tile(before, t, after):
            for name, which in (("norm", after), ("gate", t), ("turn", before), ("up", t), ("norm_T", after),
                                ("down", before)):
                if which is not None and name in steps:
                    steps[name](which)

        for name in ("norm", "norm_T"):
            if name in steps:
                steps[name](Tile(0, 0, 0))
        tile(None, Tile(0, 0, 0), Tile(1, 1, 0))
        tile(Tile(0, 0, 0), Tile(1, 1, 0), Tile(2, 0, 1))
        tile(Tile(1, 1, 0), Tile(2, 0, 1), Tile(3, 1, 1))
        with eng.Fori(1, SORTED_TILES // 2 - 1) as k:
            tile(Tile(2 * k, 0, k), Tile(2 * k + 1, 1, k), Tile(2 * k + 2, 0, k + 1))
            tile(Tile(2 * k + 1, 1, k), Tile(2 * k + 2, 0, k + 1), Tile(2 * k + 3, 1, k + 1))
        h, last = SORTED_TILES // 2, SORTED_TILES - 1
        tile(Tile(last - 2, 0, h - 1), Tile(last - 1, 1, h - 1), Tile(last, 0, h))
        tile(Tile(last - 1, 1, h - 1), Tile(last, 0, h), None)
        for name in ("turn", "down"):
            if name in steps:
                steps[name](Tile(last, 0, h))

    @block.sync
    def _(sp):
        for dst, src in ((before, "before"), (tile_start, "tile_start"), (tile_number, "tile_number")):
            sp.dma_start(dst[:], a[src]).then_inc(routing_in, 16)
        sp.dma_start(x_all[:], x5_dram.rearrange("(t p) d -> p t d", p=P)).then_inc(all_in, 16)
        for dst, src in ((wg, "wg"), (wu, "wu"), (wd, "wd")):
            sp.dma_start(dst[:], a[src]).then_inc(weights_in, 16)
        sp.wait_ge(scattered, 16 * TILES)

        def load(t):
            if not t.slot_first:
                sp.wait_ge(C["m_hid"], t.upto(1, -1))
            sp.dma_start(xs[:, t.slot], sorted_dram[ds(t.i * P, P)]).then_inc(loaded[t.slot], 16)

        load(Tile(0, 0, 0))
        load(Tile(1, 1, 0))
        with sp.Fori(1, SORTED_TILES // 2) as k:
            load(Tile(2 * k, 0, k))
            load(Tile(2 * k + 1, 1, k))
        load(Tile(SORTED_TILES - 1, 0, SORTED_TILES // 2))
        for i in range(TILES):
            sp.wait_ge(C["m_fin"], i + 1)
            sp.dma_start(out[i * P:(i + 1) * P], fin[:, i % 2]).then_inc(out_stored[i % 2], 16)
        for s in out_stored:
            sp.wait_ge(s, 16 * (TILES // 2))

    @block.gpsimd
    def _(pool):
        pool.wait_ge(all_in, 16)
        pool.wait_ge(C["placed"], 1)
        for i in range(TILES):
            pool.indirect_dma_start(out=sorted_dram, out_offset=bass.IndirectOffsetOnAxis(ap=pos[:, i:i + 1], axis=0),
                                    in_=x_all[:, i], in_offset=None).then_inc(scattered, 16)
        for i in range(TILES):
            if i == 0:
                for s, n in zip(y_stored, (SORTED_TILES // 2 + 1, SORTED_TILES // 2)):
                    pool.wait_ge(s, 16 * n)
            if i >= GATHERS:
                pool.wait_ge(C["m_fin"], i - GATHERS + 1)
            pool.indirect_dma_start(out=back[:, i % GATHERS], out_offset=None, in_=y_dram,
                                    in_offset=bass.IndirectOffsetOnAxis(ap=pos[:, i:i + 1], axis=0)
                                    ).then_inc(gathered[i % GATHERS], 16)

    @block.tensor
    def _(pe):
        pe.wait_ge(routing_in, 48)
        pe.wait_ge(C["ones_set"], 1)
        flat = chosen[:].rearrange("p t e -> p (t e)")
        pe.matmul(ps_x[:, 0:P], before[:], flat, start=True, stop=True)
        pe.matmul(ps_y[:, 0:P], ones[:], flat, start=True, stop=True).then_inc(C["counted_mm"], 1)
        pe.wait_ge(C["placed"], 1)
        pe.wait_ge(weights_in, 48)

        def norm_T(t):
            pe.wait_ge(C["m_xn"], t.upto(1, 1))
            for c in range(KC):
                mm = pe.transpose(ps_x[:, c * P:(c + 1) * P], xn[:, c * P:(c + 1) * P], ident[:])
            mm.then_inc(C["m_xnT_mm"], 1)

        def expert_of(t):
            return pe.value_load(expert[0:1, ds(t.i, 1)], min_val=0, max_val=EXPERTS - 1)

        def project(t, e, ps, w):
            for h in range(2):
                for c in range(KC):
                    mm = pe.matmul(ps[:, h], xnT[:, t.slot, c], w[:, ds(e, 1), c, h * 512:(h + 1) * 512],
                                   start=(c == 0), stop=(c == KC - 1))
            return mm

        def gate(t):
            e = expert_of(t)
            pe.wait_ge(C["m_xnT"], t.upto(1, 1))
            if not t.first:
                pe.wait_ge(C["m_gated"], t.upto(1, 0))
            project(t, e, ps_g, wg).then_inc(C["m_gate_mm"], 1)

        def up(t):
            e = expert_of(t)
            if not t.first:
                pe.wait_ge(C["m_hid"], t.upto(1, 0))
            project(t, e, ps_u, wu).then_inc(C["m_up_mm"], 1)

        def turn(t):
            pe.wait_ge(C["m_hid"], t.upto(1, 1))
            for h in range(2):
                for c in range(4):
                    at = h * 512 + c * P
                    mm = pe.transpose(ps_t[:, h, c * P:(c + 1) * P], hid[:, t.slot, at:at + P], ident[:])
                mm.then_inc(C["m_hT_mm"], 1)

        def down(t):
            e = expert_of(t)
            if not t.first:
                pe.wait_ge(C["m_y"], t.upto(1, 0))
            pe.wait_ge(C["m_hT_act"], t.upto(1, 1))
            pe.wait_ge(C["m_hT_dve"], t.upto(1, 1))
            for c in range(FC):
                mm = pe.matmul(ps_y[:, 0:D], hT[:, c * P:(c + 1) * P], wd[:, ds(e, 1), c], start=(c == 0), stop=(c == FC - 1))
            mm.then_inc(C["m_down_mm"], 1)

        run(pe, dict(norm_T=norm_T, gate=gate, up=up, turn=turn, down=down))

    @block.scalar
    def _(act):
        def norm_T(t):
            act.wait_ge(C["m_xnT_mm"], t.upto(1, 1))
            act.copy(xnT[:, t.slot].rearrange("p c q -> p (c q)"), ps_x[:, 0:D]).then_inc(C["m_xnT"], 1)

        def gate(t):
            act.wait_ge(C["m_gate_mm"], t.upto(1, 1))
            act.activation(th[:], ps_g[:].rearrange("p a n -> p (a n)"), ACT.Tanh, scale=0.5).then_inc(C["m_tanh"], 1)

        def turn(t):
            act.wait_ge(C["m_hT_mm"], t.upto(2, 1))
            act.copy(hT[:, 0:512], ps_t[:, 0]).then_inc(C["m_hT_act"], 1)

        def down(t):
            act.wait_ge(C["m_y"], t.upto(1, 1))
            act.dma_start(y_dram[ds(t.i * P, P)], y[:, t.slot]).then_inc(y_stored[t.slot], 16)

        run(act, dict(norm_T=norm_T, gate=gate, turn=turn, down=down))

    @block.vector
    def _(dve):
        dve.memset(ones[:], 1.0).then_inc(C["ones_set"], 1)
        dve.wait_ge(routing_in, 48)
        dve.wait_ge(C["counted_mm"], 1)
        rt = Tile(0, 0, 0)
        cr = Chain(dve, dve_route, 0)
        cr.open(rt)
        cr.done(dve.tensor_copy(total[:], ps_y[:, 0:P].rearrange("p (t e) -> p t e", e=EXPERTS)))
        old, step, n = total[:], 1, 0
        while step < TILES:
            new = sums[:, n % 2]
            dve.tensor_copy(new[:, 0:step], old[:, 0:step])
            cr.done(dve.tensor_tensor(new[:, step:], old[:, step:], old[:, 0:TILES - step], ALU.add))
            old, step, n = new, 2 * step, n + 1
        count = old[:, TILES - 1]
        cr.done(dve.tensor_tensor(over[:], count.unsqueeze(2).broadcast_to([P, EXPERTS, TILES]),
                                  tile_start[:].unsqueeze(1).broadcast_to([P, EXPERTS, TILES]), ALU.is_gt))
        cr.done(dve.tensor_reduce(tiles_of[:], over[:], AX.X, ALU.add))
        cr.done(dve.memset(first_tile[:, 0:1], 0.0))
        for e in range(1, EXPERTS):
            cr.done(dve.tensor_tensor(first_tile[:, e:e + 1], first_tile[:, e - 1:e], tiles_of[:, e - 1:e], ALU.add))
        cr.done(dve.tensor_scalar(first_row[:], first_tile[:], float(P), None, ALU.mult))
        cr.done(dve.tensor_tensor(place[:], old, total[:], ALU.subtract))
        cr.done(dve.tensor_tensor(place[:], place[:], ps_x[:, 0:P].rearrange("p (t e) -> p t e", e=EXPERTS), ALU.add))
        cr.done(dve.tensor_tensor(place[:], place[:], first_row[:].unsqueeze(1).broadcast_to([P, TILES, EXPERTS]), ALU.add))
        cr.done(dve.tensor_tensor(place[:], place[:], chosen[:], ALU.mult))
        cr.done(dve.tensor_reduce(pos_f[:], place[:], AX.X, ALU.add))
        dve.tensor_copy(pos[:], pos_f[:])
        cr.done(dve.tensor_scalar(expert_f[:], tile_number[:], first_tile[:, 1:2], None, ALU.is_ge))
        for e in range(2, EXPERTS):
            cr.done(dve.scalar_tensor_tensor(expert_f[:], tile_number[:], first_tile[:, e:e + 1], expert_f[:], ALU.is_ge, ALU.add))
        dve.tensor_copy(expert[:], expert_f[:]).then_inc(C["placed"], 1)

        cm = Chain(dve, dve_m, CHAIN_M)

        def norm(t):
            cm.open(t)
            dve.wait_ge(loaded[t.slot], t.n * 16 + 16)
            if not t.first:
                dve.wait_ge(C["m_xnT_mm"], t.upto(1, 0))
            layer_norm(dve, cm, xs[:, t.slot, 0:D], xn[:], stats[:], mv).then_inc(C["m_xn"], 1)
            cm.close()

        def gate(t):
            dve.wait_ge(C["m_tanh"], t.upto(1, 1))
            dve.scalar_tensor_tensor(hid[:, t.slot], th[:], 1.0, ps_g[:].rearrange("p a n -> p (a n)"), ALU.add, ALU.mult
                                     ).then_inc(C["m_gated"], 1)

        def up(t):
            dve.wait_ge(C["m_gated"], t.upto(1, 1))
            dve.wait_ge(C["m_up_mm"], t.upto(1, 1))
            dve.scalar_tensor_tensor(hid[:, t.slot], hid[:, t.slot], xs[:, t.slot, D:ROW],
                                     ps_u[:].rearrange("p a n -> p (a n)"), ALU.mult, ALU.mult).then_inc(C["m_hid"], 1)

        def turn(t):
            dve.wait_ge(C["m_hT_mm"], t.upto(2, 2))
            dve.tensor_copy(hT[:, 512:1024], ps_t[:, 1]).then_inc(C["m_hT_dve"], 1)

        def down(t):
            dve.wait_ge(C["m_down_mm"], t.upto(1, 1))
            if not t.slot_first:
                dve.wait_ge(y_stored[t.slot], 16 * t.n)
            dve.tensor_scalar(y[:, t.slot], ps_y[:, 0:D], 0.5, None, ALU.mult).then_inc(C["m_y"], 1)

        run(dve, dict(norm=norm, gate=gate, up=up, turn=turn, down=down))
        for i in range(TILES):
            dve.wait_ge(gathered[i % GATHERS], 16 * (i // GATHERS + 1))
            if i >= 2:
                dve.wait_ge(out_stored[i % 2], 16 * (i // 2))
            dve.tensor_tensor(fin[:, i % 2], back[:, i % GATHERS], x_all[:, i, 0:D], ALU.add).then_inc(C["m_fin"], 1)


def rope_tables(width, base=10000.0):
    inv = (np.float32(base) ** (-np.arange(0, width, 2, dtype=np.float32) / np.float32(width))).astype(np.float32)
    th = np.outer(np.arange(S, dtype=np.float32), inv).astype(np.float32)
    cos, sin = np.cos(th), np.sin(th)
    return (np.tile(np.concatenate([cos, cos], 1), (NB, 1)).astype(np.float32),
            np.tile(np.concatenate([-sin, sin], 1), (NB, 1)).astype(np.float32))


def lay_out(i):
    f = {n: np.asarray(v) for n, v in i.items()}

    def chunks(w):
        return w.reshape(-1, P, w.shape[-1]).transpose(1, 0, 2)

    def rep(v, n=P):
        return np.broadcast_to(v[None], (n, v.shape[0]))

    a = {}
    a["x"] = f["x"].reshape(TILES, P, D)
    a["ctx"] = f["ctx_2048"]
    a["mask"] = np.repeat(f["mask_BxS2_bk0"], S, axis=0).reshape(TILES, P, M)
    a["wkv0"] = chunks(np.concatenate([f["L0_attn_wk"], f["L0_attn_wv"]], 1))
    a["wq0"] = chunks(f["L0_attn_wq"].reshape(D, 4, 2, REP, HD0).transpose(0, 1, 3, 2, 4).reshape(D, -1))
    a["wo0"] = f["L0_attn_wo"].reshape(4, 2, REP, HD0, D).transpose(0, 2, 1, 3, 4).reshape(16, P, D).transpose(1, 0, 2)
    a["wgate0"] = chunks(f["L0_ffn_w_gate"].T)
    a["wup0"] = chunks(f["L0_ffn_w_up"].T)
    a["wdown0"] = chunks(f["L0_ffn_w_down"].T)
    a["wq1"] = chunks(f["L1_xattn_Wq"])
    a["wk1"] = chunks(f["L1_xattn_Wk_img"])
    a["wv1"] = chunks(f["L1_xattn_Wv_img"])
    a["wo1"] = f["L1_xattn_Wo"].reshape(4, REP, HD1, D).transpose(0, 2, 1, 3).reshape(64, REP, D)
    a["bv1"] = f["L1_xattn_bv_img"].reshape(4, REP, HD1).transpose(0, 2, 1).reshape(64, REP)
    a["bq1"], a["gq1"], a["bo1"] = (rep(f["L1_xattn_" + n]) for n in ("bq", "gq", "bo"))
    a["bk1"], a["gk1"] = (f["L1_xattn_" + n].reshape(KC, P).T for n in ("bk_img", "gk_img"))
    wq2 = f["L1_attn_Wq"].T.reshape(D, G2, REP, HD2).transpose(0, 2, 1, 3).reshape(D, D)
    bq2 = f["L1_attn_bq"].reshape(G2, REP, HD2).transpose(1, 0, 2).reshape(D)
    a["wqkv2"] = chunks(np.concatenate([wq2, f["L1_attn_Wk"].T, f["L1_attn_Wv"].T], 1))
    a["bqkv2"] = rep(np.concatenate([bq2, f["L1_attn_bk"], f["L1_attn_bv"]]))
    a["wo2"] = f["L1_attn_Wo"].T.reshape(G2, REP, HD2, D).transpose(0, 2, 1, 3).reshape(64, REP, D)
    a["bo2"] = rep(f["L1_attn_bo"])
    a["wr"] = chunks(f["L1_ffn_Wr"])
    a["br"] = rep(f["L1_ffn_br"])
    a["wg"], a["wu"], a["wd"] = (f["L1_ffn_" + n].reshape(EXPERTS, -1, P, m).transpose(2, 0, 1, 3)
                                 for n, m in (("Wg", F), ("Wu", F), ("Wd", D)))
    a["ident"] = np.eye(P, dtype=np.float32)
    a["cos0"], a["sin0"] = rope_tables(HD0)
    a["cos2"], a["sin2"] = rope_tables(HD2)
    q = np.arange(P)
    a["causal"] = np.where(np.arange(S)[None] <= (q % S)[:, None], 0.0, NEG).astype(np.float32)
    a["own_batch"] = (q[:, None] // S == np.arange(NB)[None]).astype(np.float32)
    a["head_rows"] = ((q[:, None] // HD1) % REP == np.arange(REP)[None]).astype(np.float32)
    a["group_rows"] = (np.arange(64)[:, None] // HD2 == np.arange(G2)[None]).astype(np.float32)
    a["before"] = (q[:, None] < q[None]).astype(np.float32)
    a["tile_start"] = rep(np.arange(TILES, dtype=np.float32) * P)
    a["tile_number"] = rep(np.arange(SORTED_TILES, dtype=np.float32))
    a["rank"] = rep(np.arange(EXPERTS, 0, -1).astype(np.float32))
    return {n: np.ascontiguousarray(v) for n, v in a.items()}


def kernel(**inputs):
    import concourse.bacc as _bacc
    from concourse.bass_utils import run_bass_kernel_spmd as _run

    nc = _bacc.Bacc("TRN2", target_bir_lowering=False, num_devices=1)
    arrays = lay_out(inputs)
    a = {n: nc.dram_tensor("in_" + n, v.shape, mybir.dt.from_np(v.dtype), kind="ExternalInput").ap() for n, v in arrays.items()}
    out = nc.dram_tensor("out", [TOKENS, D], F32, kind="ExternalOutput").ap()
    build(nc, a, out)
    r = _run(nc, [{"in_" + n: v for n, v in arrays.items()}], core_ids=[0])
    return r.results[0]["out"].reshape(BATCHES, S, D)
```
